# Optimizing a Trainium2 kernel written in Bass

```python
import numpy as np
import jax
import jax.numpy as jnp

def _softmax(x, axis=-1):
    return jax.nn.softmax(x, axis=axis)

def _gelu(x):
    return jax.nn.gelu(x, approximate=True)

def _silu(x):
    return jax.nn.silu(x)

def _sigmoid(x):
    return jax.nn.sigmoid(x)

def _layernorm(x, axis=-1, eps=1e-05):
    m = jnp.mean(x, axis=axis, keepdims=True)
    v = jnp.var(x, axis=axis, keepdims=True)
    return (x - m) / jnp.sqrt(v + eps)

def _scatter_add(tgt, idx, src, axis=0):
    return tgt.at[idx].add(src)

def _segment_sum(src, seg, n):
    return jax.ops.segment_sum(src, seg, n)
kernel_name = 'mk_lm_tower_d2_tok_ids512_r4_a0b03f'

def setup_inputs(seed: int=0):
    np.random.seed(seed)
    _w = jnp.asarray

    def _rec_inputs():
        import jax
        import jax.numpy as jnp
        _rk = jax.random.key(seed)
        x = jax.random.randint(jax.random.fold_in(_rk, 1), (4, 512), 0, 5000, jnp.int32)
        itok_BS_0_4999 = jax.random.randint(jax.random.fold_in(_rk, 21), (4, 512), 0, 1250, jnp.int32)
        fside_BS_numeric_value = -0.00495105 + 0.998799 * jax.random.normal(jax.random.fold_in(_rk, 22), (4, 512), jnp.float32)
        mask_BS_i1_0 = jnp.where(jnp.ones((4, 512), dtype=bool), 1, 0).astype(jnp.int32)
        return (x, itok_BS_0_4999, fside_BS_numeric_value, mask_BS_i1_0)
    x, itok_BS_0_4999, fside_BS_numeric_value, mask_BS_i1_0 = _rec_inputs()

    def _L0_tok_setup():
        import jax, jax.numpy as jnp
        import numpy as np
        B, S = (32, 512)
        D = 128
        H = 64
        NE = 5000
        NV = 1250
        key = jax.random.key(seed)
        ks = jax.random.split(key, 10)
        event_idx = jax.random.randint(ks[0], (B, S), 0, NE)
        value_type_mask = jax.random.randint(ks[1], (B, S), 0, 2)
        value_idx = jax.random.randint(ks[2], (B, S), 0, NV) * (1 - value_type_mask)
        numeric_value = jax.random.normal(ks[3], (B, S), dtype=jnp.float32)
        event_table = jax.random.normal(ks[4], (NE, D), dtype=jnp.float32) * 0.02
        event_table = event_table.at[0].set(0.0)
        value_table = jax.random.normal(ks[5], (NV, D), dtype=jnp.float32) * 0.02
        value_table = value_table.at[0].set(0.0)
        w1 = jax.random.normal(ks[6], (1, H), dtype=jnp.float32) * (1.0 / np.sqrt(1.0))
        b1 = jnp.zeros((H,), dtype=jnp.float32)
        w2 = jax.random.normal(ks[7], (H, D), dtype=jnp.float32) * (1.0 / np.sqrt(H))
        b2 = jnp.zeros((D,), dtype=jnp.float32)
        return {'event_idx': event_idx, 'value_idx': value_idx, 'numeric_value': numeric_value, 'value_type_mask': value_type_mask, 'event_table': event_table, 'value_table': value_table, 'w1': w1, 'b1': b1, 'w2': w2, 'b2': b2}
    _L0_tok_all = _L0_tok_setup()
    _L0_tok_in = {k: v for k, v in _L0_tok_all.items() if k in ('event_table', 'value_table', 'w1', 'b1', 'w2', 'b2')}
    del _L0_tok_all

    def _L0_attn_setup():
        import jax, jax.numpy as jnp
        import numpy as np
        B, N, DIM = (2, 512, 128)
        H = 8
        DH = DIM // H
        ALPHA = 1.0
        DELTA = 1.0
        EPS = 1e-05

        def _split_heads(x):
            b, n, _ = x.shape
            return x.reshape(b, n, H, DH).transpose(0, 2, 1, 3)
        key = jax.random.key(seed)
        ks = jax.random.split(key, 5)
        scale = 0.02
        return {'z': jax.random.normal(ks[0], (B, N, DIM), dtype=jnp.float32), 'Wq': jax.random.normal(ks[1], (DIM, DIM), dtype=jnp.float32) * scale, 'bq': jnp.zeros((DIM,), dtype=jnp.float32), 'Wk': jax.random.normal(ks[2], (DIM, DIM), dtype=jnp.float32) * scale, 'bk': jnp.zeros((DIM,), dtype=jnp.float32), 'Wv': jax.random.normal(ks[3], (DIM, DIM), dtype=jnp.float32) * scale, 'bv': jnp.zeros((DIM,), dtype=jnp.float32), 'Wo': jax.random.normal(ks[4], (DIM, DIM), dtype=jnp.float32) * scale, 'bo': jnp.zeros((DIM,), dtype=jnp.float32)}
    _L0_attn_all = _L0_attn_setup()
    _L0_attn_in = {k: v for k, v in _L0_attn_all.items() if k in ('Wq', 'bq', 'Wk', 'bk', 'Wv', 'bv', 'Wo', 'bo')}
    del _L0_attn_all

    def _L0_ffn_setup():
        import jax, jax.numpy as jnp
        import numpy as np
        from jax import lax
        N_HEADS = 8
        D_KEYS = 128
        HALF = D_KEYS // 2
        N_KEYS = 64
        TOP_K = 8
        D_MODEL = 128

        def _forward(queries, Wq, bq, keys, w_down, w_up):
            N, T, D = queries.shape
            x = queries.reshape(-1, D)
            q = (x @ Wq + bq).reshape(-1, N_HEADS, D_KEYS)
            q1, q2 = (q[..., :HALF], q[..., HALF:])
            s1 = jnp.einsum('bhc,hnc->bhn', q1, keys[:, 0])
            s2 = jnp.einsum('bhc,hnc->bhn', q2, keys[:, 1])
            s1t, i1 = lax.top_k(s1, TOP_K)
            s2t, i2 = lax.top_k(s2, TOP_K)
            all_scores = (s1t[..., :, None] + s2t[..., None, :]).reshape(-1, N_HEADS, TOP_K * TOP_K)
            all_idx = (i1[..., :, None] * N_KEYS + i2[..., None, :]).reshape(-1, N_HEADS, TOP_K * TOP_K)
            scores, best = lax.top_k(all_scores, TOP_K)
            indices = jnp.take_along_axis(all_idx, best, axis=-1)
            w_d = w_down[indices]
            w_u = w_up[indices]
            inner = jnp.einsum('bd,bhkd->bhk', x, w_d)
            vals = jax.nn.relu(inner) * jax.nn.softmax(scores, axis=-1)
            out = jnp.einsum('bhk,bhkd->bd', vals, w_u)
            return out.reshape(N, T, D)
        key = jax.random.key(seed)
        ks = jax.random.split(key, 6)
        N, T = (2, 256)
        queries = jax.random.normal(ks[0], (N, T, D_MODEL), dtype=jnp.float32)
        Wq = jax.random.normal(ks[1], (D_MODEL, N_HEADS * D_KEYS), dtype=jnp.float32) / np.sqrt(D_MODEL)
        bq = jnp.zeros((N_HEADS * D_KEYS,), dtype=jnp.float32)
        bound = 1.0 / np.sqrt(HALF)
        keys = jax.random.uniform(ks[2], (N_HEADS, 2, N_KEYS, HALF), dtype=jnp.float32, minval=-bound, maxval=bound)
        w_down = jax.random.normal(ks[3], (N_KEYS * N_KEYS, D_MODEL), dtype=jnp.float32) * 0.02
        w_up = jax.random.normal(ks[4], (N_KEYS * N_KEYS, D_MODEL), dtype=jnp.float32) * 0.02
        return {'queries': queries, 'Wq': Wq, 'bq': bq, 'keys': keys, 'w_down': w_down, 'w_up': w_up}
    _L0_ffn_all = _L0_ffn_setup()
    _L0_ffn_in = {k: v for k, v in _L0_ffn_all.items() if k in ('Wq', 'bq', 'keys', 'w_down', 'w_up')}
    del _L0_ffn_all

    def _L1_attn_setup():
        import jax, jax.numpy as jnp
        import numpy as np
        HIGHEST = jax.lax.Precision.HIGHEST
        KEY_CHUNK_SIZE = 1024 * 4
        HEADS = 8
        DIM_HEAD = 64

        def _query_chunk_size(num_q: int) -> int:
            if num_q % 64 == 0:
                return num_q // 64
            if num_q % 16 == 0:
                return num_q // 16
            if num_q % 4 == 0:
                return num_q // 4
            return num_q

        def _me_attention(q, k, v, q_chunk: int, k_chunk: int):
            S, H, D = q.shape
            num_kv = k.shape[0]
            k_chunk = min(k_chunk, num_kv)
            q = q / jnp.sqrt(jnp.asarray(D, q.dtype))
            kc = k.reshape(-1, k_chunk, H, D)
            vc = v.reshape(-1, k_chunk, H, v.shape[-1])

            def per_qchunk(qch):

                def summarize(args):
                    kch, vch = args
                    s = jnp.einsum('qhd,khd->qhk', qch, kch, precision=HIGHEST)
                    m = jax.lax.stop_gradient(jnp.max(s, axis=-1, keepdims=True))
                    e = jnp.exp(s - m)
                    ev = jnp.einsum('khf,qhk->qhf', vch, e, precision=HIGHEST)
                    return (ev, e.sum(axis=-1), m[..., 0])
                evs, ews, ms = jax.lax.map(summarize, (kc, vc))
                gm = jnp.max(ms, axis=0)
                sc = jnp.exp(ms - gm)
                num = (evs * sc[..., None]).sum(axis=0)
                den = (ews * sc).sum(axis=0)
                return num / den[..., None]
            qs = q.reshape(-1, q_chunk, H, D)
            out = jax.lax.map(per_qchunk, qs)
            return out.reshape(S, H, -1)

        def _forward(hidden_states, w_q, w_k, w_v, w_out, b_out):
            B, S, Dm = hidden_states.shape
            H, dh = (HEADS, DIM_HEAD)
            q = hidden_states @ w_q
            k = hidden_states @ w_k
            v = hidden_states @ w_v

            def to_heads(t):
                return t.reshape(B, S, H, dh).transpose(0, 2, 1, 3).reshape(B * H, S, dh)
            qs, ks, vs = (to_heads(q), to_heads(k), to_heads(v))
            qcs = _query_chunk_size(S)
            attn = _me_attention(qs.transpose(1, 0, 2), ks.transpose(1, 0, 2), vs.transpose(1, 0, 2), qcs, KEY_CHUNK_SIZE)
            attn = attn.transpose(1, 0, 2)
            attn = attn.reshape(B, H, S, dh).transpose(0, 2, 1, 3).reshape(B, S, H * dh)
            return attn @ w_out + b_out
        key = jax.random.key(seed)
        ks = jax.random.split(key, 6)
        B, S, Dm = (2, 2048, 128)
        inner = HEADS * DIM_HEAD
        return {'hidden_states': jax.random.normal(ks[0], (B, S, Dm), dtype=jnp.float32), 'w_q': jax.random.normal(ks[1], (Dm, inner), dtype=jnp.float32) * 0.02, 'w_k': jax.random.normal(ks[2], (Dm, inner), dtype=jnp.float32) * 0.02, 'w_v': jax.random.normal(ks[3], (Dm, inner), dtype=jnp.float32) * 0.02, 'w_out': jax.random.normal(ks[4], (inner, Dm), dtype=jnp.float32) * 0.02, 'b_out': jnp.zeros((Dm,), dtype=jnp.float32)}
    _L1_attn_all = _L1_attn_setup()
    _L1_attn_in = {k: v for k, v in _L1_attn_all.items() if k in ('w_q', 'w_k', 'w_v', 'w_out', 'b_out')}
    del _L1_attn_all

    def _L1_ffn_setup():
        import jax, jax.numpy as jnp
        import numpy as np
        B, S, D = (8, 2048, 128)
        E, DFF = (16, 128)
        CAPACITY = 2
        key = jax.random.key(seed)
        ks = jax.random.split(key, 4)
        x = jax.random.normal(ks[0], (B, S, D), dtype=jnp.float32)
        gate_weight = jax.random.normal(ks[1], (D, E), dtype=jnp.float32) * 0.006
        w1 = jax.random.normal(ks[2], (E, D, DFF), dtype=jnp.float32) * 0.02
        b1 = jnp.zeros((E, DFF), dtype=jnp.float32)
        w2 = jax.random.normal(ks[3], (E, DFF, D), dtype=jnp.float32) * 0.02
        b2 = jnp.zeros((E, D), dtype=jnp.float32)
        return {'x': x, 'gate_weight': gate_weight, 'w1': w1, 'b1': b1, 'w2': w2, 'b2': b2}
    _L1_ffn_all = _L1_ffn_setup()
    _L1_ffn_in = {k: v for k, v in _L1_ffn_all.items() if k in ('gate_weight', 'w1', 'b1', 'w2', 'b2')}
    del _L1_ffn_all
    return {'x': x, 'itok_BS_0_4999': itok_BS_0_4999, 'fside_BS_numeric_value': fside_BS_numeric_value, 'mask_BS_i1_0': mask_BS_i1_0, 'L0_tok_event_table': _L0_tok_in['event_table'], 'L0_tok_value_table': _L0_tok_in['value_table'], 'L0_tok_w1': _L0_tok_in['w1'], 'L0_tok_b1': _L0_tok_in['b1'], 'L0_tok_w2': _L0_tok_in['w2'], 'L0_tok_b2': _L0_tok_in['b2'], 'L0_attn_Wq': _L0_attn_in['Wq'], 'L0_attn_bq': _L0_attn_in['bq'], 'L0_attn_Wk': _L0_attn_in['Wk'], 'L0_attn_bk': _L0_attn_in['bk'], 'L0_attn_Wv': _L0_attn_in['Wv'], 'L0_attn_bv': _L0_attn_in['bv'], 'L0_attn_Wo': _L0_attn_in['Wo'], 'L0_attn_bo': _L0_attn_in['bo'], 'L0_ffn_Wq': _L0_ffn_in['Wq'], 'L0_ffn_bq': _L0_ffn_in['bq'], 'L0_ffn_keys': _L0_ffn_in['keys'], 'L0_ffn_w_down': _L0_ffn_in['w_down'], 'L0_ffn_w_up': _L0_ffn_in['w_up'], 'L1_attn_w_q': _L1_attn_in['w_q'], 'L1_attn_w_k': _L1_attn_in['w_k'], 'L1_attn_w_v': _L1_attn_in['w_v'], 'L1_attn_w_out': _L1_attn_in['w_out'], 'L1_attn_b_out': _L1_attn_in['b_out'], 'L1_ffn_gate_weight': _L1_ffn_in['gate_weight'], 'L1_ffn_w1': _L1_ffn_in['w1'], 'L1_ffn_b1': _L1_ffn_in['b1'], 'L1_ffn_w2': _L1_ffn_in['w2'], 'L1_ffn_b2': _L1_ffn_in['b2']}

def reference(x, itok_BS_0_4999, fside_BS_numeric_value, mask_BS_i1_0, L0_tok_event_table, L0_tok_value_table, L0_tok_w1, L0_tok_b1, L0_tok_w2, L0_tok_b2, L0_attn_Wq, L0_attn_bq, L0_attn_Wk, L0_attn_bk, L0_attn_Wv, L0_attn_bv, L0_attn_Wo, L0_attn_bo, L0_ffn_Wq, L0_ffn_bq, L0_ffn_keys, L0_ffn_w_down, L0_ffn_w_up, L1_attn_w_q, L1_attn_w_k, L1_attn_w_v, L1_attn_w_out, L1_attn_b_out, L1_ffn_gate_weight, L1_ffn_w1, L1_ffn_b1, L1_ffn_w2, L1_ffn_b2):
    import jax
    import jax.numpy as jnp

    def _L0_tok_ref(event_idx, value_idx, numeric_value, value_type_mask, event_table, value_table, w1, b1, w2, b2):
        import jax, jax.numpy as jnp
        import numpy as np
        B, S = (32, 512)
        D = 128
        H = 64
        NE = 5000
        NV = 1250
        e_f = event_table[event_idx]
        e_v_cat = value_table[value_idx]
        x = numeric_value[..., None]
        h = jnp.tanh(x * w1[0] + b1)
        e_v_num = jnp.einsum('bsh,hd->bsd', h, w2) + b2
        mask = value_type_mask.astype(e_v_num.dtype)[..., None]
        e_v_num = e_v_num * mask
        return e_f + e_v_cat + e_v_num

    def _L0_attn_ref(z, Wq, bq, Wk, bk, Wv, bv, Wo, bo):
        import jax, jax.numpy as jnp
        import numpy as np
        B, N, DIM = (2, 512, 128)
        H = 8
        DH = DIM // H
        ALPHA = 1.0
        DELTA = 1.0
        EPS = 1e-05

        def _split_heads(x):
            b, n, _ = x.shape
            return x.reshape(b, n, H, DH).transpose(0, 2, 1, 3)
        Q = _split_heads(z @ Wq + bq)
        K = _split_heads(z @ Wk + bk)
        V = _split_heads(z @ Wv + bv)
        qk = jnp.einsum('bhnd,bhmd->bhnm', Q, K)
        mu_q = Q.mean(axis=-1, keepdims=True)
        var_q = ((Q - mu_q) ** 2).mean(axis=-1, keepdims=True)
        sigma_q = jnp.sqrt(var_q + EPS)
        nf_q = jnp.abs(Q - mu_q).sum(axis=-1, keepdims=True) / (sigma_q + EPS)
        q2 = (Q ** 2).sum(axis=-1)
        k2 = (K ** 2).sum(axis=-1)
        omega = q2[..., :, None] + k2[..., None, :] - 2.0 * qk
        omega = omega / (jnp.exp(-DELTA * nf_q) + 1.0)
        logits = qk / jnp.sqrt(jnp.float32(DH)) - ALPHA * omega
        A = jax.nn.softmax(logits, axis=-1)
        out = jnp.einsum('bhnm,bhmd->bhnd', A, V)
        out = out.transpose(0, 2, 1, 3).reshape(z.shape[0], z.shape[1], DIM)
        return out @ Wo + bo

    def _L0_ffn_ref(queries, Wq, bq, keys, w_down, w_up):
        import jax, jax.numpy as jnp
        import numpy as np
        from jax import lax
        N_HEADS = 8
        D_KEYS = 128
        HALF = D_KEYS // 2
        N_KEYS = 64
        TOP_K = 8
        D_MODEL = 128

        def _forward(queries, Wq, bq, keys, w_down, w_up):
            N, T, D = queries.shape
            x = queries.reshape(-1, D)
            q = (x @ Wq + bq).reshape(-1, N_HEADS, D_KEYS)
            q1, q2 = (q[..., :HALF], q[..., HALF:])
            s1 = jnp.einsum('bhc,hnc->bhn', q1, keys[:, 0])
            s2 = jnp.einsum('bhc,hnc->bhn', q2, keys[:, 1])
            s1t, i1 = lax.top_k(s1, TOP_K)
            s2t, i2 = lax.top_k(s2, TOP_K)
            all_scores = (s1t[..., :, None] + s2t[..., None, :]).reshape(-1, N_HEADS, TOP_K * TOP_K)
            all_idx = (i1[..., :, None] * N_KEYS + i2[..., None, :]).reshape(-1, N_HEADS, TOP_K * TOP_K)
            scores, best = lax.top_k(all_scores, TOP_K)
            indices = jnp.take_along_axis(all_idx, best, axis=-1)
            w_d = w_down[indices]
            w_u = w_up[indices]
            inner = jnp.einsum('bd,bhkd->bhk', x, w_d)
            vals = jax.nn.relu(inner) * jax.nn.softmax(scores, axis=-1)
            out = jnp.einsum('bhk,bhkd->bd', vals, w_u)
            return out.reshape(N, T, D)
        return _forward(queries, Wq, bq, keys, w_down, w_up)

    def _L1_attn_ref(hidden_states, w_q, w_k, w_v, w_out, b_out):
        import jax, jax.numpy as jnp
        import numpy as np
        HIGHEST = jax.lax.Precision.HIGHEST
        KEY_CHUNK_SIZE = 1024 * 4
        HEADS = 8
        DIM_HEAD = 64

        def _query_chunk_size(num_q: int) -> int:
            if num_q % 64 == 0:
                return num_q // 64
            if num_q % 16 == 0:
                return num_q // 16
            if num_q % 4 == 0:
                return num_q // 4
            return num_q

        def _me_attention(q, k, v, q_chunk: int, k_chunk: int):
            S, H, D = q.shape
            num_kv = k.shape[0]
            k_chunk = min(k_chunk, num_kv)
            q = q / jnp.sqrt(jnp.asarray(D, q.dtype))
            kc = k.reshape(-1, k_chunk, H, D)
            vc = v.reshape(-1, k_chunk, H, v.shape[-1])

            def per_qchunk(qch):

                def summarize(args):
                    kch, vch = args
                    s = jnp.einsum('qhd,khd->qhk', qch, kch, precision=HIGHEST)
                    m = jax.lax.stop_gradient(jnp.max(s, axis=-1, keepdims=True))
                    e = jnp.exp(s - m)
                    ev = jnp.einsum('khf,qhk->qhf', vch, e, precision=HIGHEST)
                    return (ev, e.sum(axis=-1), m[..., 0])
                evs, ews, ms = jax.lax.map(summarize, (kc, vc))
                gm = jnp.max(ms, axis=0)
                sc = jnp.exp(ms - gm)
                num = (evs * sc[..., None]).sum(axis=0)
                den = (ews * sc).sum(axis=0)
                return num / den[..., None]
            qs = q.reshape(-1, q_chunk, H, D)
            out = jax.lax.map(per_qchunk, qs)
            return out.reshape(S, H, -1)

        def _forward(hidden_states, w_q, w_k, w_v, w_out, b_out):
            B, S, Dm = hidden_states.shape
            H, dh = (HEADS, DIM_HEAD)
            q = hidden_states @ w_q
            k = hidden_states @ w_k
            v = hidden_states @ w_v

            def to_heads(t):
                return t.reshape(B, S, H, dh).transpose(0, 2, 1, 3).reshape(B * H, S, dh)
            qs, ks, vs = (to_heads(q), to_heads(k), to_heads(v))
            qcs = _query_chunk_size(S)
            attn = _me_attention(qs.transpose(1, 0, 2), ks.transpose(1, 0, 2), vs.transpose(1, 0, 2), qcs, KEY_CHUNK_SIZE)
            attn = attn.transpose(1, 0, 2)
            attn = attn.reshape(B, H, S, dh).transpose(0, 2, 1, 3).reshape(B, S, H * dh)
            return attn @ w_out + b_out
        return _forward(hidden_states, w_q, w_k, w_v, w_out, b_out)

    def _L1_ffn_ref(x, gate_weight, w1, b1, w2, b2):
        import jax, jax.numpy as jnp
        import numpy as np
        B, S, D = (8, 2048, 128)
        E, DFF = (16, 128)
        CAPACITY = 2
        Bx, Sx, Dx = x.shape
        num_experts = gate_weight.shape[1]
        k = Sx // num_experts * CAPACITY
        logits = jnp.einsum('bsd,de->bse', x, gate_weight)
        affinity = jax.nn.softmax(logits, axis=-1).transpose(0, 2, 1)
        gating, index = jax.lax.top_k(affinity, k)
        x_in = jnp.take_along_axis(x[:, None, :, :], index[..., None], axis=2)
        h = jax.nn.gelu(jnp.einsum('bekd,edh->bekh', x_in, w1) + b1[None, :, None, :])
        x_e = jnp.einsum('bekh,ehd->bekd', h, w2) + b2[None, :, None, :]
        weighted = gating[..., None] * x_e
        out = jnp.zeros_like(x)
        idx_flat = index.reshape(Bx, num_experts * k)
        vals_flat = weighted.reshape(Bx, num_experts * k, Dx)
        out = out.at[jnp.arange(Bx)[:, None], idx_flat].add(vals_flat)
        return out
    h = _L0_tok_ref(x, itok_BS_0_4999, fside_BS_numeric_value, mask_BS_i1_0, L0_tok_event_table, L0_tok_value_table, L0_tok_w1, L0_tok_b1, L0_tok_w2, L0_tok_b2)
    h = h + _L0_attn_ref(_layernorm(h, axis=-1), L0_attn_Wq, L0_attn_bq, L0_attn_Wk, L0_attn_bk, L0_attn_Wv, L0_attn_bv, L0_attn_Wo, L0_attn_bo)
    h = h + _L0_ffn_ref(_layernorm(h, axis=-1), L0_ffn_Wq, L0_ffn_bq, L0_ffn_keys, L0_ffn_w_down, L0_ffn_w_up)
    h = h + _L1_attn_ref(_layernorm(h, axis=-1), L1_attn_w_q, L1_attn_w_k, L1_attn_w_v, L1_attn_w_out, L1_attn_b_out)
    h = h + _L1_ffn_ref(_layernorm(h, axis=-1), L1_ffn_gate_weight, L1_ffn_w1, L1_ffn_b1, L1_ffn_w2, L1_ffn_b2)
    return h

_drawn_inputs = setup_inputs


def setup_inputs(seed=0):
    import zlib

    import numpy as np

    out = dict(_drawn_inputs(seed))
    spreads = {'L0_tok_b1': (0.0, 0.1),
     'L0_tok_b2': (0.0, 0.1),
     'L0_attn_bq': (0.0, 0.589),
     'L0_attn_bk': (0.0, 0.702),
     'L0_attn_bv': (0.0, 0.1),
     'L0_attn_bo': (0.0, 0.1),
     'L0_ffn_bq': (0.0, 0.8),
     'L1_attn_b_out': (0.0, 0.1),
     'L1_ffn_b1': (0.0, 0.8),
     'L1_ffn_b2': (0.0, 0.526)}
    factors = {'L0_attn_Wk': 2.793,
     'L0_ffn_Wq': 8.0,
     'L0_ffn_keys': 8.0,
     'L0_ffn_w_down': 8.0,
     'L0_ffn_w_up': 8.0,
     'L1_attn_w_q': 8.0,
     'L1_attn_w_k': 8.0,
     'L1_ffn_gate_weight': 3.821,
     'L1_ffn_w1': 8.0,
     'L1_ffn_w2': 8.0}
    for name, (base, spread) in spreads.items():
        noise = np.random.default_rng([zlib.crc32(name.encode()), seed]).standard_normal(out[name].shape)
        drawn = base * np.exp(spread * noise) if base else spread * noise
        out[name] = jnp.asarray(drawn.astype(out[name].dtype))
    for name, factor in factors.items():
        out[name] = (out[name] * factor).astype(out[name].dtype)
    return out
```

```python
import concourse.bass as bass
from concourse import mybir
from contextlib import ExitStack



def tower(nc, x_idx, val_idx, num_rows, mask_idx, event_table, value_table, tok_w1, tok_b1, tok_w2b2,
          a0_wqkv, a0_bqkv, a0_wo, a0_bo, pk_wqT, pk_bq, pk_keys, pk_down, pk_up,
          a1_wq, a1_wk, a1_wv, a1_wo, a1_bo, moe_gate, moe_w1, moe_b1, moe_w2, moe_b2, out):
    F32, BF16 = mybir.dt.float32, mybir.dt.bfloat16
    I32, U32 = mybir.dt.int32, mybir.dt.uint32
    ALU, ACT, AX = mybir.AluOpType, mybir.ActivationFunctionType, mybir.AxisListType
    ds = bass.ds

    P = 128
    B, S, D = 4, 512, 128
    TPB = S // P
    NT = B * TPB
    EPS = 1e-5
    HD = tok_w1.shape[0]
    H = 8
    UNITS = H * TPB
    DH0 = D // H
    AUG = 32
    HPG = P // AUG
    DH1 = 64
    HP = P // DH1
    PAIRS = H // HP
    NK, TOP = 64, 8
    HK = H * TOP
    NU, NV = 128, 32
    HALF = P // 2
    GT = 16
    GP = HALF // GT
    IG = 4
    NE, CAP = 16, S // 16 * 2
    EP = 32

    with ExitStack() as ctx:
        def sb(name, shape, dt=F32):
            return ctx.enter_context(nc.sbuf_tensor(name, shape, dt))

        def sem(name):
            return ctx.enter_context(nc.semaphore(name))

        bank = [ctx.enter_context(nc.psum_tensor(f"bank{i}", [P, 512], F32)) for i in range(2)]
        quad = ctx.enter_context(nc.psum_tensor("quad", [P, 4, 512], F32))
        bank += [quad[:, i, :] for i in range(4)]
        bank += [ctx.enter_context(nc.psum_tensor(f"bank{i}", [P, 512], F32)) for i in (6, 7)]

        h = sb("h", [P, NT * D])
        ident = sb("ident", [P, P])
        ones = sb("ones", [P, P])
        mhalf = sb("mhalf", [P, TPB * H])
        phalf = sb("phalf", [P, TPB * H])

        def h_tile(t):
            return h[:, ds(t * D, D)]

        stats = sb("stats", [P, TPB, 6])
        mv = sb("mv", [P, TPB, 2])
        veps = sb("veps", [P, TPB])
        rstd = sb("rstd", [P, TPB])
        xn = sb("xn", [P, TPB, D])
        xnT = sb("xnT", [P, S])

        region_r = sb("region_r", [P, 4096])
        region_v = sb("region_v", [P, 4096])
        region_a = sb("region_a", [P, 4096])
        region_iota = sb("region_iota", [P, 4096])
        region_down = sb("region_down", [P, 4096])
        region_up = sb("region_up", [P, 4096])

        ev_rows = region_r[:, 0:2048]
        vv_rows = region_r[:, 2048:4096]
        num_b = region_v[0:HD, 0:2048]
        tanhT = region_v[0:HD + 1, 2048:4096]
        idx_e = sb("idx_e", [P, NT], I32)
        idx_v = sb("idx_v", [P, NT], I32)
        mask_i = sb("mask_i", [P, NT], I32)
        mask_f = sb("mask_f", [P, NT])
        w1c = sb("w1c", [HD, 1])
        b1c = sb("b1c", [HD, 1])
        w2b2 = sb("w2b2", [HD + 1, D])

        wqkv0 = sb("wqkv0", [P, 3 * D])
        bqkv0 = sb("bqkv0", [1, 3 * D])
        wo0 = sb("wo0", [P, D])
        bo0 = sb("bo0", [1, D])
        qkv0 = region_r[:, 0:TPB * 3 * D].rearrange("p (j c) -> p j c", j=TPB)
        q_aug = region_v[:, 0:1024].rearrange("p (j h a) -> p j h a", j=TPB, h=H)
        k_aug = region_v[:, 1024:2048].rearrange("p (j h a) -> p j h a", j=TPB, h=H)
        qT0 = region_v[:, 2048:3072].rearrange("p (g t) -> p g t", g=2)
        kT0 = region_v[:, 3072:4096].rearrange("p (g t) -> p g t", g=2)
        dev = region_r[:, 1536:2048].rearrange("p (j h d) -> p j h d", j=TPB, h=H)
        sqr = region_r[:, 2048:2560].rearrange("p (j h d) -> p j h d", j=TPB, h=H)
        st0 = sb("st0", [P, 12, TPB, H])

        e_sb = sb("e_sb", [P, 3, S])
        eT_sb = sb("eT_sb", [P, 2, S])
        negmax = sb("negmax", [P, 4])
        rowsum = sb("rowsum", [P, 2, H])
        rrec = sb("rrec", [P, H])
        o_sb = sb("o_sb", [P, 512])
        oT_sb = sb("oT_sb", [P, 512])

        wd = region_down[:, :].rearrange("p (v u) -> p v u", v=NV)
        wu = region_up[:, :].rearrange("p (v d) -> p v d", v=NV)
        relu_in = region_r[:, :].rearrange("p (v t) -> p v t", v=NV)
        vals = region_v[:, :].rearrange("p (v t) -> p v t", v=NV)
        one_u = region_a[:, :].bitcast(BF16).rearrange("p (u t) -> p u t", u=NU)
        iota_u = region_iota[:, :].bitcast(BF16).rearrange("p (u t) -> p u t", u=NU)
        one_v = sb("one_v", [P, NV, HALF], BF16)
        w_v = sb("w_v", [P, 3, NV, HALF], BF16)
        iota8 = sb("iota8", [P, HK, TOP])
        wqT_s = region_v[:, 0:1024].rearrange("p (h d) -> p h d", h=H)
        keys_s = region_v[:, 1024:2048].rearrange("p (h n) -> p h n", h=H)
        bqb_s = region_v[:, 2048:3072].rearrange("p (h t) -> p h t", h=H)
        bq_s = sb("bq_s", [P, H])
        keyw = sb("keyw", [P, H * P])
        keyb = sb("keyb", [P, H * P])
        sc = sb("sc", [P, H, 2, NK])
        m8 = sb("m8", [P, H, 2, TOP])
        i8 = sb("i8", [P, H, 2, TOP], U32)
        pair_s = sb("pair_s", [P, H, TOP, TOP])
        b8 = sb("b8", [P, H, TOP])
        bi = sb("bi", [P, H, TOP], U32)
        bab = sb("bab", [P, 2, HK], U32)
        ext = sb("ext", [P, 2, HK, TOP])
        ij = sb("ij", [P, 2, HK])
        jhi = sb("jhi", [P, HK])
        uvp = sb("uvp", [P, 3, 2, HK])
        pe_ = sb("pe_", [P, H, TOP])
        pz = sb("pz", [P, 2, H])
        uT = sb("uT", [P, HALF], BF16)
        vT = sb("vT", [P, HALF], BF16)
        pT = sb("pT", [P, HALF])
        pres = sb("pres", [P, 2, HALF])
        psp = sb("psp", [P, 3, HALF], BF16)

        wq1 = sb("wq1", [P, H * DH1])
        wk1 = sb("wk1", [P, H * DH1])
        wv1 = region_iota[:, 0:512]
        wo1 = region_iota[:, 512:1024].rearrange("p (c d) -> p c d", c=PAIRS)
        bo1 = sb("bo1", [1, D])
        qT1 = region_r[:, 0:2048].rearrange("p (c t) -> p c t", c=PAIRS)
        kT1 = region_r[:, 2048:4096].rearrange("p (c t) -> p c t", c=PAIRS)
        v1 = region_v[:, 0:2048].rearrange("p (j c) -> p j c", j=TPB)

        w1e = region_down[:, 0:2048].rearrange("p (e f) -> p e f", e=NE)
        w2e = region_down[:, 2048:4096].rearrange("p (e f) -> p e f", e=NE)
        b1e = sb("b1e", [P, NE])
        b2e = region_iota[:, 1024:1152]
        gate_w = sb("gate_w", [P, NE])
        xnT_all = region_up[:, 0:B * S]
        logit = region_up[:, 2048:2304].rearrange("p (j b e) -> p j b e", j=TPB, b=B)
        aff = region_up[:, 2304:2816].rearrange("p (j b e) -> p j b e", j=TPB, b=B)
        rmax = sb("rmax", [P, 2, NT])
        affT = region_a[:, 0:512]
        work = region_a[:, 512:1024]
        gT = region_a[:, 1024:1536]
        gN = region_a[:, 1536:2048]
        top8 = sb("top8", [P, 8])
        hidT = region_a[:, 2048:3072].rearrange("p (r t) -> p r t", r=2)

        consts = sem("consts_ready")
        ld_idx, ld_tok, ld_a0, ld_pk, ld_exp = sem("ld_idx"), sem("ld_tok"), sem("ld_a0"), sem("ld_pk"), sem("ld_exp")
        ld_a1, ld_moe, gath = sem("ld_a1"), sem("ld_moe"), sem("rows_gathered")
        tanh_done, emb_ps, h_ready = sem("tanh_done"), sem("emb_ps"), sem("h_ready")
        out_dma = sem("out_dma")

        class LN:
            def __init__(self, n):
                self.var = sem(n + "_var_ready")
                self.rstd = sem(n + "_rstd_ready")
                self.xn = sem(n + "_xn_ready")
                self.ps = sem(n + "_xnT_in_psum")
                self.sb = sem(n + "_xnT_in_sbuf")

        lnB, lnC, lnD, lnE = LN("lnB"), LN("lnC"), LN("lnD"), LN("lnE")

        class ATT:
            def __init__(self, n, dh, ln):
                self.dh, self.ln = dh, ln
                self.chunks = H * dh // P
                self.qk = sem(n + "_logits_in_psum")
                self.mx = sem(n + "_max_ready")
                self.ex = sem(n + "_exp_done")
                self.tr = sem(n + "_expT_in_psum")
                self.ev = [sem(n + "_expT_by_dve"), sem(n + "_expT_by_act")]
                self.pv = sem(n + "_pv_done")
                self.norm = sem(n + "_out_normalised")
                self.otp = sem(n + "_outT_in_psum")
                self.ots = sem(n + "_outT_in_sbuf")
                self.proj = sem(n + "_projected")
                self.add = sem(n + "_h_added")

        a0, a1 = ATT("a0", DH0, lnB), ATT("a1", DH1, lnD)
        qkv_ps, qkv_sb = sem("qkv_in_psum"), sem("qkv_in_sbuf")
        sig2, sigma, nf, enf, aug = sem("q_var"), sem("q_sigma"), sem("q_nf"), sem("q_exp_nf"), sem("aug_ready")
        augT_ps, augT_sb = sem("augT_in_psum"), sem("augT_in_sbuf")
        p1_ps, p1_sb = sem("proj1_in_psum"), sem("proj1_in_sbuf")

        bq_b, kw_ps, kw_sb = sem("bq_spread"), sem("keyw_in_psum"), sem("keyw_in_sbuf")
        sc_ps, sc_sb, best, pexp, uvp_rdy = sem("scores_in_psum"), sem("scores_in_sbuf"), sem("best_ready"), sem("pexp"), sem("uvp_ready")
        uvpT_ps, uvpT_sb, onehot = sem("uvpT_in_psum"), sem("uvpT_in_sbuf"), sem("onehot_ready")
        g_ps, vals_rdy, in_ps, relu_rdy = sem("g_in_psum"), sem("vals_ready"), sem("inner_in_psum"), sem("relu_ready")
        ffn_ps, ffn_add = sem("ffn_in_psum"), sem("ffn_added")

        lg_ps, lg_sb, lg_exp_in, lg_exp, aff_rdy = sem("gate_in_psum"), sem("gate_max"), sem("gate_exp_in"), sem("gate_exp"), sem("aff_ready")
        affT_ps, affT_sb, gT_rdy, gN_ps, gN_rdy = sem("affT_in_psum"), sem("affT_in_sbuf"), sem("gT_ready"), sem("gN_in_psum"), sem("gN_ready")
        hid_ps, hid_sb, y_ps, y_add, b2_ps = sem("hid_in_psum"), sem("hid_ready"), sem("y_in_psum"), sem("y_added"), sem("b2_in_psum")
        seq_done = sem("sequence_done")

        block = ctx.enter_context(nc.Block())

        @block.sync
        def _(sp):
            sp.dma_start(idx_e[:], x_idx).then_inc(ld_idx, 16)
            sp.dma_start(idx_v[:], val_idx).then_inc(ld_idx, 16)
            sp.dma_start(mask_i[:], mask_idx).then_inc(ld_tok, 16)
            sp.dma_start(num_b, num_rows.partition_broadcast(HD)).then_inc(ld_tok, 16)
            sp.dma_start(w1c[:], tok_w1).then_inc(ld_tok, 16)
            sp.dma_start(b1c[:], tok_b1).then_inc(ld_tok, 16)
            sp.dma_start(w2b2[:], tok_w2b2).then_inc(ld_tok, 16)
            sp.dma_start(wqkv0[:], a0_wqkv).then_inc(ld_a0, 16)
            sp.dma_start(bqkv0[:], a0_bqkv).then_inc(ld_a0, 16)
            sp.dma_start(wo0[:], a0_wo).then_inc(ld_a0, 16)
            sp.dma_start(bo0[:], a0_bo).then_inc(ld_a0, 16)
            sp.dma_start(region_down[:], pk_down).then_inc(ld_exp, 16)
            sp.dma_start(region_up[:], pk_up).then_inc(ld_exp, 16)
            sp.dma_start(bq_s[:], pk_bq).then_inc(ld_pk, 16)
            sp.dma_start(wq1[:], a1_wq).then_inc(ld_a1, 16)
            sp.dma_start(wk1[:], a1_wk).then_inc(ld_a1, 16)
            sp.dma_start(bo1[:], a1_bo).then_inc(ld_a1, 16)
            sp.dma_start(gate_w[:], moe_gate).then_inc(ld_moe, 16)
            sp.dma_start(b1e[:], moe_b1).then_inc(ld_moe, 16)
            sp.wait_ge(a0.add, B * TPB)
            sp.dma_start(region_v[:, 0:1024], pk_wqT).then_inc(ld_pk, 16)
            sp.dma_start(region_v[:, 1024:2048], pk_keys).then_inc(ld_pk, 16)
            sp.wait_ge(ffn_add, NT)
            sp.dma_start(wv1, a1_wv).then_inc(ld_a1, 16)
            sp.dma_start(region_iota[:, 512:1024], a1_wo).then_inc(ld_a1, 16)
            sp.dma_start(b2e, moe_b2).then_inc(ld_moe, 16)
            sp.dma_start(region_down[:, 0:2048], moe_w1).then_inc(ld_moe, 16)
            sp.dma_start(region_down[:, 2048:4096], moe_w2).then_inc(ld_moe, 16)
            for b in range(B):
                sp.wait_ge(seq_done, b + 1)
                sp.dma_start(out[b].rearrange("(j p) d -> p j d", p=P),
                             h[:, b * S:(b + 1) * S].rearrange("p (j d) -> p j d", j=TPB)).then_inc(out_dma, 16)
            sp.wait_ge(out_dma, 16 * B)

        @block.gpsimd
        def _(pool):
            pool.wait_ge(ld_idx, 32)
            for t in range(NT):
                for rows, idx, table in ((ev_rows, idx_e, event_table), (vv_rows, idx_v, value_table)):
                    nc.gpsimd.indirect_dma_start(
                        out=rows[:, t * D:(t + 1) * D], out_offset=None, in_=table,
                        in_offset=bass.IndirectOffsetOnAxis(ap=idx[:, t:t + 1].bitcast(U32), axis=0)).then_inc(gath, 16)
            nc.gpsimd.memset(ident[:], 0.0)
            nc.gpsimd.memset(ones[:], 1.0)
            nc.gpsimd.memset(mhalf[:], -0.5)
            nc.gpsimd.memset(phalf[:], 0.5)
            pool.drain()
            nc.gpsimd.affine_select(out=ident[:], in_=ident[:], compare_op=ALU.not_equal, fill=1.0, base=0,
                                    pattern=[[-1, P]], channel_multiplier=1).then_inc(consts, 1)
            nc.gpsimd.iota(iota_u, [[1, NU], [0, HALF]], base=0, channel_multiplier=0,
                           allow_small_or_imprecise_dtypes=True).then_inc(consts, 1)
            nc.gpsimd.iota(iota8[:], [[0, HK], [1, TOP]], base=0, channel_multiplier=0,
                           allow_small_or_imprecise_dtypes=True).then_inc(consts, 1)

            def rstd_step(ln, i, n):
                pool.wait_ge(ln.var, i + 1)
                nc.gpsimd.tensor_tensor(rstd[:, 0:n], veps[:, 0:n], mhalf[:, 0:n], ALU.pow).then_inc(ln.rstd, 1)

            with pool.Fori(0, B) as b:
                rstd_step(lnB, b, TPB)
                pool.wait_ge(sig2, b + 1)
                nc.gpsimd.tensor_tensor(st0[:, 2], st0[:, 1], phalf[:].rearrange("p (j h) -> p j h", j=TPB),
                                        ALU.pow).then_inc(sigma, 1)
            with pool.Fori(0, NT) as t:
                rstd_step(lnC, t, 1)
            with pool.Fori(0, B) as b:
                rstd_step(lnD, b, TPB)
            with pool.Fori(0, B) as b:
                rstd_step(lnE, b, TPB)

        @block.scalar
        def _(act):
            def copy_xnT(ln, i, n=S, src=None, dst=None):
                act.wait_ge(ln.ps, i + 1)
                nc.scalar.copy(xnT[:, 0:n] if dst is None else dst,
                               bank[7][:, 0:n]).then_inc(ln.sb, 1)

            def attention(a, b):
                def exp(s):
                    act.wait_ge(a.mx, b * UNITS + s + 1)
                    if s >= 3:
                        act.wait_ge(a.tr, b * UNITS + s - 2)
                    if s % H == 0 and s >= 2 * H:
                        act.wait_ge(a.norm, b * TPB + s // H - 1)
                    nc.scalar.activation(e_sb[:, s % 3, :], bank[s % 2][:, :], ACT.Exp,
                                         bias=negmax[:, s % 4:s % 4 + 1],
                                         accum_out=rowsum[:, (s // H) % 2, s % H:s % H + 1]).then_inc(a.ex, 1)

                def expT(s):
                    act.wait_ge(a.tr, b * UNITS + s + 1)
                    if s >= 2:
                        act.wait_ge(a.pv, b * UNITS + s - 1)
                    nc.scalar.copy(eT_sb[:, s % 2, :], bank[2 + s % 2]).then_inc(a.ev[1], 1)

                def outT(j):
                    act.wait_ge(a.otp, b * TPB + j + 1)
                    nc.scalar.copy(oT_sb[:, 0:H * a.dh], bank[6][:, 0:H * a.dh]).then_inc(a.ots, 1)

                for s in range(UNITS + 6):
                    if s < UNITS:
                        exp(s)
                    if 0 <= s - 2 < UNITS and (s - 2) % 2:
                        expT(s - 2)
                    if s >= 13 and (s - 5) % H == 0:
                        outT((s - 5) // H - 1)

            act.wait_ge(ld_tok, 80)
            for b in range(B):
                nc.scalar.activation(tanhT[0:HD, b * S:(b + 1) * S], num_b[:, b * S:(b + 1) * S], ACT.Tanh,
                                     bias=b1c[:, 0:1], scale=w1c[:, 0:1]).then_inc(tanh_done, 1)
            with act.Fori(0, B) as b:
                copy_xnT(lnB, b)
                for j in range(TPB):
                    act.wait_ge(qkv_ps, b * TPB + j + 1)
                    nc.scalar.copy(qkv0[:, j, :], bank[j][:, 0:3 * D]).then_inc(qkv_sb, 1)
                act.wait_ge(nf, b + 1)
                nc.scalar.activation(st0[:, 6], st0[:, 5], ACT.Exp, scale=-1.0).then_inc(enf, 1)
                for n, dst in enumerate((qT0[:, 0], qT0[:, 1], kT0[:, 0], kT0[:, 1])):
                    act.wait_ge(augT_ps, b * 4 + n + 1)
                    nc.scalar.copy(dst, bank[n][:, :]).then_inc(augT_sb, 1)
                attention(a0, b)

            for n, (dst, src) in enumerate(((keyw, 0), (keyw, 1), (keyb, 2), (keyb, 3))):
                act.wait_ge(kw_ps, n + 1)
                nc.scalar.copy(dst[:, (src % 2) * 512:(src % 2) * 512 + 512], bank[src][:, :]).then_inc(kw_sb, 1)

            def relu_inner(t):
                if not (isinstance(t, int) and t == 0):
                    act.wait_ge(vals_rdy, t * GP)
                for g in range(NV // IG):
                    act.wait_ge(in_ps, t * (NV // IG) + g + 1)
                    nc.scalar.activation(relu_in[:, IG * g:IG * g + IG, :],
                                         bank[g % 2][:, :].rearrange("p (v t) -> p v t", v=IG),
                                         ACT.Relu).then_inc(relu_rdy, 1)

            def softmax_exp(t):
                act.wait_ge(best, t + 1)
                nc.scalar.activation(pe_[:], pe_[:], ACT.Exp).then_inc(pexp, 1)

            def copy_xnT_tile(t):
                if not (isinstance(t, int) and t == 0):
                    act.wait_ge(in_ps, t * (NV // IG))
                copy_xnT(lnC, t, P)

            def copy_uvpT(t):
                act.wait_ge(uvpT_ps, t + 1)
                for dst, c in ((uT, 1), (vT, 2), (pT, 3)):
                    for q in range(2):
                        last = nc.scalar.copy(dst[q * HALF:(q + 1) * HALF, :],
                                              bank[7][q * HALF:(q + 1) * HALF,
                                                      c * P + q * HALF:c * P + (q + 1) * HALF])
                last.then_inc(uvpT_sb, 1)

            copy_xnT_tile(0)
            relu_inner(0)
            softmax_exp(0)
            with act.Fori(0, NT - 1) as t:
                copy_uvpT(t)
                copy_xnT_tile(t + 1)
                relu_inner(t + 1)
                softmax_exp(t + 1)
            copy_uvpT(NT - 1)

            with act.Fori(0, B) as b:
                copy_xnT(lnD, b)
                for n in range(3 * PAIRS):
                    act.wait_ge(p1_ps, b * 3 * PAIRS + n + 1)
                    kind, c = n // PAIRS, n % PAIRS
                    src = bank[n % 4][:, :]
                    if kind == 0:
                        nc.scalar.mul(qT1[:, c, :], src, DH1 ** -0.5).then_inc(p1_sb, 1)
                    else:
                        nc.scalar.copy(kT1[:, c, :] if kind == 1 else v1[:, c, :], src).then_inc(p1_sb, 1)
                attention(a1, b)

            for b in range(B):
                act.wait_ge(lnE.ps, b + 1)
                nc.scalar.copy(xnT[:], bank[7][:, :])
                nc.scalar.copy(xnT_all[:, b * S:(b + 1) * S], bank[7][:, :]).then_inc(lnE.sb, 1)
            act.wait_ge(lg_exp_in, 1)
            nc.scalar.activation(logit, logit, ACT.Exp).then_inc(lg_exp, 1)
            act.wait_ge(affT_ps, 1)
            nc.scalar.copy(affT, bank[0][:, :]).then_inc(affT_sb, 1)
            act.wait_ge(gN_ps, 1)
            nc.scalar.copy(gN, bank[1][:, :]).then_inc(gN_rdy, 1)
            with act.Fori(0, B) as b:
                for e in range(NE):
                    act.wait_ge(hid_ps, b * NE + e + 1)
                    if e >= 2:
                        act.wait_ge(y_ps, b * NE + e - 1)
                    nc.scalar.activation(hidT[:, e % 2, :], bank[e % 2][:, :], ACT.Gelu_apprx_tanh,
                                         bias=b1e[:, e:e + 1]).then_inc(hid_sb, 1)

        @block.vector
        def _(dve):
            V = nc.vector

            def layer_norm(ln, i, first, n):
                for j in range(n):
                    V.bn_stats(stats[:, j, :], h_tile(first + j))
                dve.drain()
                for j in range(n):
                    V.bn_aggr(mv[:, j, :], stats[:, j, :])
                dve.drain()
                V.tensor_scalar(veps[:, 0:n], mv[:, 0:n, 1], EPS, None, ALU.add).then_inc(ln.var, 1)
                if ln is lnE and i:
                    dve.wait_ge(ln.ps, i)
                dve.wait_ge(ln.rstd, i + 1)
                for j in range(n):
                    last = V.tensor_scalar(xn[:, j, :], h_tile(first + j), mv[:, j, 0:1], rstd[:, j:j + 1],
                                           ALU.subtract, ALU.mult)
                last.then_inc(ln.xn, 1)

            def attention(a, b):
                def rowmax(s):
                    dve.wait_ge(a.qk, b * UNITS + s + 1)
                    V.tensor_reduce(negmax[:, s % 4:s % 4 + 1], bank[s % 2][:, :], AX.X, ALU.max,
                                    negate=True).then_inc(a.mx, 1)

                def expT(s):
                    dve.wait_ge(a.tr, b * UNITS + s + 1)
                    if s >= 2:
                        dve.wait_ge(a.pv, b * UNITS + s - 1)
                    V.tensor_copy(eT_sb[:, s % 2, :], bank[2 + s % 2]).then_inc(a.ev[0], 1)

                def normalise(j):
                    dve.wait_ge(a.pv, b * UNITS + H * (j + 1))
                    V.reciprocal(rrec[:], rowsum[:, j % 2, :])
                    dve.drain()
                    if j:
                        dve.wait_ge(a.otp, b * TPB + j)
                    V.tensor_tensor(o_sb[:, 0:H * a.dh].rearrange("p (h d) -> p h d", h=H),
                                    bank[4 + j % 2][:, 0:H * a.dh].rearrange("p (h d) -> p h d", h=H),
                                    rrec[:].unsqueeze(2).to_broadcast([P, H, a.dh]),
                                    ALU.mult).then_inc(a.norm, 1)

                def residual(j):
                    dve.wait_ge(a.proj, b * TPB + j + 1)
                    t = b * TPB + j
                    V.tensor_tensor(h_tile(t), h_tile(t), bank[7][:, 0:D], ALU.add).then_inc(a.add, 1)

                for s in range(UNITS + 6):
                    if s < UNITS:
                        rowmax(s)
                    if 0 <= s - 2 < UNITS and (s - 2) % 2 == 0:
                        expT(s - 2)
                    if s >= 11 and (s - 3) % H == 0:
                        normalise((s - 3) // H - 1)
                    if s >= 13 and (s - 5) % H == 0:
                        residual((s - 5) // H - 1)

            V.memset(tanhT[HD:HD + 1, :], 1.0).then_inc(tanh_done, 1)
            dve.wait_ge(ld_tok, 80)
            V.tensor_copy(mask_f[:], mask_i[:])
            dve.drain()
            dve.wait_ge(gath, 16 * 2 * NT)
            for b in range(B):
                span = slice(b * S, (b + 1) * S)
                dve.wait_ge(emb_ps, b + 1)
                V.tensor_tensor(h[:, span].rearrange("p (j d) -> p j d", j=TPB),
                                bank[b][:, :].rearrange("p (j d) -> p j d", j=TPB),
                                mask_f[:, b * TPB:(b + 1) * TPB].unsqueeze(2).to_broadcast([P, TPB, D]), ALU.mult)
                V.tensor_tensor(ev_rows[:, span], ev_rows[:, span], vv_rows[:, span], ALU.add)
                dve.drain()
                V.tensor_tensor(h[:, span], h[:, span], ev_rows[:, span], ALU.add)
            dve.drain()

            V.memset(q_aug, 0.0)
            V.memset(k_aug, 0.0)
            dve.drain()
            V.memset(k_aug[:, :, :, DH0 + 1:DH0 + 2], 1.0)
            with dve.Fori(0, B) as b:
                layer_norm(lnB, b, b * TPB, TPB)
                q4 = qkv0[:, :, 0:D].rearrange("p j (h d) -> p j h d", h=H)
                k4 = qkv0[:, :, D:2 * D].rearrange("p j (h d) -> p j h d", h=H)

                def wide(s):
                    return st0[:, s].unsqueeze(3).to_broadcast([P, TPB, H, DH0])

                dve.wait_ge(qkv_sb, b * TPB + TPB)
                V.tensor_reduce(st0[:, 0], q4, AX.X, ALU.add)
                V.tensor_tensor(sqr, k4, k4, ALU.mult)
                dve.drain()
                V.tensor_scalar(st0[:, 0], st0[:, 0], 1.0 / DH0, None, ALU.mult)
                V.tensor_reduce(st0[:, 9], sqr, AX.X, ALU.add)
                dve.drain()
                V.tensor_tensor(dev, q4, wide(0), ALU.subtract)
                V.tensor_copy(k_aug[:, :, :, DH0], st0[:, 9])
                dve.drain()
                V.tensor_tensor(sqr, dev, dev, ALU.mult)
                V.tensor_reduce(st0[:, 3], dev, AX.X, ALU.add, apply_absolute_value=True)
                dve.drain()
                V.tensor_reduce(st0[:, 1], sqr, AX.X, ALU.add)
                dve.drain()
                V.tensor_scalar(st0[:, 1], st0[:, 1], 1.0 / DH0, EPS, ALU.mult, ALU.add).then_inc(sig2, 1)
                V.tensor_tensor(sqr, q4, q4, ALU.mult)
                V.tensor_copy(k_aug[:, :, :, 0:DH0], k4)
                dve.drain()
                V.tensor_reduce(st0[:, 8], sqr, AX.X, ALU.add)
                dve.wait_ge(sigma, b + 1)
                V.tensor_scalar(st0[:, 4], st0[:, 2], EPS, None, ALU.add)
                dve.drain()
                V.reciprocal(st0[:, 4], st0[:, 4])
                dve.drain()
                V.tensor_tensor(st0[:, 5], st0[:, 3], st0[:, 4], ALU.mult).then_inc(nf, 1)
                dve.wait_ge(enf, b + 1)
                V.tensor_scalar(st0[:, 7], st0[:, 6], 1.0, None, ALU.add)
                dve.drain()
                V.reciprocal(st0[:, 7], st0[:, 7])
                dve.drain()
                V.tensor_scalar(st0[:, 10], st0[:, 7], 2.0, DH0 ** -0.5, ALU.mult, ALU.add)
                V.tensor_scalar(q_aug[:, :, :, DH0], st0[:, 7], -1.0, None, ALU.mult)
                dve.drain()
                V.tensor_tensor(q_aug[:, :, :, DH0 + 1], q_aug[:, :, :, DH0], st0[:, 8], ALU.mult)
                V.tensor_tensor(q_aug[:, :, :, 0:DH0], q4, wide(10), ALU.mult)
                dve.drain()
                V.engine_nop().then_inc(aug, 1)
                attention(a0, b)
                dve.drain()

            dve.wait_ge(ld_pk, 48)
            V.tensor_copy(bqb_s, bq_s[:].unsqueeze(2).to_broadcast([P, H, P])).then_inc(bq_b, 1)

            def scores_to_sbuf(t):
                for q in range(2):
                    dve.wait_ge(sc_ps, t * 2 + q + 1)
                    V.tensor_tensor(sc[:, 4 * q:4 * q + 4].rearrange("p h a n -> p (h a n)"), bank[q][:, :],
                                    keyb[:, q * 512:(q + 1) * 512], ALU.add).then_inc(sc_sb, 1)
                dve.drain()

            def half_max():
                for n in range(2 * H):
                    V.max(m8[:, n // 2, n % 2, :], sc[:, n // 2, n % 2, :])
                dve.drain()

            def half_index():
                for n in range(2 * H):
                    V.max_index(i8[:, n // 2, n % 2, :], m8[:, n // 2, n % 2, :], sc[:, n // 2, n % 2, :])
                V.tensor_tensor(pair_s[:], m8[:, :, 0, :].unsqueeze(3).to_broadcast([P, H, TOP, TOP]),
                                m8[:, :, 1, :].unsqueeze(2).to_broadcast([P, H, TOP, TOP]), ALU.add)
                dve.drain()

            def pair_best():
                for n in range(H):
                    V.max(b8[:, n, :], pair_s[:, n].rearrange("p a b -> p (a b)"))
                dve.drain()
                V.tensor_tensor(pe_[:], b8[:], b8[:, :, 0:1].to_broadcast([P, H, TOP]),
                                ALU.subtract).then_inc(best, 1)
                for n in range(H):
                    V.max_index(bi[:, n, :], b8[:, n, :], pair_s[:, n].rearrange("p a b -> p (a b)"))
                dve.drain()

            def expert_numbers(t):
                flat = bi[:].rearrange("p h k -> p (h k)")
                V.tensor_scalar(bab[:, 0], flat, 3, None, ALU.logical_shift_right)
                V.tensor_scalar(bab[:, 1], flat, TOP - 1, None, ALU.bitwise_and)
                dve.drain()
                V.tensor_tensor(ext[:].rearrange("p s k a -> p (s k) a"),
                                bab[:].rearrange("p s k -> p (s k)").unsqueeze(2).to_broadcast([P, 2 * HK, TOP]),
                                iota8[:, 0:1, :].to_broadcast([P, 2 * HK, TOP]), ALU.is_equal)
                dve.drain()
                for s in range(2):
                    V.tensor_tensor(ext[:, s].rearrange("p (h k) a -> p h k a", h=H),
                                    ext[:, s].rearrange("p (h k) a -> p h k a", h=H),
                                    i8[:, :, s, :].unsqueeze(2).to_broadcast([P, H, TOP, TOP]), ALU.mult)
                dve.drain()
                V.tensor_reduce(ij[:], ext[:], AX.X, ALU.add)
                dve.drain()
                V.tensor_scalar(jhi[:], ij[:, 1], float(NV), None, ALU.is_ge)
                dve.wait_ge(pexp, t + 1)
                V.tensor_reduce(pz[:, 0], pe_[:], AX.X, ALU.add)
                dve.drain()
                V.reciprocal(pz[:, 1], pz[:, 0])
                for q in range(2):
                    V.scalar_tensor_tensor(uvp[:, 0, q], ij[:, 0], 2.0, jhi[:], ALU.mult, ALU.add)
                    V.scalar_tensor_tensor(uvp[:, 1, q], jhi[:], -float(NV), ij[:, 1], ALU.mult, ALU.add)
                dve.drain()
                for q in range(2):
                    last = V.tensor_tensor(uvp[:, 2, q].rearrange("p (h k) -> p h k", h=H), pe_[:],
                                           pz[:, 1].unsqueeze(2).to_broadcast([P, H, TOP]), ALU.mult)
                last.then_inc(uvp_rdy, 1)

            def one_hots(t):
                dve.wait_ge(uvpT_sb, t + 1)
                V.tensor_copy(psp[:, 0], pT[:])
                V.tensor_tensor(one_u, iota_u, uT[:].unsqueeze(1).to_broadcast([P, NU, HALF]), ALU.is_equal)
                dve.drain()
                V.tensor_tensor(pres[:, 0], pT[:], psp[:, 0], ALU.subtract)
                V.tensor_tensor(one_v[:], iota_u[:, 0:NV, :], vT[:].unsqueeze(1).to_broadcast([P, NV, HALF]),
                                ALU.is_equal)
                dve.drain()
                V.tensor_copy(psp[:, 1], pres[:, 0])
                dve.drain()
                V.tensor_tensor(psp[:, 2], pres[:, 0], psp[:, 1], ALU.subtract)
                dve.drain()
                for s in range(3):
                    last = V.tensor_tensor(w_v[:, s], one_v[:], psp[:, s].unsqueeze(1).to_broadcast([P, NV, HALF]),
                                           ALU.mult)
                last.then_inc(onehot, 1)

            def weigh(t, c):
                dve.wait_ge(g_ps, t * GP + c + 1)
                if c == 0:
                    dve.wait_ge(relu_rdy, (t + 1) * (NV // IG))
                for q in range(2):
                    span = slice(q * HALF + c * GT, q * HALF + (c + 1) * GT)
                    last = V.tensor_tensor(vals[:, :, span], relu_in[:, :, span],
                                           quad[:, 2 * (c % 2) + q, :].rearrange("p (t v) -> p v t", v=NV), ALU.mult)
                last.then_inc(vals_rdy, 1)

            def ffn_residual(t):
                dve.wait_ge(ffn_ps, t + 1)
                V.tensor_tensor(h_tile(t), h_tile(t), bank[6][:, 0:D], ALU.add).then_inc(ffn_add, 1)

            dve.wait_ge(kw_sb, 4)
            dve.wait_ge(consts, 3)
            layer_norm(lnC, 0, 0, 1)
            scores_to_sbuf(0)
            half_max()
            half_index()
            pair_best()
            expert_numbers(0)
            with dve.Fori(0, NT - 1) as t:
                layer_norm(lnC, t + 1, t + 1, 1)
                one_hots(t)
                scores_to_sbuf(t + 1)
                weigh(t, 0)
                half_max()
                weigh(t, 1)
                half_index()
                weigh(t, 2)
                pair_best()
                weigh(t, 3)
                expert_numbers(t + 1)
                ffn_residual(t)
            one_hots(NT - 1)
            for c in range(GP):
                weigh(NT - 1, c)
            ffn_residual(NT - 1)
            dve.drain()

            with dve.Fori(0, B) as b:
                layer_norm(lnD, b, b * TPB, TPB)
                attention(a1, b)
                dve.drain()

            for b in range(B):
                layer_norm(lnE, b, b * TPB, TPB)
            V.memset(aff, 0.0)
            dve.wait_ge(lg_ps, B)
            l3 = logit.rearrange("p j b e -> p (j b) e")
            V.tensor_copy(l3, bank[0][:, 0:NT * NE].rearrange("p (n e) -> p n e", n=NT))
            dve.drain()
            V.tensor_reduce(rmax[:, 0], l3, AX.X, ALU.max)
            dve.drain()
            V.tensor_tensor(l3, l3, rmax[:, 0].unsqueeze(2).to_broadcast([P, NT, NE]),
                            ALU.subtract).then_inc(lg_exp_in, 1)
            dve.wait_ge(lg_exp, 1)
            V.tensor_reduce(rmax[:, 0], l3, AX.X, ALU.add)
            dve.drain()
            V.reciprocal(rmax[:, 1], rmax[:, 0])
            dve.drain()
            V.tensor_tensor(aff.rearrange("p j b e -> p (j b) e")[:, :, 0:NE], l3,
                            rmax[:, 1].unsqueeze(2).to_broadcast([P, NT, NE]), ALU.mult).then_inc(aff_rdy, 1)
            dve.wait_ge(affT_sb, 1)
            for r in range(CAP // 8):
                src = work if r else affT
                V.max(top8[:], src)
                dve.drain()
                V.match_replace(work, top8[:], src, -1.0)
                dve.drain()
            V.tensor_tensor(gT, affT, work, ALU.not_equal)
            dve.drain()
            V.tensor_tensor(gT, gT, affT, ALU.mult).then_inc(gT_rdy, 1)
            dve.wait_ge(gN_rdy, 1)
            for b in range(B):
                dve.wait_ge(b2_ps, b + 1)
                V.tensor_tensor(h[:, b * S:(b + 1) * S], h[:, b * S:(b + 1) * S], bank[2 + b],
                                ALU.add).then_inc(y_add, 1)
            dve.drain()
            with dve.Fori(0, B) as b:
                for e in range(NE):
                    dve.wait_ge(y_ps, b * NE + e + 1)
                    for j in range(TPB):
                        last = V.scalar_tensor_tensor(h_tile(b * TPB + j), bank[2 + e % 2][:, j * D:(j + 1) * D],
                                                      gN[:, ds(b * EP + j * P + e, 1)], h_tile(b * TPB + j),
                                                      ALU.mult, ALU.add)
                    last.then_inc(y_add, 1)
                    dve.drain()
                V.engine_nop().then_inc(seq_done, 1)

        @block.tensor
        def _(pe):
            mm, tp = nc.tensor.matmul, nc.tensor.transpose

            def transpose_xn(ln, i, n=TPB):
                pe.wait_ge(ln.xn, i + 1)
                for j in range(n):
                    last = tp(bank[7][:, j * P:(j + 1) * P], xn[:, j, :], ident[:])
                last.then_inc(ln.ps, 1)

            def attention(a, b, logits, v_rhs, wo, bo):
                def pv(s):
                    j, hd = s // H, s % H
                    pe.wait_ge(a.ev[s % 2], b * (UNITS // 2) + s // 2 + 1)
                    if hd == 0 and j >= 2:
                        pe.wait_ge(a.norm, b * TPB + j - 1)
                    for c in range(TPB):
                        last = mm(bank[4 + j % 2][:, hd * a.dh:(hd + 1) * a.dh], eT_sb[:, s % 2, c * P:(c + 1) * P],
                                  v_rhs(c, hd), start=(c == 0), stop=(c == TPB - 1))
                    last.then_inc(a.pv, 1)

                def expT(s):
                    pe.wait_ge(a.ex, b * UNITS + s + 1)
                    if s >= 2:
                        pe.wait_ge(a.ev[s % 2], b * (UNITS // 2) + s // 2)
                    for c in range(TPB):
                        last = tp(bank[2 + s % 2][:, c * P:(c + 1) * P], e_sb[:, s % 3, c * P:(c + 1) * P], ident[:])
                    last.then_inc(a.tr, 1)

                def outT(j):
                    pe.wait_ge(a.norm, b * TPB + j + 1)
                    if j:
                        pe.wait_ge(a.ots, b * TPB + j)
                    for c in range(a.chunks):
                        last = tp(bank[6][:, c * P:(c + 1) * P], o_sb[:, c * P:(c + 1) * P], ident[:])
                    last.then_inc(a.otp, 1)

                def project(j):
                    pe.wait_ge(a.ots, b * TPB + j + 1)
                    if j:
                        pe.wait_ge(a.add, b * TPB + j)
                    for c in range(a.chunks):
                        mm(bank[7][:, 0:D], oT_sb[:, c * P:(c + 1) * P], wo(c), start=(c == 0), stop=False)
                    mm(bank[7][:, 0:D], ones[0:1, :], bo, start=False, stop=True).then_inc(a.proj, 1)

                for s in range(UNITS + 6):
                    if s < UNITS:
                        if s >= 2:
                            pe.wait_ge(a.ex, b * UNITS + s - 1)
                        logits(s)
                    if 0 <= s - 2 < UNITS:
                        expT(s - 2)
                    if 0 <= s - 3 < UNITS:
                        pv(s - 3)
                    if s >= 12 and (s - 4) % H == 0:
                        outT((s - 4) // H - 1)
                    if s >= 13 and (s - 5) % H == 0:
                        project((s - 5) // H - 1)

            pe.wait_ge(ld_tok, 80)
            pe.wait_ge(tanh_done, B + 1)
            for b in range(B):
                for j in range(TPB):
                    last = mm(bank[b][:, j * D:(j + 1) * D], tanhT[:, b * S + j * P:b * S + (j + 1) * P], w2b2[:],
                              start=True, stop=True)
                last.then_inc(emb_ps, 1)
            pe.wait_ge(consts, 1)
            pe.wait_ge(ld_a0, 64)

            def logits0(b):
                def f(s):
                    j, hd = s // H, s % H
                    r = slice((hd % HPG) * AUG, (hd % HPG + 1) * AUG)
                    mm(bank[s % 2][:, :], qT0[r, hd // HPG, j * P:(j + 1) * P], kT0[r, hd // HPG, :],
                       start=True, stop=True).then_inc(a0.qk, 1)
                return f

            with pe.Fori(0, B) as b:
                transpose_xn(lnB, b)
                pe.wait_ge(lnB.sb, b + 1)
                for j in range(TPB):
                    mm(bank[j][:, 0:3 * D], xnT[:, j * P:(j + 1) * P], wqkv0[:], start=True, stop=False)
                    mm(bank[j][:, 0:3 * D], ones[0:1, :], bqkv0[:], start=False, stop=True).then_inc(qkv_ps, 1)
                pe.wait_ge(qkv_sb, b * TPB + TPB)
                pe.wait_ge(aug, b + 1)
                for n in range(4):
                    src = (q_aug, k_aug)[n // 2]
                    for j in range(TPB):
                        last = tp(bank[n][:, j * P:(j + 1) * P],
                                  src[:, j, (n % 2) * HPG:(n % 2 + 1) * HPG, :].rearrange("p h a -> p (h a)"), ident[:])
                    last.then_inc(augT_ps, 1)
                pe.wait_ge(augT_sb, b * 4 + 4)
                attention(a0, b, logits0(b), lambda c, hd: qkv0[:, c, 2 * D + hd * DH0:2 * D + (hd + 1) * DH0],
                          lambda c: wo0[:], bo0[:])

            pe.wait_ge(bq_b, 1)
            pe.wait_ge(ld_pk, 48)
            for k, lhs in enumerate((wqT_s, bqb_s)):
                for q in range(2):
                    for n in range(H // 2):
                        hd = q * (H // 2) + n
                        last = mm(bank[2 * k + q][:, n * P:(n + 1) * P], lhs[:, hd, :], keys_s[:, hd, :],
                                  start=True, stop=True)
                    last.then_inc(kw_ps, 1)
            pe.wait_ge(kw_sb, 4)
            pe.wait_ge(ld_exp, 32)

            def scores(t):
                pe.wait_ge(lnC.sb, t + 1)
                if not (isinstance(t, int) and t == 0):
                    pe.wait_ge(relu_rdy, t * (NV // IG))
                for q in range(2):
                    mm(bank[q][:, :], xnT[:, 0:P], keyw[:, q * 512:(q + 1) * 512],
                       start=True, stop=True).then_inc(sc_ps, 1)

            def inner(t):
                for g in range(NV // IG):
                    if g < 2:
                        pe.wait_ge(sc_sb, t * 2 + g + 1)
                    else:
                        pe.wait_ge(relu_rdy, t * (NV // IG) + g - 1)
                    for q in range(IG):
                        last = mm(bank[g % 2][:, q * P:(q + 1) * P], wd[:, IG * g + q, :], xnT[:, 0:P],
                                  start=True, stop=True)
                    last.then_inc(in_ps, 1)

            def transpose_uvp(t):
                pe.wait_ge(lnC.sb, t + 1)
                pe.wait_ge(uvp_rdy, t + 1)
                for n in range(3):
                    last = tp(bank[7][:, (n + 1) * P:(n + 2) * P], uvp[:, n].rearrange("p q k -> p (q k)"), ident[:])
                last.then_inc(uvpT_ps, 1)

            def spread(t):
                pe.wait_ge(onehot, t + 1)
                for c in range(GP):
                    if c >= 2:
                        pe.wait_ge(vals_rdy, t * GP + c - 1)
                    for i in range(GT):
                        for q in range(2):
                            rows = slice(q * HALF, (q + 1) * HALF)
                            tok = c * GT + i
                            for s in range(3):
                                last = mm(quad[:, 2 * (c % 2) + q, i * NV:(i + 1) * NV], one_u[rows, :, tok],
                                          w_v[rows, s, :, tok], start=(s == 0), stop=(s == 2))
                    last.then_inc(g_ps, 1)

            def combine(t):
                pe.wait_ge(vals_rdy, (t + 1) * GP)
                for v in range(NV):
                    last = mm(bank[6][:, 0:D], vals[:, v, :], wu[:, v, :], start=(v == 0), stop=(v == NV - 1))
                last.then_inc(ffn_ps, 1)

            transpose_xn(lnC, 0, 1)
            scores(0)
            inner(0)
            with pe.Fori(0, NT - 1) as t:
                transpose_uvp(t)
                pe.wait_ge(uvpT_sb, t + 1)
                transpose_xn(lnC, t + 1, 1)
                scores(t + 1)
                spread(t)
                inner(t + 1)
                combine(t)
            transpose_uvp(NT - 1)
            spread(NT - 1)
            combine(NT - 1)

            pe.wait_ge(ld_a1, 80)

            def logits1(s):
                j, hd = s // H, s % H
                r = slice((hd % HP) * DH1, (hd % HP + 1) * DH1)
                mm(bank[s % 2][:, :], qT1[r, hd // HP, j * P:(j + 1) * P], kT1[r, hd // HP, :],
                   start=True, stop=True).then_inc(a1.qk, 1)

            with pe.Fori(0, B) as b:
                transpose_xn(lnD, b)
                pe.wait_ge(lnD.sb, b + 1)
                for n in range(3 * PAIRS):
                    kind, c = n // PAIRS, n % PAIRS
                    if n >= 4:
                        pe.wait_ge(p1_sb, b * 3 * PAIRS + n - 3)
                    if kind == 2:
                        last = mm(bank[n % 4][:, :], xnT[:, c * P:(c + 1) * P], wv1, start=True, stop=True)
                    else:
                        last = mm(bank[n % 4][:, :], (wq1, wk1)[kind][:, c * P:(c + 1) * P], xnT[:],
                                  start=True, stop=True)
                    last.then_inc(p1_ps, 1)
                pe.wait_ge(p1_sb, b * 3 * PAIRS + 3 * PAIRS)
                attention(a1, b, logits1, lambda c, hd: v1[:, c, hd * DH1:(hd + 1) * DH1],
                          lambda c: wo1[:, c, :], bo1[:])

            pe.wait_ge(ld_moe, 80)
            for b in range(B):
                if b:
                    pe.wait_ge(lnE.sb, b)
                transpose_xn(lnE, b)
                pe.wait_ge(lnE.sb, b + 1)
                for j in range(TPB):
                    last = mm(bank[0][:, (j * B + b) * NE:(j * B + b + 1) * NE], xnT[:, j * P:(j + 1) * P], gate_w[:],
                              start=True, stop=True)
                last.then_inc(lg_ps, 1)
            pe.wait_ge(aff_rdy, 1)
            for j in range(TPB):
                last = tp(bank[0][:, j * P:(j + 1) * P], aff[:, j].rearrange("p b e -> p (b e)"), ident[:])
            last.then_inc(affT_ps, 1)
            pe.wait_ge(gT_rdy, 1)
            for j in range(TPB):
                last = tp(bank[1][:, j * P:(j + 1) * P], gT[:, j * P:(j + 1) * P], ident[:])
            last.then_inc(gN_ps, 1)
            for b in range(B):
                for j in range(TPB):
                    last = mm(bank[2 + b][:, j * D:(j + 1) * D], gT[b * EP:(b + 1) * EP, j * P:(j + 1) * P],
                              b2e[b * EP:(b + 1) * EP, :], start=True, stop=True)
                last.then_inc(b2_ps, 1)
            pe.wait_ge(gN_rdy, 1)

            with pe.Fori(0, B) as b:
                def up(e):
                    if e >= 2:
                        pe.wait_ge(hid_sb, b * NE + e - 1)
                    mm(bank[e % 2][:, :], w1e[:, e, :], xnT_all[:, ds(b * S, S)], start=True, stop=True).then_inc(hid_ps, 1)

                def down(e):
                    pe.wait_ge(hid_sb, b * NE + e + 1)
                    pe.wait_ge(y_add, B + b * NE + e - 1)
                    for j in range(TPB):
                        last = mm(bank[2 + e % 2][:, j * D:(j + 1) * D], hidT[:, e % 2, j * P:(j + 1) * P], w2e[:, e, :],
                                  start=True, stop=True)
                    last.then_inc(y_ps, 1)

                up(0)
                for e in range(NE):
                    if e + 1 < NE:
                        up(e + 1)
                    down(e)


_OUT = ((4, 512, 128), "float32")


def kernel(**inputs):
    import numpy as np
    import concourse.bacc as bacc
    from concourse.bass_utils import run_bass_kernel_spmd

    g = {k: np.asarray(v) for k, v in inputs.items()}
    P, H, NK = 128, 8, 64
    c = np.ascontiguousarray
    keys = g["L0_ffn_keys"]
    kbd = np.zeros((P, H, P), keys.dtype)
    for q in range(2):
        kbd[q * 64:(q + 1) * 64, :, q * 64:(q + 1) * 64] = keys[:, q].transpose(2, 0, 1)
    b2 = np.zeros((4, 32, 128), g["L1_ffn_b2"].dtype)
    b2[:, 0:16] = g["L1_ffn_b2"]
    arrays = {
        "x_idx": c(g["x"].reshape(16, P).T),
        "val_idx": c(g["itok_BS_0_4999"].reshape(16, P).T),
        "num_rows": c(g["fside_BS_numeric_value"].reshape(2048)),
        "mask_idx": c(g["mask_BS_i1_0"].reshape(16, P).T),
        "event_table": g["L0_tok_event_table"],
        "value_table": g["L0_tok_value_table"],
        "tok_w1": c(g["L0_tok_w1"].reshape(64, 1)),
        "tok_b1": c(g["L0_tok_b1"].reshape(64, 1)),
        "tok_w2b2": np.concatenate([g["L0_tok_w2"], g["L0_tok_b2"][None]], 0),
        "a0_wqkv": np.concatenate([g["L0_attn_Wq"], g["L0_attn_Wk"], g["L0_attn_Wv"]], 1),
        "a0_bqkv": np.concatenate([g["L0_attn_bq"], g["L0_attn_bk"], g["L0_attn_bv"]])[None],
        "a0_wo": g["L0_attn_Wo"],
        "a0_bo": g["L0_attn_bo"][None],
        "pk_wqT": c(g["L0_ffn_Wq"].reshape(P, H, P).transpose(2, 1, 0).reshape(P, H * P)),
        "pk_bq": c(g["L0_ffn_bq"].reshape(H, P).T),
        "pk_keys": kbd.reshape(P, H * P),
        "pk_down": c(g["L0_ffn_w_down"].reshape(128, 32, 128).transpose(2, 1, 0).reshape(P, 4096)),
        "pk_up": g["L0_ffn_w_up"].reshape(128, 4096),
        "a1_wq": g["L1_attn_w_q"],
        "a1_wk": g["L1_attn_w_k"],
        "a1_wv": g["L1_attn_w_v"],
        "a1_wo": c(g["L1_attn_w_out"].reshape(4, P, 128).transpose(1, 0, 2).reshape(P, 512)),
        "a1_bo": g["L1_attn_b_out"][None],
        "moe_gate": g["L1_ffn_gate_weight"],
        "moe_w1": c(g["L1_ffn_w1"].transpose(1, 0, 2).reshape(P, 2048)),
        "moe_b1": c(g["L1_ffn_b1"].T),
        "moe_w2": c(g["L1_ffn_w2"].transpose(1, 0, 2).reshape(P, 2048)),
        "moe_b2": b2.reshape(P, 128),
    }
    nc = bacc.Bacc("TRN2", target_bir_lowering=False, num_devices=1)
    aps = {k: nc.dram_tensor("in_" + k, a.shape, mybir.dt.from_np(a.dtype), kind="ExternalInput").ap()
           for k, a in arrays.items()}
    out = nc.dram_tensor("out_0", _OUT[0], mybir.dt.float32, kind="ExternalOutput").ap()
    tower(nc, *aps.values(), out)
    r = run_bass_kernel_spmd(nc, [{"in_" + k: a for k, a in arrays.items()}], core_ids=[0])
    return r.results[0]["out_0"]
```

```python
import concourse.bass as bass
from concourse import mybir
from contextlib import ExitStack



def tower(nc, x_idx, val_idx, num_rows, mask_idx, event_table, value_table, tok_w1, tok_b1, tok_w2b2,
          a0_wqkv, a0_bqkv, a0_wo, a0_bo, pk_wqT, pk_bq, pk_keys, pk_down, pk_up,
          a1_wq, a1_wk, a1_wv, a1_wo, a1_bo, moe_gate, moe_w1, moe_b1, moe_w2, moe_b2, out):
    F32, BF16, F32R = mybir.dt.float32, mybir.dt.bfloat16, mybir.dt.float32r
    I32, U32 = mybir.dt.int32, mybir.dt.uint32
    ALU, ACT, AX = mybir.AluOpType, mybir.ActivationFunctionType, mybir.AxisListType
    ds = bass.ds

    P = 128
    B, S, D = 4, 512, 128
    TPB = S // P
    NT = B * TPB
    EPS = 1e-5
    HD = tok_w1.shape[0]
    H = 8
    UNITS = H * TPB
    DH0 = D // H
    AUG = 32
    HPG = P // AUG
    DH1 = 64
    NK, TOP = 64, 8
    HK = H * TOP
    NU, NV = 128, 32
    HALF = P // 2
    GT = 16
    GP = HALF // GT
    IG = 4
    NE, CAP = 16, S // 16 * 2
    EP = 32

    with ExitStack() as ctx:
        def sb(name, shape, dt=F32):
            return ctx.enter_context(nc.sbuf_tensor(name, shape, dt))

        def sem(name):
            return ctx.enter_context(nc.semaphore(name))

        bank = [ctx.enter_context(nc.psum_tensor(f"bank{i}", [P, 512], F32))[:, :] for i in range(2)]
        quad = ctx.enter_context(nc.psum_tensor("quad", [P, 4, 512], F32))
        bank += [quad[:, i, :] for i in range(4)]
        bank += [ctx.enter_context(nc.psum_tensor(f"bank{i}", [P, 512], F32))[:, :] for i in (6, 7)]

        h = sb("h", [P, NT * D])
        ident = sb("ident", [P, P])
        ones = sb("ones", [P, P])
        mhalf = sb("mhalf", [P, TPB * H])
        phalf = sb("phalf", [P, TPB * H])

        def h_tile(t):
            return h[:, ds(t * D, D)]

        stats = sb("stats", [P, TPB, 6])
        mv = sb("mv", [P, TPB, 2])
        veps = sb("veps", [P, TPB])
        rstd = sb("rstd", [P, TPB])
        xn = sb("xn", [P, TPB, D])
        xnT = sb("xnT", [P, S])

        w2b2 = sb("w2b2", [HD + 1, D])
        bo0 = sb("bo0", [1, D])
        bo1 = sb("bo1", [1, D])
        gate_w = sb("gate_w", [P, NE])
        b1e = sb("b1e", [P, NE])
        bq_s = sb("bq_s", [P, H])
        wd_t = sb("wd", [P, NV * P])
        wu_t = sb("wu", [P, NV * D])
        wd = wd_t[:].rearrange("p (v u) -> p v u", v=NV)
        wu = wu_t[:].rearrange("p (v d) -> p v d", v=NV)

        class Scope:
            def __init__(self):
                self.stack = ExitStack()

            def sb(self, name, shape, dt=F32):
                return self.stack.enter_context(nc.sbuf_tensor(name, shape, dt))

            def close(self):
                self.stack.close()

        class AttentionMemory:
            def __init__(self, n, sc, k_parts):
                self.qT = sc.sb(n + "_qT", [P, H, S], F32R)
                self.kT = sc.sb(n + "_kT", [P, k_parts, H, S], F32R)
                self.v = sc.sb(n + "_v", [P, TPB, H, P], F32R)
                self.eT = sc.sb(n + "_eT", [P, 2, 2, TPB, S], F32R)
                self.e = sc.sb(n + "_e", [P, 3, S])
                self.en = sc.sb(n + "_en", [P, 3, S])
                self.negmax = sc.sb(n + "_negmax", [P, 4])
                self.rowsum = sc.sb(n + "_rowsum", [P, 4])
                self.rrec = sc.sb(n + "_rrec", [P, 4])

        sA = Scope()
        ev_rows = sA.sb("ev_rows", [P, NT * D])
        vv_rows = sA.sb("vv_rows", [P, NT * D])
        num_b = sA.sb("num_b", [HD, B * S])
        tanhT = sA.sb("tanhT", [HD + 1, B * S])
        idx_e = sA.sb("idx_e", [P, NT], I32)
        idx_v = sA.sb("idx_v", [P, NT], I32)
        mask_i = sA.sb("mask_i", [P, NT], I32)
        mask_f = sA.sb("mask_f", [P, NT])
        w1c = sA.sb("w1c", [HD, 1])
        b1c = sA.sb("b1c", [HD, 1])
        sA.close()

        sB = Scope()
        mB = AttentionMemory("a0", sB, 1)
        oT0 = sB.sb("oT0", [P, H // HPG, S])
        wo0 = sB.sb("wo0", [P, H // HPG, D])
        wqkv0 = sB.sb("wqkv0", [P, 3 * D])
        bqkv0 = sB.sb("bqkv0", [1, 3 * D])
        qkv0 = sB.sb("qkv0", [P, TPB, 3 * D])
        q_aug = sB.sb("q_aug", [P, TPB * H, AUG])
        k_aug = sB.sb("k_aug", [P, TPB * H, AUG])
        q_st = sB.sb("q_st", [P, TPB * H, 4, AUG])
        k_st = sB.sb("k_st", [P, TPB * H, 2, 2, AUG])
        st0 = sB.sb("st0", [P, 12, TPB, H])
        dev = q_st[:, :, 0, 0:DH0].rearrange("p (j h) d -> p j h d", j=TPB)
        sqr = q_st[:, :, 1, 0:DH0].rearrange("p (j h) d -> p j h d", j=TPB)
        qa = q_aug[:].rearrange("p (j h) a -> p j h a", j=TPB)
        ka = k_aug[:].rearrange("p (j h) a -> p j h a", j=TPB)
        sB.close()

        sC = Scope()
        relu_in = sC.sb("relu_in", [P, NV, P])
        vals_t = sC.sb("vals", [P, NV * P])
        vals = vals_t[:].rearrange("p (v t) -> p v t", v=NV)
        one_u_t = sC.sb("one_u", [P, NU, HALF], BF16)
        iota_u_t = sC.sb("iota_u", [P, NU, HALF], BF16)
        one_u, iota_u = one_u_t[:], iota_u_t[:]
        one_v = sC.sb("one_v", [P, NV, HALF], BF16)
        w_v = sC.sb("w_v", [P, 3, NV, HALF], BF16)
        iota8 = sC.sb("iota8", [P, 1, TOP])
        wqT_s = vals_t[:, 0:1024].rearrange("p (h d) -> p h d", h=H)
        keys_s = vals_t[:, 1024:2048].rearrange("p (h n) -> p h n", h=H)
        bqb_s = vals_t[:, 2048:3072].rearrange("p (h t) -> p h t", h=H)
        keyw = sC.sb("keyw", [P, H * P])
        keyb = sC.sb("keyb", [P, H * P])
        sc = sC.sb("sc", [P, H, 2, NK])
        m8 = sC.sb("m8", [P, H, 2, TOP])
        i8 = sC.sb("i8", [P, H, 2, TOP], U32)
        i8f = sC.sb("i8f", [P, H, TOP])
        pair_s = sC.sb("pair_s", [P, H, TOP, TOP])
        b8 = sC.sb("b8", [P, H, TOP])
        bi = sC.sb("bi", [P, H, TOP], U32)
        bab = sC.sb("bab", [P, 2, HK], U32)
        ext = sC.sb("ext", [P, 2, HK, TOP])
        ij = sC.sb("ij", [P, 2, HK])
        jhi = sC.sb("jhi", [P, HK])
        uvp = sC.sb("uvp", [P, 3, 2, HK])
        pe_ = sC.sb("pe_", [P, H, TOP])
        pz = sC.sb("pz", [P, 2, H])
        uT = sC.sb("uT", [P, HALF], BF16)
        vT = sC.sb("vT", [P, HALF], BF16)
        pT = sC.sb("pT", [P, HALF])
        pres = sC.sb("pres", [P, 2, HALF])
        psp = sC.sb("psp", [P, 3, HALF], BF16)
        sC.close()

        sD = Scope()
        mD = AttentionMemory("a1", sD, 2)
        oT1 = sD.sb("oT1", [P, H, S])
        wo1 = sD.sb("wo1", [P, H, D])
        wq1 = wd_t[:, 0:1024]
        wk1 = wd_t[:, 1024:2048]
        wv1 = wd_t[:, 2048:2560]
        sD.close()

        sE = Scope()
        w1_t = sE.sb("w1e", [P, NE * P])
        w2_t = sE.sb("w2e", [P, NE * D])
        w1e = w1_t[:].rearrange("p (e f) -> p e f", e=NE)
        w2e = w2_t[:].rearrange("p (e f) -> p e f", e=NE)
        b2e = sE.sb("b2e", [P, D])
        xnT_all = sE.sb("xnT_all", [P, B * S])
        logit_t = sE.sb("logit", [P, TPB, B, NE])
        aff_t = sE.sb("aff", [P, TPB, B, EP])
        logit, aff = logit_t[:], aff_t[:]
        rmax = sE.sb("rmax", [P, 2, NT])
        affT = sE.sb("affT", [P, S])[:]
        work = sE.sb("work", [P, S])[:]
        gT = sE.sb("gT", [P, S])[:]
        gN = sE.sb("gN", [P, S])[:]
        top8 = sE.sb("top8", [P, 8])
        hidT = sE.sb("hidT", [P, 2, S])
        sE.close()

        consts, v_zero = sem("consts_ready"), sem("v0_cleared")
        ld_idx, ld_tok, ld_a0, ld_pk, ld_exp = sem("ld_idx"), sem("ld_tok"), sem("ld_a0"), sem("ld_pk"), sem("ld_exp")
        ld_a1, ld_moe, gath = sem("ld_a1"), sem("ld_moe"), sem("rows_gathered")
        tanh_done, emb_ps, h_ready = sem("tanh_done"), sem("emb_ps"), sem("h_ready")
        out_dma = sem("out_dma")

        class LN:
            def __init__(self, n):
                self.var = sem(n + "_var_ready")
                self.rstd = sem(n + "_rstd_ready")
                self.xn = sem(n + "_xn_ready")
                self.ps = sem(n + "_xnT_in_psum")
                self.sb = sem(n + "_xnT_in_sbuf")

        lnB, lnC, lnD, lnE = LN("lnB"), LN("lnC"), LN("lnD"), LN("lnE")

        class ATT:
            def __init__(self, n, mem, oT, group, scale):
                self.mem, self.oT, self.group, self.scale = mem, oT, group, scale
                self.groups = H // group
                self.qk = sem(n + "_logits_in_psum")
                self.mx = sem(n + "_max_ready")
                self.ex = sem(n + "_exp_done")
                self.rc = sem(n + "_sum_inverted")
                self.nr = sem(n + "_exp_normalised")
                self.tr = sem(n + "_expT_in_psum")
                self.hi = sem(n + "_expT_hi")
                self.lo = sem(n + "_expT_lo")
                self.pv = sem(n + "_pv_done")
                self.ots = sem(n + "_outT_in_sbuf")
                self.proj = sem(n + "_projected")
                self.add = sem(n + "_h_added")

        a0, a1 = ATT("a0", mB, oT0, HPG, 1.0), ATT("a1", mD, oT1, 1, DH1 ** -0.5)
        qkv_ps, qkv_sb = sem("qkv_in_psum"), sem("qkv_in_sbuf")
        sig2, sigma, nf, enf, aug = sem("q_var"), sem("q_sigma"), sem("q_nf"), sem("q_exp_nf"), sem("aug_ready")
        st_hi, st_lo, v0_hi, v0_lo = sem("stack_hi"), sem("stack_lo"), sem("v0_hi"), sem("v0_lo")
        augT_ps, augT_act, augT_dve = sem("augT_in_psum"), sem("augT_by_act"), sem("augT_by_dve")
        p1_ps, p1_hi, p1_lo = sem("proj1_in_psum"), sem("proj1_hi"), sem("proj1_lo")

        bq_b, kw_ps, kw_sb = sem("bq_spread"), sem("keyw_in_psum"), sem("keyw_in_sbuf")
        sc_ps, sc_raw, sc_sb, best, pexp, uvp_rdy = sem("scores_in_psum"), sem("scores_copied"), sem("scores_ready"), sem("best_ready"), sem("pexp"), sem("uvp_ready")
        uvpT_ps, uvpT_sb, onehot = sem("uvpT_in_psum"), sem("uvpT_in_sbuf"), sem("onehot_ready")
        i8f_rdy = sem("second_index_as_float")
        place_rdy, ext_rdy, psp_rdy, third_w = sem("second_place_one_hot"), sem("second_index_picked"), sem("weight_parts_ready"), sem("third_weight_part")
        g_ps, vals_rdy, in_ps, relu_rdy = sem("g_in_psum"), sem("vals_ready"), sem("inner_in_psum"), sem("relu_ready")
        ffn_ps, ffn_add = sem("ffn_in_psum"), sem("ffn_added")

        lg_ps, lg_sb, lg_exp_in, lg_exp, aff_rdy = sem("gate_in_psum"), sem("gate_max"), sem("gate_exp_in"), sem("gate_exp"), sem("aff_ready")
        affT_ps, affT_sb, gT_rdy, gN_ps, gN_rdy = sem("affT_in_psum"), sem("affT_in_sbuf"), sem("gT_ready"), sem("gN_in_psum"), sem("gN_ready")
        hid_ps, hid_sb, y_ps, y_add, b2_ps = sem("hid_in_psum"), sem("hid_ready"), sem("y_in_psum"), sem("y_added"), sem("b2_in_psum")
        seq_done = sem("sequence_done")

        block = ctx.enter_context(nc.Block())

        @block.sync
        def _(sp):
            sp.dma_start(idx_e[:], x_idx).then_inc(ld_idx, 16)
            sp.dma_start(idx_v[:], val_idx).then_inc(ld_idx, 16)
            sp.dma_start(mask_i[:], mask_idx).then_inc(ld_tok, 16)
            sp.dma_start(num_b[:], num_rows.partition_broadcast(HD)).then_inc(ld_tok, 16)
            sp.dma_start(w1c[:], tok_w1).then_inc(ld_tok, 16)
            sp.dma_start(b1c[:], tok_b1).then_inc(ld_tok, 16)
            sp.dma_start(w2b2[:], tok_w2b2).then_inc(ld_tok, 16)
            sp.dma_start(bo0[:], a0_bo).then_inc(ld_a0, 16)
            sp.dma_start(bo1[:], a1_bo).then_inc(ld_a1, 16)
            sp.dma_start(gate_w[:], moe_gate).then_inc(ld_moe, 16)
            sp.dma_start(b1e[:], moe_b1).then_inc(ld_moe, 16)
            sp.dma_start(bq_s[:], pk_bq).then_inc(ld_pk, 16)
            sp.wait_ge(h_ready, 1)
            sp.dma_start(wqkv0[:], a0_wqkv).then_inc(ld_a0, 16)
            sp.dma_start(bqkv0[:], a0_bqkv).then_inc(ld_a0, 16)
            sp.dma_start(wo0[:], a0_wo.rearrange("p (g d) -> p g d", g=H // HPG)).then_inc(ld_a0, 16)
            sp.dma_start(wd_t[:], pk_down).then_inc(ld_exp, 16)
            sp.dma_start(wu_t[:], pk_up).then_inc(ld_exp, 16)
            sp.wait_ge(a0.add, B)
            sp.dma_start(vals_t[:, 0:1024], pk_wqT).then_inc(ld_pk, 16)
            sp.dma_start(vals_t[:, 1024:2048], pk_keys).then_inc(ld_pk, 16)
            sp.wait_ge(ffn_add, NT)
            sp.dma_start(wq1, a1_wq).then_inc(ld_a1, 16)
            sp.dma_start(wk1, a1_wk).then_inc(ld_a1, 16)
            sp.dma_start(wv1, a1_wv).then_inc(ld_a1, 16)
            sp.dma_start(wo1[:], a1_wo.rearrange("p (h d) -> p h d", h=H)).then_inc(ld_a1, 16)
            sp.wait_ge(a1.add, B)
            sp.dma_start(b2e[:], moe_b2).then_inc(ld_moe, 16)
            sp.dma_start(w1_t[:], moe_w1).then_inc(ld_moe, 16)
            sp.dma_start(w2_t[:], moe_w2).then_inc(ld_moe, 16)
            for b in range(B):
                sp.wait_ge(seq_done, b + 1)
                sp.dma_start(out[b].rearrange("(j p) d -> p j d", p=P),
                             h[:, b * S:(b + 1) * S].rearrange("p (j d) -> p j d", j=TPB)).then_inc(out_dma, 16)
            sp.wait_ge(out_dma, 16 * B)

        @block.gpsimd
        def _(pool):
            pool.wait_ge(ld_idx, 32)
            for t in range(NT):
                for rows, idx, table in ((ev_rows, idx_e, event_table), (vv_rows, idx_v, value_table)):
                    nc.gpsimd.indirect_dma_start(
                        out=rows[:, t * D:(t + 1) * D], out_offset=None, in_=table,
                        in_offset=bass.IndirectOffsetOnAxis(ap=idx[:, t:t + 1].bitcast(U32), axis=0)).then_inc(gath, 16)
            nc.gpsimd.memset(ident[:], 0.0)
            nc.gpsimd.memset(ones[:], 1.0)
            nc.gpsimd.memset(mhalf[:], -0.5)
            nc.gpsimd.memset(phalf[:], 0.5)
            pool.drain()
            nc.gpsimd.affine_select(out=ident[:], in_=ident[:], compare_op=ALU.not_equal, fill=1.0, base=0,
                                    pattern=[[-1, P]], channel_multiplier=1).then_inc(consts, 1)

            def rstd_step(ln, i, n):
                pool.wait_ge(ln.var, i + 1)
                nc.gpsimd.tensor_tensor(rstd[:, 0:n], veps[:, 0:n], mhalf[:, 0:n], ALU.pow).then_inc(ln.rstd, 1)

            def normalise(a, b):
                m = a.mem
                for s in range(UNITS):
                    pool.wait_ge(a.rc, b * UNITS + s + 1)
                    if s >= 3:
                        pool.wait_ge(a.tr, b * UNITS + s - 2)
                    nc.gpsimd.tensor_tensor(m.en[:, s % 3, :], m.e[:, s % 3, :],
                                            m.rrec[:, s % 4:s % 4 + 1].to_broadcast([P, S]),
                                            ALU.mult).then_inc(a.nr, 1)

            with pool.Fori(0, B) as b:
                rstd_step(lnB, b, TPB)
                pool.wait_ge(sig2, b + 1)
                nc.gpsimd.tensor_tensor(st0[:, 2], st0[:, 1], phalf[:].rearrange("p (j h) -> p j h", j=TPB),
                                        ALU.pow).then_inc(sigma, 1)
                normalise(a0, b)
            pool.wait_ge(a0.add, B)
            nc.gpsimd.iota(iota_u, [[1, NU], [0, HALF]], base=0, channel_multiplier=0,
                           allow_small_or_imprecise_dtypes=True).then_inc(consts, 1)
            nc.gpsimd.iota(iota8[:], [[0, 1], [1, TOP]], base=0, channel_multiplier=0,
                           allow_small_or_imprecise_dtypes=True).then_inc(consts, 1)

            def scores_bias(t):
                for q in range(2):
                    pool.wait_ge(sc_raw, t * 2 + q + 1)
                    part = sc[:, 4 * q:4 * q + 4].rearrange("p h a n -> p (h a n)")
                    nc.gpsimd.tensor_tensor(part, part, keyb[:, q * 512:(q + 1) * 512], ALU.add).then_inc(sc_sb, 1)

            def pick_second(t):
                pool.wait_ge(i8f_rdy, t + 1)
                pool.wait_ge(place_rdy, t + 1)
                nc.gpsimd.tensor_tensor(ext[:, 1].rearrange("p (h k) a -> p h k a", h=H),
                                        ext[:, 1].rearrange("p (h k) a -> p h k a", h=H),
                                        i8f[:].unsqueeze(2).to_broadcast([P, H, TOP, TOP]),
                                        ALU.mult).then_inc(ext_rdy, 1)

            def third_part(t):
                pool.wait_ge(psp_rdy, t + 1)
                nc.gpsimd.tensor_tensor(w_v[:, 2], one_v[:], psp[:, 2].unsqueeze(1).to_broadcast([P, NV, HALF]),
                                        ALU.mult).then_inc(third_w, 1)

            rstd_step(lnC, 0, 1)
            scores_bias(0)
            rstd_step(lnC, 1, 1)
            pick_second(0)
            third_part(0)
            scores_bias(1)
            with pool.Fori(0, NT - 2) as t:
                rstd_step(lnC, t + 2, 1)
                pick_second(t + 1)
                third_part(t + 1)
                scores_bias(t + 2)
            pick_second(NT - 1)
            third_part(NT - 1)
            with pool.Fori(0, B) as b:
                rstd_step(lnD, b, TPB)
                normalise(a1, b)
            with pool.Fori(0, B) as b:
                rstd_step(lnE, b, TPB)

        @block.scalar
        def _(act):
            def copy_xnT(ln, i, n=S, src=None, dst=None):
                act.wait_ge(ln.ps, i + 1)
                nc.scalar.copy(xnT[:, 0:n] if dst is None else dst,
                               bank[7][:, 0:n]).then_inc(ln.sb, 1)

            def attention(a, b):
                m = a.mem

                def exp(s):
                    act.wait_ge(a.mx, b * UNITS + s + 1)
                    if s >= 3:
                        act.wait_ge(a.nr, b * UNITS + s - 2)
                    nc.scalar.activation(m.e[:, s % 3, :], bank[s % 2][:, :], ACT.Exp,
                                         bias=m.negmax[:, s % 4:s % 4 + 1],
                                         accum_out=m.rowsum[:, s % 4:s % 4 + 1]).then_inc(a.ex, 1)

                def expT_hi(s):
                    hd, j = s // TPB, s % TPB
                    act.wait_ge(a.tr, b * UNITS + s + 1)
                    if j == 0 and hd >= 2:
                        act.wait_ge(a.pv, b * UNITS + TPB * (hd - 1))
                    nc.scalar.copy(m.eT[:, hd % 2, 0, :, j * P:(j + 1) * P],
                                   bank[2 + s % 2].rearrange("p (c n) -> p c n", c=TPB)).then_inc(a.hi, 1)

                def outT(g):
                    act.wait_ge(a.pv, b * UNITS + TPB * a.group * (g + 1))
                    nc.scalar.copy(a.oT[:, g, :], bank[4 + g % 2]).then_inc(a.ots, 1)

                for s in range(UNITS + 9):
                    if s < UNITS:
                        exp(s)
                    if 0 <= s - 3 < UNITS:
                        expT_hi(s - 3)
                    done = s - 8
                    if done > 0 and done % (TPB * a.group) == 0:
                        outT(done // (TPB * a.group) - 1)

            act.wait_ge(ld_tok, 80)
            for b in range(B):
                nc.scalar.activation(tanhT[0:HD, b * S:(b + 1) * S], num_b[:, b * S:(b + 1) * S], ACT.Tanh,
                                     bias=b1c[:, 0:1], scale=w1c[:, 0:1]).then_inc(tanh_done, 1)
            with act.Fori(0, B) as b:
                copy_xnT(lnB, b)
                for j in range(TPB):
                    act.wait_ge(qkv_ps, b * TPB + j + 1)
                    nc.scalar.copy(qkv0[:, j, :], bank[j][:, 0:3 * D]).then_inc(qkv_sb, 1)
                act.wait_ge(nf, b + 1)
                nc.scalar.activation(st0[:, 6], st0[:, 5], ACT.Exp, scale=-1.0).then_inc(enf, 1)
                act.wait_ge(v_zero, 1)
                for a in range(HPG):
                    last = nc.scalar.copy(mB.v[:, :, a:H:HPG, a * AUG:a * AUG + DH0],
                                          qkv0[:, :, 2 * D:].rearrange("p j (g a d) -> p j g a d", a=HPG, d=DH0)[:, :, :, a, :])
                last.then_inc(v0_hi, 1)
                act.wait_ge(aug, b + 1)
                nc.scalar.copy(q_st[:, :, 0:2, :].bitcast(F32R), q_aug[:].unsqueeze(2).to_broadcast([P, TPB * H, 2, AUG])).then_inc(st_hi, 1)
                nc.scalar.copy(k_st[:, :, :, 0, :].bitcast(F32R), k_aug[:].unsqueeze(2).to_broadcast([P, TPB * H, 2, AUG])).then_inc(st_hi, 1)
                for n in range(0, 2 * H, 2):
                    act.wait_ge(augT_ps, b * 2 * H + n + 1)
                    dst = mB.qT[:, n, :] if n < H else mB.kT[:, 0, n - H, :]
                    nc.scalar.copy(dst, bank[n % 4][:, :]).then_inc(augT_act, 1)
                attention(a0, b)

            for n, (dst, src) in enumerate(((keyw, 0), (keyw, 1), (keyb, 2), (keyb, 3))):
                act.wait_ge(kw_ps, n + 1)
                nc.scalar.copy(dst[:, (src % 2) * 512:(src % 2) * 512 + 512], bank[src][:, :]).then_inc(kw_sb, 1)

            def relu_inner(t):
                if not (isinstance(t, int) and t == 0):
                    act.wait_ge(vals_rdy, t * GP)
                for g in range(NV // IG):
                    act.wait_ge(in_ps, t * (NV // IG) + g + 1)
                    nc.scalar.activation(relu_in[:, IG * g:IG * g + IG, :],
                                         bank[g % 2][:, :].rearrange("p (v t) -> p v t", v=IG),
                                         ACT.Relu).then_inc(relu_rdy, 1)

            def softmax_exp(t):
                act.wait_ge(best, t + 1)
                nc.scalar.activation(pe_[:], pe_[:], ACT.Exp).then_inc(pexp, 1)

            def copy_xnT_tile(t):
                if not (isinstance(t, int) and t == 0):
                    act.wait_ge(in_ps, t * (NV // IG))
                copy_xnT(lnC, t, P)

            def copy_uvpT(t):
                act.wait_ge(uvpT_ps, t + 1)
                for dst, c in ((uT, 1), (vT, 2), (pT, 3)):
                    for q in range(2):
                        last = nc.scalar.copy(dst[q * HALF:(q + 1) * HALF, :],
                                              bank[7][q * HALF:(q + 1) * HALF,
                                                      c * P + q * HALF:c * P + (q + 1) * HALF])
                last.then_inc(uvpT_sb, 1)

            def copy_scores(t):
                if not (isinstance(t, int) and t == 0):
                    act.wait_ge(best, t)
                for q in range(2):
                    act.wait_ge(sc_ps, t * 2 + q + 1)
                    nc.scalar.copy(sc[:, 4 * q:4 * q + 4].rearrange("p h a n -> p (h a n)"),
                                   bank[q][:, :]).then_inc(sc_raw, 1)

            def second_index(t):
                act.wait_ge(best, t + 1)
                if not (isinstance(t, int) and t == 0):
                    act.wait_ge(ext_rdy, t)
                nc.scalar.copy(i8f[:], i8[:, :, 1, :]).then_inc(i8f_rdy, 1)

            copy_xnT_tile(0)
            copy_scores(0)
            relu_inner(0)
            softmax_exp(0)
            second_index(0)
            copy_uvpT(0)
            copy_xnT_tile(1)
            copy_scores(1)
            with act.Fori(0, NT - 2) as t:
                softmax_exp(t + 1)
                second_index(t + 1)
                copy_uvpT(t + 1)
                relu_inner(t + 1)
                copy_xnT_tile(t + 2)
                copy_scores(t + 2)
            softmax_exp(NT - 1)
            second_index(NT - 1)
            copy_uvpT(NT - 1)
            relu_inner(NT - 1)

            with act.Fori(0, B) as b:
                copy_xnT(lnD, b)
                for n in range(2 * H + TPB):
                    act.wait_ge(p1_ps, b * (2 * H + TPB) + n + 1)
                    src = bank[n % 4][:, :]
                    if n < H:
                        nc.scalar.mul(mD.qT[:, n, :], src, a1.scale).then_inc(p1_hi, 1)
                    elif n < 2 * H:
                        nc.scalar.copy(mD.kT[:, 0, n - H, :], src).then_inc(p1_hi, 1)
                    else:
                        nc.scalar.copy(mD.v[:, n - 2 * H, :, 0:DH1],
                                       src.rearrange("p (h d) -> p h d", h=H)).then_inc(p1_hi, 1)
                attention(a1, b)

            for b in range(B):
                act.wait_ge(lnE.ps, b + 1)
                nc.scalar.copy(xnT[:], bank[7][:, :])
                nc.scalar.copy(xnT_all[:, b * S:(b + 1) * S], bank[7][:, :]).then_inc(lnE.sb, 1)
            act.wait_ge(lg_exp_in, 1)
            nc.scalar.activation(logit, logit, ACT.Exp).then_inc(lg_exp, 1)
            act.wait_ge(affT_ps, 1)
            nc.scalar.copy(affT, bank[0][:, :]).then_inc(affT_sb, 1)
            act.wait_ge(gN_ps, 1)
            nc.scalar.copy(gN, bank[1][:, :]).then_inc(gN_rdy, 1)
            with act.Fori(0, B) as b:
                for e in range(NE):
                    act.wait_ge(hid_ps, b * NE + e + 1)
                    if e >= 2:
                        act.wait_ge(y_ps, b * NE + e - 1)
                    nc.scalar.activation(hidT[:, e % 2, :], bank[e % 2][:, :], ACT.Gelu_apprx_tanh,
                                         bias=b1e[:, e:e + 1]).then_inc(hid_sb, 1)

        @block.vector
        def _(dve):
            V = nc.vector

            def ln_stats(ln, first, n):
                for j in range(n):
                    V.bn_stats(stats[:, j, :], h_tile(first + j))
                dve.drain()
                for j in range(n):
                    V.bn_aggr(mv[:, j, :], stats[:, j, :])
                dve.drain()
                V.tensor_scalar(veps[:, 0:n], mv[:, 0:n, 1], EPS, None, ALU.add).then_inc(ln.var, 1)

            def ln_scale(ln, i, first, n):
                if ln is lnE and i:
                    dve.wait_ge(ln.ps, i)
                dve.wait_ge(ln.rstd, i + 1)
                for j in range(n):
                    last = V.tensor_scalar(xn[:, j, :], h_tile(first + j), mv[:, j, 0:1], rstd[:, j:j + 1],
                                           ALU.subtract, ALU.mult)
                last.then_inc(ln.xn, 1)

            def layer_norm(ln, i, first, n):
                ln_stats(ln, first, n)
                ln_scale(ln, i, first, n)

            def attention(a, b):
                m = a.mem

                def rowmax(s):
                    dve.wait_ge(a.qk, b * UNITS + s + 1)
                    V.tensor_reduce(m.negmax[:, s % 4:s % 4 + 1], bank[s % 2][:, :], AX.X, ALU.max,
                                    negate=True).then_inc(a.mx, 1)

                def invert(s):
                    dve.wait_ge(a.ex, b * UNITS + s + 1)
                    if s >= 4:
                        dve.wait_ge(a.nr, b * UNITS + s - 3)
                    V.reciprocal(m.rrec[:, s % 4:s % 4 + 1], m.rowsum[:, s % 4:s % 4 + 1]).then_inc(a.rc, 1)

                def expT_lo(s):
                    hd, j = s // TPB, s % TPB
                    dve.wait_ge(a.hi, b * UNITS + s + 1)
                    part = m.eT[:, hd % 2, :, :, j * P:(j + 1) * P]
                    V.tensor_tensor(part[:, 1], bank[2 + s % 2].rearrange("p (c n) -> p c n", c=TPB),
                                    part[:, 0].bitcast(F32), ALU.subtract).then_inc(a.lo, 1)

                for s in range(UNITS + 4):
                    if s < UNITS:
                        rowmax(s)
                    if 0 <= s - 1 < UNITS:
                        invert(s - 1)
                    if 0 <= s - 4 < UNITS:
                        expT_lo(s - 4)
                dve.wait_ge(a.proj, b + 1)
                V.tensor_tensor(h[:, ds(b * S, S)], h[:, ds(b * S, S)], bank[6], ALU.add).then_inc(a.add, 1)

            V.memset(tanhT[HD:HD + 1, :], 1.0).then_inc(tanh_done, 1)
            dve.wait_ge(ld_tok, 80)
            V.tensor_copy(mask_f[:], mask_i[:])
            dve.drain()
            dve.wait_ge(gath, 16 * 2 * NT)
            for b in range(B):
                span = slice(b * S, (b + 1) * S)
                dve.wait_ge(emb_ps, b + 1)
                V.tensor_tensor(h[:, span].rearrange("p (j d) -> p j d", j=TPB),
                                bank[b][:, :].rearrange("p (j d) -> p j d", j=TPB),
                                mask_f[:, b * TPB:(b + 1) * TPB].unsqueeze(2).to_broadcast([P, TPB, D]), ALU.mult)
                V.tensor_tensor(ev_rows[:, span], ev_rows[:, span], vv_rows[:, span], ALU.add)
                dve.drain()
                last = V.tensor_tensor(h[:, span], h[:, span], ev_rows[:, span], ALU.add)
            last.then_inc(h_ready, 1)
            dve.drain()

            V.memset(q_aug[:], 0.0)
            V.memset(k_aug[:], 0.0)
            V.memset(mB.v[:].bitcast(F32), 0.0).then_inc(v_zero, 1)
            dve.drain()
            V.memset(ka[:, :, :, DH0 + 1:DH0 + 2], 1.0)
            with dve.Fori(0, B) as b:
                layer_norm(lnB, b, b * TPB, TPB)
                q4 = qkv0[:, :, 0:D].rearrange("p j (h d) -> p j h d", h=H)
                k4 = qkv0[:, :, D:2 * D].rearrange("p j (h d) -> p j h d", h=H)

                def wide(s):
                    return st0[:, s].unsqueeze(3).to_broadcast([P, TPB, H, DH0])

                dve.wait_ge(qkv_sb, b * TPB + TPB)
                V.tensor_reduce(st0[:, 0], q4, AX.X, ALU.add)
                V.tensor_tensor(sqr, k4, k4, ALU.mult)
                dve.drain()
                V.tensor_scalar(st0[:, 0], st0[:, 0], 1.0 / DH0, None, ALU.mult)
                V.tensor_reduce(st0[:, 9], sqr, AX.X, ALU.add)
                dve.drain()
                V.tensor_tensor(dev, q4, wide(0), ALU.subtract)
                V.tensor_copy(ka[:, :, :, DH0], st0[:, 9])
                dve.drain()
                V.tensor_tensor(sqr, dev, dev, ALU.mult)
                V.tensor_reduce(st0[:, 3], dev, AX.X, ALU.add, apply_absolute_value=True)
                dve.drain()
                V.tensor_reduce(st0[:, 1], sqr, AX.X, ALU.add)
                dve.drain()
                V.tensor_scalar(st0[:, 1], st0[:, 1], 1.0 / DH0, EPS, ALU.mult, ALU.add).then_inc(sig2, 1)
                V.tensor_tensor(sqr, q4, q4, ALU.mult)
                V.tensor_copy(ka[:, :, :, 0:DH0], k4)
                dve.drain()
                V.tensor_reduce(st0[:, 8], sqr, AX.X, ALU.add)
                dve.wait_ge(sigma, b + 1)
                V.tensor_scalar(st0[:, 4], st0[:, 2], EPS, None, ALU.add)
                dve.drain()
                V.reciprocal(st0[:, 4], st0[:, 4])
                dve.drain()
                V.tensor_tensor(st0[:, 5], st0[:, 3], st0[:, 4], ALU.mult).then_inc(nf, 1)
                dve.wait_ge(enf, b + 1)
                V.tensor_scalar(st0[:, 7], st0[:, 6], 1.0, None, ALU.add)
                dve.drain()
                V.reciprocal(st0[:, 7], st0[:, 7])
                dve.drain()
                V.tensor_scalar(st0[:, 10], st0[:, 7], 2.0, DH0 ** -0.5, ALU.mult, ALU.add)
                V.tensor_scalar(qa[:, :, :, DH0], st0[:, 7], -1.0, None, ALU.mult)
                dve.drain()
                V.tensor_tensor(qa[:, :, :, DH0 + 1], qa[:, :, :, DH0], st0[:, 8], ALU.mult)
                V.tensor_tensor(qa[:, :, :, 0:DH0], q4, wide(10), ALU.mult)
                dve.drain()
                V.engine_nop().then_inc(aug, 1)
                dve.wait_ge(v0_hi, b + 1)
                for a in range(HPG):
                    lo = a * AUG + DH0
                    last = V.tensor_tensor(mB.v[:, :, a:H:HPG, lo:lo + DH0],
                                           qkv0[:, :, 2 * D:].rearrange("p j (g a d) -> p j g a d", a=HPG, d=DH0)[:, :, :, a, :],
                                           mB.v[:, :, a:H:HPG, lo - DH0:lo].bitcast(F32), ALU.subtract)
                last.then_inc(v0_lo, 1)
                dve.wait_ge(st_hi, 2 * b + 1)
                V.tensor_tensor(q_st[:, :, 2:4, :].bitcast(F32R), q_aug[:].unsqueeze(2).to_broadcast([P, TPB * H, 2, AUG]),
                                q_st[:, :, 0:2, :], ALU.subtract).then_inc(st_lo, 1)
                dve.wait_ge(st_hi, 2 * b + 2)
                V.tensor_tensor(k_st[:, :, :, 1, :].bitcast(F32R), k_aug[:].unsqueeze(2).to_broadcast([P, TPB * H, 2, AUG]),
                                k_st[:, :, :, 0, :], ALU.subtract).then_inc(st_lo, 1)
                for n in range(1, 2 * H, 2):
                    dve.wait_ge(augT_ps, b * 2 * H + n + 1)
                    dst = mB.qT[:, n, :] if n < H else mB.kT[:, 0, n - H, :]
                    V.tensor_copy(dst, bank[n % 4][:, :]).then_inc(augT_dve, 1)
                attention(a0, b)
                dve.drain()

            dve.wait_ge(ld_pk, 48)
            V.tensor_copy(bqb_s, bq_s[:].unsqueeze(2).to_broadcast([P, H, P])).then_inc(bq_b, 1)

            def half_max():
                for n in range(2 * H):
                    V.max(m8[:, n // 2, n % 2, :], sc[:, n // 2, n % 2, :])
                dve.drain()

            def half_index(q):
                for n in range(q * H, q * H + H):
                    V.max_index(i8[:, n // 2, n % 2, :], m8[:, n // 2, n % 2, :], sc[:, n // 2, n % 2, :])

            def pair_scores():
                V.tensor_tensor(pair_s[:], m8[:, :, 0, :].unsqueeze(3).to_broadcast([P, H, TOP, TOP]),
                                m8[:, :, 1, :].unsqueeze(2).to_broadcast([P, H, TOP, TOP]), ALU.add)

            def pair_best():
                for n in range(H):
                    V.max(b8[:, n, :], pair_s[:, n].rearrange("p a b -> p (a b)"))
                dve.drain()
                V.tensor_tensor(pe_[:], b8[:], b8[:, :, 0:1].to_broadcast([P, H, TOP]),
                                ALU.subtract).then_inc(best, 1)
                for n in range(H):
                    V.max_index(bi[:, n, :], b8[:, n, :], pair_s[:, n].rearrange("p a b -> p (a b)"))
                dve.drain()

            def expert_numbers(t):
                flat = bi[:].rearrange("p h k -> p (h k)")
                V.tensor_scalar(bab[:, 1], flat, TOP - 1, None, ALU.bitwise_and)
                V.tensor_scalar(bab[:, 0], flat, 3, None, ALU.logical_shift_right)
                dve.wait_ge(pexp, t + 1)
                V.tensor_reduce(pz[:, 0], pe_[:], AX.X, ALU.add)
                dve.drain()
                for s in (1, 0):
                    last = V.tensor_tensor(ext[:, s], bab[:, s].unsqueeze(2).to_broadcast([P, HK, TOP]),
                                           iota8[:].to_broadcast([P, HK, TOP]), ALU.is_equal)
                    if s:
                        last.then_inc(place_rdy, 1)
                V.reciprocal(pz[:, 1], pz[:, 0])
                dve.drain()
                V.tensor_tensor(ext[:, 0].rearrange("p (h k) a -> p h k a", h=H),
                                ext[:, 0].rearrange("p (h k) a -> p h k a", h=H),
                                i8[:, :, 0, :].unsqueeze(2).to_broadcast([P, H, TOP, TOP]), ALU.mult)
                for q in range(2):
                    V.tensor_tensor(uvp[:, 2, q].rearrange("p (h k) -> p h k", h=H), pe_[:],
                                    pz[:, 1].unsqueeze(2).to_broadcast([P, H, TOP]), ALU.mult)
                dve.drain()
                V.tensor_reduce(ij[:, 0], ext[:, 0], AX.X, ALU.add)
                dve.wait_ge(ext_rdy, t + 1)
                V.tensor_reduce(ij[:, 1], ext[:, 1], AX.X, ALU.add)
                dve.drain()
                V.tensor_scalar(jhi[:], ij[:, 1], float(NV), None, ALU.is_ge)
                dve.drain()
                for q in range(2):
                    V.scalar_tensor_tensor(uvp[:, 0, q], ij[:, 0], 2.0, jhi[:], ALU.mult, ALU.add)
                    last = V.scalar_tensor_tensor(uvp[:, 1, q], jhi[:], -float(NV), ij[:, 1], ALU.mult, ALU.add)
                last.then_inc(uvp_rdy, 1)

            def one_hots(t):
                dve.wait_ge(uvpT_sb, t + 1)
                V.tensor_copy(psp[:, 0], pT[:])
                V.tensor_tensor(one_v[:], iota_u[:, 0:NV, :], vT[:].unsqueeze(1).to_broadcast([P, NV, HALF]),
                                ALU.is_equal)
                dve.drain()
                V.tensor_tensor(pres[:, 0], pT[:], psp[:, 0], ALU.subtract)
                V.tensor_tensor(w_v[:, 0], one_v[:], psp[:, 0].unsqueeze(1).to_broadcast([P, NV, HALF]), ALU.mult)
                dve.drain()
                V.tensor_copy(psp[:, 1], pres[:, 0])
                dve.drain()
                V.tensor_tensor(psp[:, 2], pres[:, 0], psp[:, 1], ALU.subtract).then_inc(psp_rdy, 1)
                V.tensor_tensor(w_v[:, 1], one_v[:], psp[:, 1].unsqueeze(1).to_broadcast([P, NV, HALF]), ALU.mult)
                V.tensor_tensor(one_u, iota_u, uT[:].unsqueeze(1).to_broadcast([P, NU, HALF]),
                                ALU.is_equal).then_inc(onehot, 1)

            def weigh(t, c):
                dve.wait_ge(g_ps, t * GP + c + 1)
                if c == 0:
                    dve.wait_ge(relu_rdy, (t + 1) * (NV // IG))
                for q in range(2):
                    span = slice(q * HALF + c * GT, q * HALF + (c + 1) * GT)
                    last = V.tensor_tensor(vals[:, :, span], relu_in[:, :, span],
                                           quad[:, 2 * (c % 2) + q, :].rearrange("p (t v) -> p v t", v=NV), ALU.mult)
                last.then_inc(vals_rdy, 1)

            def ffn_residual(t):
                dve.wait_ge(ffn_ps, t + 1)
                V.tensor_tensor(h_tile(t), h_tile(t), bank[6][:, 0:D], ALU.add).then_inc(ffn_add, 1)

            dve.wait_ge(kw_sb, 4)
            dve.wait_ge(consts, 3)
            layer_norm(lnC, 0, 0, 1)
            ln_stats(lnC, 1, 1)
            dve.wait_ge(sc_sb, 2)
            ln_scale(lnC, 1, 1, 1)
            half_max()
            half_index(0)
            half_index(1)
            pair_scores()
            dve.drain()
            pair_best()
            expert_numbers(0)
            one_hots(0)

            def spread_and_best(t):
                half_max()
                weigh(t, 0)
                half_index(0)
                weigh(t, 1)
                half_index(1)
                pair_scores()
                weigh(t, 2)
                weigh(t, 3)

            dve.wait_ge(sc_sb, 4)
            dve.drain()
            with dve.Fori(0, NT - 2) as t:
                spread_and_best(t)
                ln_stats(lnC, t + 2, 1)
                pair_best()
                ln_scale(lnC, t + 2, t + 2, 1)
                expert_numbers(t + 1)
                one_hots(t + 1)
                dve.wait_ge(sc_sb, 2 * (t + 3))
                ffn_residual(t)
            spread_and_best(NT - 2)
            dve.drain()
            pair_best()
            expert_numbers(NT - 1)
            one_hots(NT - 1)
            ffn_residual(NT - 2)
            for c in range(GP):
                weigh(NT - 1, c)
            ffn_residual(NT - 1)
            dve.drain()

            with dve.Fori(0, B) as b:
                layer_norm(lnD, b, b * TPB, TPB)
                for n in range(2 * H + TPB):
                    dve.wait_ge(p1_hi, b * (2 * H + TPB) + n + 1)
                    src = bank[n % 4][:, :]
                    if n < H:
                        half = mD.qT[DH1:P, n, :]
                        V.scalar_tensor_tensor(half, src[DH1:P, :], a1.scale, half.bitcast(F32),
                                               ALU.mult, ALU.subtract).then_inc(p1_lo, 1)
                    elif n < 2 * H:
                        V.tensor_tensor(mD.kT[:, 1, n - H, :], src, mD.kT[:, 0, n - H, :].bitcast(F32),
                                        ALU.subtract).then_inc(p1_lo, 1)
                    else:
                        part = mD.v[:, n - 2 * H, :, :]
                        V.tensor_tensor(part[:, :, DH1:P], src.rearrange("p (h d) -> p h d", h=H),
                                        part[:, :, 0:DH1].bitcast(F32), ALU.subtract).then_inc(p1_lo, 1)
                attention(a1, b)
                dve.drain()

            for b in range(B):
                layer_norm(lnE, b, b * TPB, TPB)
            V.memset(aff, 0.0)
            dve.wait_ge(lg_ps, B)
            l3 = logit.rearrange("p j b e -> p (j b) e")
            V.tensor_copy(l3, bank[0][:, 0:NT * NE].rearrange("p (n e) -> p n e", n=NT))
            dve.drain()
            V.tensor_reduce(rmax[:, 0], l3, AX.X, ALU.max)
            dve.drain()
            V.tensor_tensor(l3, l3, rmax[:, 0].unsqueeze(2).to_broadcast([P, NT, NE]),
                            ALU.subtract).then_inc(lg_exp_in, 1)
            dve.wait_ge(lg_exp, 1)
            V.tensor_reduce(rmax[:, 0], l3, AX.X, ALU.add)
            dve.drain()
            V.reciprocal(rmax[:, 1], rmax[:, 0])
            dve.drain()
            V.tensor_tensor(aff.rearrange("p j b e -> p (j b) e")[:, :, 0:NE], l3,
                            rmax[:, 1].unsqueeze(2).to_broadcast([P, NT, NE]), ALU.mult).then_inc(aff_rdy, 1)
            dve.wait_ge(affT_sb, 1)
            for r in range(CAP // 8):
                src = work if r else affT
                V.max(top8[:], src)
                dve.drain()
                V.match_replace(work, top8[:], src, -1.0)
                dve.drain()
            V.tensor_tensor(gT, affT, work, ALU.not_equal)
            dve.drain()
            V.tensor_tensor(gT, gT, affT, ALU.mult).then_inc(gT_rdy, 1)
            dve.wait_ge(gN_rdy, 1)
            for b in range(B):
                dve.wait_ge(b2_ps, b + 1)
                V.tensor_tensor(h[:, b * S:(b + 1) * S], h[:, b * S:(b + 1) * S], bank[2 + b],
                                ALU.add).then_inc(y_add, 1)
            dve.drain()
            with dve.Fori(0, B) as b:
                for e in range(NE):
                    dve.wait_ge(y_ps, b * NE + e + 1)
                    for j in range(TPB):
                        last = V.scalar_tensor_tensor(h_tile(b * TPB + j), bank[2 + e % 2][:, j * D:(j + 1) * D],
                                                      gN[:, ds(b * EP + j * P + e, 1)], h_tile(b * TPB + j),
                                                      ALU.mult, ALU.add)
                    last.then_inc(y_add, 1)
                    dve.drain()
                V.engine_nop().then_inc(seq_done, 1)

        @block.tensor
        def _(pe):
            mm, tp = nc.tensor.matmul, nc.tensor.transpose

            def transpose_xn(ln, i, n=TPB):
                pe.wait_ge(ln.xn, i + 1)
                for j in range(n):
                    last = tp(bank[7][:, j * P:(j + 1) * P], xn[:, j, :], ident[:])
                last.then_inc(ln.ps, 1)

            def attention(a, b, logits, wo, bo):
                m = a.mem

                def expT(s):
                    pe.wait_ge(a.nr, b * UNITS + s + 1)
                    if s >= 2:
                        pe.wait_ge(a.lo, b * UNITS + s - 1)
                    for c in range(TPB):
                        last = tp(bank[2 + s % 2][:, c * P:(c + 1) * P], m.en[:, s % 3, c * P:(c + 1) * P], ident[:])
                    last.then_inc(a.tr, 1)

                def pv(s):
                    hd, c = s // TPB, s % TPB
                    g = hd // a.group
                    if c == 0:
                        pe.wait_ge(a.lo, b * UNITS + TPB * (hd + 1))
                    if s % (TPB * a.group) == 0 and g >= 2:
                        pe.wait_ge(a.ots, b * a.groups + g - 1)
                    for part in range(2):
                        last = mm(bank[4 + g % 2], m.v[:, c, hd, :], m.eT[:, hd % 2, part, c, :],
                                  start=(hd % a.group == 0 and c == 0 and part == 0),
                                  stop=(hd % a.group == a.group - 1 and c == TPB - 1 and part == 1))
                    last.then_inc(a.pv, 1)

                for s in range(UNITS + 8):
                    if s < UNITS:
                        if s >= 2:
                            pe.wait_ge(a.ex, b * UNITS + s - 1)
                        logits(s)
                    if 0 <= s - 3 < UNITS:
                        expT(s - 3)
                    if s >= 8:
                        pv(s - 8)
                pe.wait_ge(a.ots, b * a.groups + a.groups)
                for j in range(TPB):
                    dst = bank[6][:, j * D:(j + 1) * D]
                    for g in range(a.groups):
                        mm(dst, a.oT[:, g, j * P:(j + 1) * P], wo(g), start=(g == 0), stop=False)
                    last = mm(dst, ones[0:1, :], bo, start=False, stop=True)
                last.then_inc(a.proj, 1)

            pe.wait_ge(ld_tok, 80)
            pe.wait_ge(tanh_done, B + 1)
            for b in range(B):
                for j in range(TPB):
                    last = mm(bank[b][:, j * D:(j + 1) * D], tanhT[:, b * S + j * P:b * S + (j + 1) * P], w2b2[:],
                              start=True, stop=True)
                last.then_inc(emb_ps, 1)
            pe.wait_ge(consts, 1)
            pe.wait_ge(ld_a0, 64)

            def logits0(s):
                hd, j = s // TPB, s % TPB
                mm(bank[s % 2][:, :], mB.qT[:, hd, j * P:(j + 1) * P], mB.kT[:, 0, hd, :],
                   start=True, stop=True).then_inc(a0.qk, 1)

            with pe.Fori(0, B) as b:
                transpose_xn(lnB, b)
                pe.wait_ge(lnB.sb, b + 1)
                for j in range(TPB):
                    mm(bank[j][:, 0:3 * D], xnT[:, j * P:(j + 1) * P], wqkv0[:], start=True, stop=False)
                    mm(bank[j][:, 0:3 * D], ones[0:1, :], bqkv0[:], start=False, stop=True).then_inc(qkv_ps, 1)
                pe.wait_ge(qkv_sb, b * TPB + TPB)
                pe.wait_ge(v0_lo, b + 1)
                for n in range(2 * H):
                    if n % H == 0:
                        pe.wait_ge(st_lo, 2 * b + n // H + 1)
                    if n >= 4:
                        pe.wait_ge(augT_dve if n % 2 else augT_act, b * H + (n - 4) // 2 + 1)
                    for j in range(TPB):
                        row = j * H + n % H
                        src = q_st[:, row, :, :].rearrange("p q a -> p (q a)") if n < H else \
                            k_st[:, row, :, :, :].rearrange("p q r a -> p (q r a)")
                        last = tp(bank[n % 4][:, j * P:(j + 1) * P], src, ident[:])
                    last.then_inc(augT_ps, 1)
                pe.wait_ge(augT_act, b * H + H)
                pe.wait_ge(augT_dve, b * H + H)
                attention(a0, b, logits0, lambda g: wo0[:, g, :], bo0[:])

            pe.wait_ge(bq_b, 1)
            pe.wait_ge(ld_pk, 48)
            for k, lhs in enumerate((wqT_s, bqb_s)):
                for q in range(2):
                    for n in range(H // 2):
                        hd = q * (H // 2) + n
                        last = mm(bank[2 * k + q][:, n * P:(n + 1) * P], lhs[:, hd, :], keys_s[:, hd, :],
                                  start=True, stop=True)
                    last.then_inc(kw_ps, 1)
            pe.wait_ge(kw_sb, 4)
            pe.wait_ge(ld_exp, 32)

            def scores(t):
                pe.wait_ge(lnC.sb, t + 1)
                if not (isinstance(t, int) and t == 0):
                    pe.wait_ge(relu_rdy, t * (NV // IG))
                for q in range(2):
                    mm(bank[q][:, :], xnT[:, 0:P], keyw[:, q * 512:(q + 1) * 512],
                       start=True, stop=True).then_inc(sc_ps, 1)

            def inner(t):
                for g in range(NV // IG):
                    if g < 2:
                        pe.wait_ge(sc_raw, t * 2 + g + 1)
                    else:
                        pe.wait_ge(relu_rdy, t * (NV // IG) + g - 1)
                    for q in range(IG):
                        last = mm(bank[g % 2][:, q * P:(q + 1) * P], wd[:, IG * g + q, :], xnT[:, 0:P],
                                  start=True, stop=True)
                    last.then_inc(in_ps, 1)

            def transpose_uvp(t):
                pe.wait_ge(uvp_rdy, t + 1)
                for n in range(3):
                    last = tp(bank[7][:, (n + 1) * P:(n + 2) * P], uvp[:, n].rearrange("p q k -> p (q k)"), ident[:])
                last.then_inc(uvpT_ps, 1)

            def spread(t):
                pe.wait_ge(onehot, t + 1)
                pe.wait_ge(third_w, t + 1)
                for c in range(GP):
                    if c >= 2:
                        pe.wait_ge(vals_rdy, t * GP + c - 1)
                    for i in range(GT):
                        for q in range(2):
                            rows = slice(q * HALF, (q + 1) * HALF)
                            tok = c * GT + i
                            for s in range(3):
                                last = mm(quad[:, 2 * (c % 2) + q, i * NV:(i + 1) * NV], one_u[rows, :, tok],
                                          w_v[rows, s, :, tok], start=(s == 0), stop=(s == 2))
                    last.then_inc(g_ps, 1)

            def combine(t, part):
                if part == 0:
                    pe.wait_ge(vals_rdy, (t + 1) * GP)
                for v in range(part * NV // 2, (part + 1) * NV // 2):
                    last = mm(bank[6][:, 0:D], vals[:, v, :], wu[:, v, :], start=(v == 0), stop=(v == NV - 1))
                if part == 1:
                    last.then_inc(ffn_ps, 1)

            transpose_xn(lnC, 0, 1)
            scores(0)
            inner(0)
            transpose_xn(lnC, 1, 1)
            transpose_uvp(0)
            scores(1)
            with pe.Fori(0, NT - 2) as t:
                spread(t)
                combine(t, 0)
                pe.wait_ge(lnC.sb, t + 2)
                transpose_xn(lnC, t + 2, 1)
                transpose_uvp(t + 1)
                combine(t, 1)
                inner(t + 1)
                scores(t + 2)
            spread(NT - 2)
            combine(NT - 2, 0)
            pe.wait_ge(lnC.sb, NT)
            transpose_uvp(NT - 1)
            combine(NT - 2, 1)
            inner(NT - 1)
            spread(NT - 1)
            combine(NT - 1, 0)
            combine(NT - 1, 1)

            pe.wait_ge(ld_a1, 80)

            def logits1(s):
                hd, j = s // TPB, s % TPB
                for part in range(2):
                    last = mm(bank[s % 2][:, :], mD.qT[:, hd, j * P:(j + 1) * P], mD.kT[:, part, hd, :],
                              start=(part == 0), stop=(part == 1))
                last.then_inc(a1.qk, 1)

            with pe.Fori(0, B) as b:
                transpose_xn(lnD, b)
                pe.wait_ge(lnD.sb, b + 1)
                for n in range(2 * H + TPB):
                    if n >= 4:
                        pe.wait_ge(p1_lo, b * (2 * H + TPB) + n - 3)
                    if n < 2 * H:
                        w = (wq1, wk1)[n // H][:, (n % H) * P:(n % H + 1) * P]
                        last = mm(bank[n % 4][:, :], w, xnT[:], start=True, stop=True)
                    else:
                        j = n - 2 * H
                        last = mm(bank[n % 4][:, :], xnT[:, j * P:(j + 1) * P], wv1, start=True, stop=True)
                    last.then_inc(p1_ps, 1)
                pe.wait_ge(p1_lo, (b + 1) * (2 * H + TPB))
                attention(a1, b, logits1, lambda g: wo1[:, g, :], bo1[:])

            pe.wait_ge(ld_moe, 80)
            for b in range(B):
                if b:
                    pe.wait_ge(lnE.sb, b)
                transpose_xn(lnE, b)
                pe.wait_ge(lnE.sb, b + 1)
                for j in range(TPB):
                    last = mm(bank[0][:, (j * B + b) * NE:(j * B + b + 1) * NE], xnT[:, j * P:(j + 1) * P], gate_w[:],
                              start=True, stop=True)
                last.then_inc(lg_ps, 1)
            pe.wait_ge(aff_rdy, 1)
            for j in range(TPB):
                last = tp(bank[0][:, j * P:(j + 1) * P], aff[:, j].rearrange("p b e -> p (b e)"), ident[:])
            last.then_inc(affT_ps, 1)
            pe.wait_ge(gT_rdy, 1)
            for j in range(TPB):
                last = tp(bank[1][:, j * P:(j + 1) * P], gT[:, j * P:(j + 1) * P], ident[:])
            last.then_inc(gN_ps, 1)
            for b in range(B):
                for j in range(TPB):
                    last = mm(bank[2 + b][:, j * D:(j + 1) * D], gT[b * EP:(b + 1) * EP, j * P:(j + 1) * P],
                              b2e[b * EP:(b + 1) * EP, :], start=True, stop=True)
                last.then_inc(b2_ps, 1)
            pe.wait_ge(gN_rdy, 1)

            with pe.Fori(0, B) as b:
                def up(e):
                    if e >= 2:
                        pe.wait_ge(hid_sb, b * NE + e - 1)
                    mm(bank[e % 2][:, :], w1e[:, e, :], xnT_all[:, ds(b * S, S)], start=True, stop=True).then_inc(hid_ps, 1)

                def down(e):
                    pe.wait_ge(hid_sb, b * NE + e + 1)
                    pe.wait_ge(y_add, B + b * NE + e - 1)
                    for j in range(TPB):
                        last = mm(bank[2 + e % 2][:, j * D:(j + 1) * D], hidT[:, e % 2, j * P:(j + 1) * P], w2e[:, e, :],
                                  start=True, stop=True)
                    last.then_inc(y_ps, 1)

                up(0)
                for e in range(NE):
                    if e + 1 < NE:
                        up(e + 1)
                    down(e)


_OUT = ((4, 512, 128), "float32")


def kernel(**inputs):
    import numpy as np
    import concourse.bacc as bacc
    from concourse.bass_utils import run_bass_kernel_spmd

    g = {k: np.asarray(v) for k, v in inputs.items()}
    P, H, NK = 128, 8, 64
    c = np.ascontiguousarray

    def twice(w):
        return c(np.broadcast_to(w.reshape(P, 8, 1, 64), (P, 8, 2, 64))).reshape(P, 1024)

    keys = g["L0_ffn_keys"]
    kbd = np.zeros((P, H, P), keys.dtype)
    for q in range(2):
        kbd[q * 64:(q + 1) * 64, :, q * 64:(q + 1) * 64] = keys[:, q].transpose(2, 0, 1)
    b2 = np.zeros((4, 32, 128), g["L1_ffn_b2"].dtype)
    b2[:, 0:16] = g["L1_ffn_b2"]
    arrays = {
        "x_idx": c(g["x"].reshape(16, P).T),
        "val_idx": c(g["itok_BS_0_4999"].reshape(16, P).T),
        "num_rows": c(g["fside_BS_numeric_value"].reshape(2048)),
        "mask_idx": c(g["mask_BS_i1_0"].reshape(16, P).T),
        "event_table": g["L0_tok_event_table"],
        "value_table": g["L0_tok_value_table"],
        "tok_w1": c(g["L0_tok_w1"].reshape(64, 1)),
        "tok_b1": c(g["L0_tok_b1"].reshape(64, 1)),
        "tok_w2b2": np.concatenate([g["L0_tok_w2"], g["L0_tok_b2"][None]], 0),
        "a0_wqkv": np.concatenate([g["L0_attn_Wq"], g["L0_attn_Wk"], g["L0_attn_Wv"]], 1),
        "a0_bqkv": np.concatenate([g["L0_attn_bq"], g["L0_attn_bk"], g["L0_attn_bv"]])[None],
        "a0_wo": c(np.broadcast_to(g["L0_attn_Wo"].reshape(2, 4, 1, 16, P), (2, 4, 2, 16, P))
                   .transpose(1, 2, 3, 0, 4)).reshape(P, 2 * P),
        "a0_bo": g["L0_attn_bo"][None],
        "pk_wqT": c(g["L0_ffn_Wq"].reshape(P, H, P).transpose(2, 1, 0).reshape(P, H * P)),
        "pk_bq": c(g["L0_ffn_bq"].reshape(H, P).T),
        "pk_keys": kbd.reshape(P, H * P),
        "pk_down": c(g["L0_ffn_w_down"].reshape(128, 32, 128).transpose(2, 1, 0).reshape(P, 4096)),
        "pk_up": g["L0_ffn_w_up"].reshape(128, 4096),
        "a1_wq": twice(g["L1_attn_w_q"]),
        "a1_wk": twice(g["L1_attn_w_k"]),
        "a1_wv": g["L1_attn_w_v"],
        "a1_wo": c(np.broadcast_to(g["L1_attn_w_out"].reshape(8, 1, 64, P), (8, 2, 64, P))
                   .transpose(1, 2, 0, 3)).reshape(P, 8 * P),
        "a1_bo": g["L1_attn_b_out"][None],
        "moe_gate": g["L1_ffn_gate_weight"],
        "moe_w1": c(g["L1_ffn_w1"].transpose(1, 0, 2).reshape(P, 2048)),
        "moe_b1": c(g["L1_ffn_b1"].T),
        "moe_w2": c(g["L1_ffn_w2"].transpose(1, 0, 2).reshape(P, 2048)),
        "moe_b2": b2.reshape(P, 128),
    }
    nc = bacc.Bacc("TRN2", target_bir_lowering=False, num_devices=1)
    aps = {k: nc.dram_tensor("in_" + k, a.shape, mybir.dt.from_np(a.dtype), kind="ExternalInput").ap()
           for k, a in arrays.items()}
    out = nc.dram_tensor("out_0", _OUT[0], mybir.dt.float32, kind="ExternalOutput").ap()
    tower(nc, *aps.values(), out)
    r = run_bass_kernel_spmd(nc, [{"in_" + k: a for k, a in arrays.items()}], core_ids=[0])
    return r.results[0]["out_0"]
```

```python
import concourse.bass as bass
from concourse import mybir
from contextlib import ExitStack



def tower(nc, x_idx, val_idx, num_rows, mask_idx, event_table, value_table, tok_w1, tok_b1, tok_w2b2,
          a0_wqkv, a0_bqkv, a0_wo, a0_bo, pk_wqT, pk_bq, pk_keys, pk_down, pk_up,
          a1_wq, a1_wk, a1_wv, a1_wo, a1_bo, moe_gate, moe_w1, moe_b1, moe_w2, moe_b2, out):
    F32, BF16, F32R = mybir.dt.float32, mybir.dt.bfloat16, mybir.dt.float32r
    I32, U32 = mybir.dt.int32, mybir.dt.uint32
    ALU, ACT, AX = mybir.AluOpType, mybir.ActivationFunctionType, mybir.AxisListType
    ds = bass.ds

    P = 128
    B, S, D = 4, 512, 128
    TPB = S // P
    NT = B * TPB
    EPS = 1e-5
    HD = tok_w1.shape[0]
    H = 8
    UNITS = H * TPB
    DH0 = D // H
    AUG = 32
    HPG = P // AUG
    DH1 = 64
    NK, TOP = 64, 8
    HK = H * TOP
    NU, NV = 128, 32
    HALF = P // 2
    GT = 16
    GP = HALF // GT
    IG = 4
    NE, CAP = 16, S // 16 * 2
    EP = 32
    EMB = (0, 4, 5, 6)
    VD, VP = GP - 1, GP + 1
    LOGITS = (0, 1, 6)
    GATED = 9

    with ExitStack() as ctx:
        def sb(name, shape, dt=F32):
            return ctx.enter_context(nc.sbuf_tensor(name, shape, dt))

        def sem(name):
            return ctx.enter_context(nc.semaphore(name))

        bank = [ctx.enter_context(nc.psum_tensor(f"bank{i}", [P, 512], F32))[:, :] for i in range(2)]
        quad = ctx.enter_context(nc.psum_tensor("quad", [P, 4, 512], F32))
        bank += [quad[:, i, :] for i in range(4)]
        bank += [ctx.enter_context(nc.psum_tensor(f"bank{i}", [P, 512], F32))[:, :] for i in (6, 7)]

        h = sb("h", [P, NT * D])
        ident = sb("ident", [P, P])
        ones = sb("ones", [P, P])
        mhalf = sb("mhalf", [P, TPB * H])
        phalf = sb("phalf", [P, TPB * H])

        def h_tile(t):
            return h[:, ds(t * D, D)]

        stats = sb("stats", [P, TPB, 6])
        mv = sb("mv", [P, TPB, 2])
        veps = sb("veps", [P, TPB])
        rstd = sb("rstd", [P, TPB])
        xn = sb("xn", [P, TPB, D])
        xnT = sb("xnT", [P, S])

        w2b2 = sb("w2b2", [HD + 1, D])
        bo0 = sb("bo0", [1, D])
        bo1 = sb("bo1", [1, D])
        gate_w = sb("gate_w", [P, NE])
        b1e = sb("b1e", [P, NE])
        b2e = sb("b2e", [P, D])
        bq_s = sb("bq_s", [P, H])
        wo0 = sb("wo0", [P, H // HPG, D])
        wqkv0 = sb("wqkv0", [P, 3 * D])
        bqkv0 = sb("bqkv0", [P, 3 * D])
        wd_t = sb("wd", [P, NV * P])
        wu_t = sb("wu", [P, NV * D])
        wd = wd_t[:].rearrange("p (v u) -> p v u", v=NV)
        wu = wu_t[:].rearrange("p (v d) -> p v d", v=NV)

        class Scope:
            def __init__(self):
                self.stack = ExitStack()

            def sb(self, name, shape, dt=F32):
                return self.stack.enter_context(nc.sbuf_tensor(name, shape, dt))

            def close(self):
                self.stack.close()

        class AttentionMemory:
            def __init__(self, n, sc, k_parts):
                self.qT = sc.sb(n + "_qT", [P, H, S], F32R)
                self.kT = sc.sb(n + "_kT", [P, k_parts, H, S], F32R)
                self.v = sc.sb(n + "_v", [P, TPB, H, P], F32R)
                self.eT = sc.sb(n + "_eT", [P, 2, 2, TPB, S], F32R)
                self.e = sc.sb(n + "_e", [P, 3, S])
                self.en = sc.sb(n + "_en", [P, 3, S])
                self.negmax = sc.sb(n + "_negmax", [P, 4])
                self.rowsum = sc.sb(n + "_rowsum", [P, 4])
                self.rrec = sc.sb(n + "_rrec", [P, 4])

        num_b, tanhT = wd_t[0:HD, 0:B * S], wd_t[0:HD + 1, B * S:2 * B * S]
        ev_rows, vv_rows = wu_t[:, 0:NT * D], wu_t[:, NT * D:2 * NT * D]
        idx_e = sb("idx_e", [P, NT], I32)
        idx_v = sb("idx_v", [P, NT], I32)
        mask_i = sb("mask_i", [P, NT], I32)
        mask_f = sb("mask_f", [P, NT])
        w1c = sb("w1c", [HD, 1])
        b1c = sb("b1c", [HD, 1])

        sB = Scope()
        mB = AttentionMemory("a0", sB, 1)
        oT0 = sB.sb("oT0", [P, H // HPG, S])
        qkv0 = sB.sb("qkv0", [P, TPB, 3 * D])
        q_aug = sB.sb("q_aug", [P, TPB * H, AUG])
        k_aug = sB.sb("k_aug", [P, TPB * H, AUG])
        q_st = sB.sb("q_st", [P, TPB * H, 4, AUG])
        k_st = sB.sb("k_st", [P, TPB * H, 2, 2, AUG])
        st0 = sB.sb("st0", [P, 12, TPB, H])
        dev, dev2, k2, q2 = [q_st[:, :, n, 0:DH0].rearrange("p (j h) d -> p j h d", j=TPB) for n in range(4)]
        q4 = qkv0[:, :, 0:D].rearrange("p j (h d) -> p j h d", h=H)
        k4 = qkv0[:, :, D:2 * D].rearrange("p j (h d) -> p j h d", h=H)
        qa = q_aug[:].rearrange("p (j h) a -> p j h a", j=TPB)
        ka = k_aug[:].rearrange("p (j h) a -> p j h a", j=TPB)
        sB.close()

        sC = Scope()
        relu_in = sC.sb("relu_in", [P, NV, P])
        vals_t = sC.sb("vals", [P, NV * P])
        vals = vals_t[:].rearrange("p (v t) -> p v t", v=NV)
        one_u_t = sC.sb("one_u", [P, NU, HALF], BF16)
        iota_u_t = sC.sb("iota_u", [P, NU, HALF], BF16)
        one_u, iota_u = one_u_t[:], iota_u_t[:]
        one_v = sC.sb("one_v", [P, NV, HALF], BF16)
        w_v = sC.sb("w_v", [P, 3, 2, NV, HALF], BF16)
        iota8 = sC.sb("iota8", [P, 1, TOP])
        wqT_s = vals_t[:, 0:1024].rearrange("p (h d) -> p h d", h=H)
        keys_s = vals_t[:, 1024:2048].rearrange("p (h n) -> p h n", h=H)
        bqb_s = vals_t[:, 2048:3072].rearrange("p (h t) -> p h t", h=H)
        keyw = sC.sb("keyw", [P, H * P])
        keyb = sC.sb("keyb", [1, 2, H * P], F32R)
        ones_r = sC.sb("ones_r", [1, P], F32R)
        sc = sC.sb("sc", [P, H, 2, NK])
        m8 = sC.sb("m8", [P, H, 2, TOP])
        i8 = sC.sb("i8", [P, H, 2, TOP], U32)
        i8f = sC.sb("i8f", [P, H, TOP])
        g_sb = sC.sb("g_sb", [P, 3, GT * NV])
        pair_s = sC.sb("pair_s", [P, H, TOP, TOP])
        b8 = sC.sb("b8", [P, H, TOP])
        bi = sC.sb("bi", [P, H, TOP], U32)
        bab = sC.sb("bab", [P, 2, HK], U32)
        ext = sC.sb("ext", [P, 2, HK, TOP])
        ij = sC.sb("ij", [P, 2, HK])
        jhi = sC.sb("jhi", [P, HK])
        uvp = sC.sb("uvp", [P, 3, 2, HK])
        pe_ = sC.sb("pe_", [P, H, TOP])
        pz = sC.sb("pz", [P, 2, H])
        uT = sC.sb("uT", [P, HALF], BF16)
        vT = sC.sb("vT", [P, HALF], BF16)
        pT = sC.sb("pT", [P, HALF])
        pres = sC.sb("pres", [P, 2, HALF])
        psp = sC.sb("psp", [P, 3, HALF], BF16)
        sC.close()

        def weigh_args(c, k, bank_copy):
            tok = slice(c * GT + k * GT // 2, c * GT + (k + 1) * GT // 2)
            return (vals.rearrange("p v (q t) -> p v q t", q=2)[:, :, :, tok],
                    relu_in[:].rearrange("p v (q t) -> p v q t", q=2)[:, :, :, tok],
                    bank_copy.rearrange("p (t q v) -> p v q t", q=2, v=NV), ALU.mult)

        sD = Scope()
        mD = AttentionMemory("a1", sD, 2)
        oT1 = sD.sb("oT1", [P, H, S])
        wo1 = sD.sb("wo1", [P, H, D])
        wq1 = wd_t[:, 0:1024]
        wk1 = wd_t[:, 1024:2048]
        wv1 = wd_t[:, 2048:2560]
        sD.close()

        sE = Scope()
        w1_flat = wu_t[:, 0:NE * P]
        w2_flat = wu_t[:, NE * P:NE * (P + D)]
        w1e = w1_flat.rearrange("p (e f) -> p e f", e=NE)
        w2e = w2_flat.rearrange("p (e f) -> p e f", e=NE)
        xnT_all = sE.sb("xnT_all", [P, B * S])
        logit_t = sE.sb("logit", [P, TPB, B, NE])
        aff_t = sE.sb("aff", [P, TPB, B, EP])
        logit, aff = logit_t[:], aff_t[:]
        rmax = sE.sb("rmax", [P, 2, NT])
        affT = sE.sb("affT", [P, S])[:]
        work = sE.sb("work", [P, S])[:]
        gT = sE.sb("gT", [P, S])[:]
        gN = sE.sb("gN", [P, S])[:]
        top8 = sE.sb("top8", [P, 8])
        hidT = sE.sb("hidT", [P, 2, S])
        y0 = sE.sb("y0", [P, NE, S])
        sE.close()

        consts, v_zero = sem("consts_ready"), sem("v0_cleared")
        ld_idx, ld_tok, ld_a0, ld_pk, ld_exp = sem("ld_idx"), sem("ld_tok"), sem("ld_a0"), sem("ld_pk"), sem("ld_exp")
        ld_a1, ld_moe = sem("ld_a1"), sem("ld_moe")
        gath = [sem(f"rows_gathered{b}") for b in range(B)]
        tanh_done, emb_ps, h_ready = sem("tanh_done"), sem("emb_ps"), sem("h_ready")
        out_dma = sem("out_dma")

        class LN:
            def __init__(self, n):
                self.var = sem(n + "_var_ready")
                self.rstd = sem(n + "_rstd_ready")
                self.xn = sem(n + "_xn_ready")
                self.ps = sem(n + "_xnT_in_psum")
                self.sb = sem(n + "_xnT_in_sbuf")

        lnB, lnC, lnD, lnE = LN("lnB"), LN("lnC"), LN("lnD"), LN("lnE")

        class ATT:
            def __init__(self, n, mem, oT, group, scale):
                self.mem, self.oT, self.group, self.scale = mem, oT, group, scale
                self.groups = H // group
                self.qk = sem(n + "_logits_in_psum")
                self.mx = sem(n + "_max_ready")
                self.ex = sem(n + "_exp_done")
                self.rc = sem(n + "_sum_inverted")
                self.nr = sem(n + "_exp_normalised")
                self.tr = sem(n + "_expT_in_psum")
                self.hi = sem(n + "_expT_hi")
                self.lo = sem(n + "_expT_lo")
                self.pv = sem(n + "_pv_done")
                self.ots = sem(n + "_outT_in_sbuf")
                self.proj = sem(n + "_projected")
                self.add = sem(n + "_h_added")

        a0, a1 = ATT("a0", mB, oT0, HPG, 1.0), ATT("a1", mD, oT1, 1, DH1 ** -0.5)
        qkv_ps, qkv_sb = sem("qkv_in_psum"), sem("qkv_in_sbuf")
        squares, dev_rdy, k_aug_rdy = sem("squares"), sem("q_centred"), sem("k_aug_ready")
        sig2, sigma, nf, enf, aug = sem("q_var"), sem("q_sigma"), sem("q_nf"), sem("q_exp_nf"), sem("aug_ready")
        st_hi, st_lo, v0_hi, v0_lo = sem("stack_hi"), sem("stack_lo"), sem("v0_hi"), sem("v0_lo")
        augT_ps, augT_act, augT_dve = sem("augT_in_psum"), sem("augT_by_act"), sem("augT_by_dve")
        p1_ps, p1_hi, p1_lo = sem("proj1_in_psum"), sem("proj1_hi"), sem("proj1_lo")

        bq_b, kw_ps, kw_sb = sem("bq_spread"), sem("keyw_in_psum"), sem("keyw_in_sbuf")
        sc_ps, sc_sb, best, pexp, uvp_rdy = sem("scores_in_psum"), sem("scores_in_sbuf"), sem("best_ready"), sem("pexp"), sem("uvp_ready")
        uvpT_ps, uvpT_sb, onehot = sem("uvpT_in_psum"), sem("uvpT_in_sbuf"), sem("onehot_ready")
        g_cp, vals_pool = sem("g_copied"), sem("vals_by_pool")
        kb_lo, xnT_in = sem("keyb_lo"), sem("xnT_for_inner")
        i8f_rdy = sem("second_index_as_float")
        place_rdy, ext_rdy, psp_rdy, w_second = sem("second_place_one_hot"), sem("second_index_picked"), sem("weight_parts_ready"), sem("second_half_weights")
        g_ps, vals_rdy, in_ps, relu_rdy = sem("g_in_psum"), sem("vals_ready"), sem("inner_in_psum"), sem("relu_ready")
        ffn_ps, ffn_add = sem("ffn_in_psum"), sem("ffn_added")

        lg_ps, lg_exp_in, lg_exp, aff_rdy = sem("gate_in_psum"), sem("gate_exp_in"), sem("gate_exp"), sem("aff_ready")
        affT_ps, affT_sb, gT_rdy, gN_ps, gN_rdy = sem("affT_in_psum"), sem("affT_in_sbuf"), sem("gT_ready"), sem("gN_in_psum"), sem("gN_ready")
        hid_ps, hid_sb, y_ps, y_add, b2_ps = sem("hid_in_psum"), sem("hid_ready"), sem("y_in_psum"), sem("y_added"), sem("b2_in_psum")
        seq_done = sem("sequence_done")
        y0_sb, ld_wo1 = sem("y0_in_sbuf"), sem("ld_wo1")

        block = ctx.enter_context(nc.Block())

        @block.sync
        def _(sp):
            sp.dma_start(idx_e[:], x_idx).then_inc(ld_idx, 16)
            sp.dma_start(idx_v[:], val_idx).then_inc(ld_idx, 16)
            sp.dma_start(mask_i[:], mask_idx).then_inc(ld_tok, 16)
            sp.dma_start(num_b, num_rows.partition_broadcast(HD)).then_inc(ld_tok, 16)
            sp.dma_start(w1c[:], tok_w1).then_inc(ld_tok, 16)
            sp.dma_start(b1c[:], tok_b1).then_inc(ld_tok, 16)
            sp.dma_start(w2b2[:], tok_w2b2).then_inc(ld_tok, 16)
            sp.dma_start(bo0[:], a0_bo).then_inc(ld_a0, 16)
            sp.dma_start(bo1[:], a1_bo).then_inc(ld_a1, 16)
            sp.dma_start(gate_w[:], moe_gate).then_inc(ld_moe, 16)
            sp.dma_start(b1e[:], moe_b1).then_inc(ld_moe, 16)
            sp.dma_start(bq_s[:], pk_bq).then_inc(ld_pk, 16)
            sp.dma_start(b2e[:], moe_b2).then_inc(ld_moe, 16)
            sp.dma_start(wqkv0[:], a0_wqkv).then_inc(ld_a0, 16)
            sp.dma_start(bqkv0[:], a0_bqkv.partition_broadcast(P)).then_inc(ld_a0, 16)
            sp.dma_start(wo0[:], a0_wo.rearrange("p (g d) -> p g d", g=H // HPG)).then_inc(ld_a0, 16)
            sp.wait_ge(h_ready, B)
            sp.dma_start(wd_t[:], pk_down).then_inc(ld_exp, 16)
            sp.dma_start(wu_t[:], pk_up).then_inc(ld_exp, 16)
            sp.wait_ge(a0.add, B)
            sp.dma_start(vals_t[:, 0:1024], pk_wqT).then_inc(ld_pk, 16)
            sp.dma_start(vals_t[:, 1024:2048], pk_keys).then_inc(ld_pk, 16)
            sp.wait_ge(relu_rdy, NT * NV // IG)
            sp.dma_start(wq1, a1_wq).then_inc(ld_a1, 16)
            sp.dma_start(wk1, a1_wk).then_inc(ld_a1, 16)
            sp.dma_start(wv1, a1_wv).then_inc(ld_a1, 16)
            sp.wait_ge(ffn_add, NT)
            sp.dma_start(wo1[:], a1_wo.rearrange("p (h d) -> p h d", h=H)).then_inc(ld_wo1, 16)
            sp.dma_start(w1_flat, moe_w1).then_inc(ld_moe, 16)
            sp.dma_start(w2_flat, moe_w2).then_inc(ld_moe, 16)
            for n, b in enumerate((1, 2, 3, 0)):
                sp.wait_ge(seq_done, n + 1)
                sp.dma_start(out[b].rearrange("(j p) d -> p j d", p=P),
                             h[:, b * S:(b + 1) * S].rearrange("p (j d) -> p j d", j=TPB)).then_inc(out_dma, 16)
            sp.wait_ge(out_dma, 16 * B)

        @block.gpsimd
        def _(pool):
            nc.gpsimd.memset(ident[:], 0.0)
            nc.gpsimd.memset(ones[:], 1.0)
            nc.gpsimd.memset(mhalf[:], -0.5)
            nc.gpsimd.memset(phalf[:], 0.5)
            pool.drain()
            nc.gpsimd.affine_select(out=ident[:], in_=ident[:], compare_op=ALU.not_equal, fill=1.0, base=0,
                                    pattern=[[-1, P]], channel_multiplier=1).then_inc(consts, 1)

            def gather(b):
                for t in range(b * TPB, (b + 1) * TPB):
                    for rows, idx, table in ((ev_rows, idx_e, event_table), (vv_rows, idx_v, value_table)):
                        nc.gpsimd.indirect_dma_start(
                            out=rows[:, t * D:(t + 1) * D], out_offset=None, in_=table,
                            in_offset=bass.IndirectOffsetOnAxis(ap=idx[:, t:t + 1].bitcast(U32), axis=0)).then_inc(gath[b], 16)

            pool.wait_ge(ld_idx, 32)
            gather(0)
            gather(1)

            def rstd_step(ln, i, n):
                pool.wait_ge(ln.var, i + 1)
                nc.gpsimd.tensor_tensor(rstd[:, 0:n], veps[:, 0:n], mhalf[:, 0:n], ALU.pow).then_inc(ln.rstd, 1)

            def normalise(a, b):
                m = a.mem
                for s in range(UNITS):
                    pool.wait_ge(a.rc, b * UNITS + s + 1)
                    if s >= 3:
                        pool.wait_ge(a.tr, b * UNITS + s - 2)
                    nc.gpsimd.tensor_tensor(m.en[:, s % 3, :], m.e[:, s % 3, :],
                                            m.rrec[:, s % 4:s % 4 + 1].to_broadcast([P, S]),
                                            ALU.mult).then_inc(a.nr, 1)

            def powers0(b):
                rstd_step(lnB, b, TPB)
                if isinstance(b, int) and b == 0:
                    gather(2)
                    gather(3)
                pool.wait_ge(sig2, b + 1)
                nc.gpsimd.tensor_tensor(st0[:, 2], st0[:, 1], phalf[:].rearrange("p (j h) -> p j h", j=TPB),
                                        ALU.pow).then_inc(sigma, 1)

            powers0(0)
            with pool.Fori(0, B - 1) as b:
                normalise(a0, b)
                powers0(b + 1)
            normalise(a0, B - 1)
            pool.wait_ge(a0.add, B)
            nc.gpsimd.iota(iota_u, [[1, NU], [0, HALF]], base=0, channel_multiplier=0,
                           allow_small_or_imprecise_dtypes=True).then_inc(consts, 1)
            nc.gpsimd.iota(iota8[:], [[0, 1], [1, TOP]], base=0, channel_multiplier=0,
                           allow_small_or_imprecise_dtypes=True).then_inc(consts, 1)

            nc.gpsimd.memset(w_v[:], 0.0)
            nc.gpsimd.memset(ones_r[:].bitcast(F32), 1.0).then_inc(consts, 1)

            def pick_second(t):
                pool.wait_ge(i8f_rdy, t + 1)
                pool.wait_ge(place_rdy, t + 1)
                nc.gpsimd.tensor_tensor(ext[:, 1].rearrange("p (h k) a -> p h k a", h=H),
                                        ext[:, 1].rearrange("p (h k) a -> p h k a", h=H),
                                        i8f[:].unsqueeze(2).to_broadcast([P, H, TOP, TOP]),
                                        ALU.mult).then_inc(ext_rdy, 1)

            def weights_second(t):
                pool.drain()
                pool.wait_ge(psp_rdy, t + 1)
                for n in range(2):
                    tok = slice(n * HALF // 2, (n + 1) * HALF // 2)
                    for k in range(1, 3):
                        last = nc.gpsimd.tensor_tensor(w_v[HALF:P, k, 1, :, tok], one_v[HALF:P, :, tok],
                                                       psp[HALF:P, k, tok].unsqueeze(1).to_broadcast([HALF, NV, HALF // 2]),
                                                       ALU.mult)
                    last.then_inc(w_second, 1)
                pool.drain()

            def weigh_second(t):
                for n, (c, k, slot) in enumerate(((0, 0, 2), (0, 1, 0), (1, 1, 1), (2, 1, 0), (3, 1, 1))):
                    pool.wait_ge(g_cp, t * VP + n + 1)
                    nc.gpsimd.tensor_tensor(*weigh_args(c, k, g_sb[:, slot, :])).then_inc(vals_pool, 1)

            rstd_step(lnC, 0, 1)
            rstd_step(lnC, 1, 1)
            rstd_step(lnC, 2, 1)
            pick_second(0)
            weights_second(0)
            with pool.Fori(0, NT - 3) as t:
                weigh_second(t)
                pick_second(t + 1)
                rstd_step(lnC, t + 3, 1)
                weights_second(t + 1)
            for t in range(NT - 3, NT - 1):
                weigh_second(t)
                pick_second(t + 1)
                weights_second(t + 1)
            weigh_second(NT - 1)
            rstd_step(lnD, 0, TPB)
            with pool.Fori(0, B - 1) as b:
                normalise(a1, b)
                rstd_step(lnD, b + 1, TPB)
            normalise(a1, B - 1)
            with pool.Fori(0, B) as b:
                rstd_step(lnE, b, TPB)

        @block.scalar
        def _(act):
            def copy_xnT(ln, i, n=S, src=None, dst=None):
                act.wait_ge(ln.ps, i + 1)
                nc.scalar.copy(xnT[:, 0:n] if dst is None else dst,
                               bank[7][:, 0:n]).then_inc(ln.sb, 1)

            def attention(a, b, next_ln=None):
                m = a.mem

                def exp(s):
                    act.wait_ge(a.mx, b * UNITS + s + 1)
                    if s >= 3:
                        act.wait_ge(a.nr, b * UNITS + s - 2)
                    nc.scalar.activation(m.e[:, s % 3, :], bank[LOGITS[s % 3]][:, :], ACT.Exp,
                                         bias=m.negmax[:, s % 4:s % 4 + 1],
                                         accum_out=m.rowsum[:, s % 4:s % 4 + 1]).then_inc(a.ex, 1)

                def expT_hi(s):
                    hd, j = s // TPB, s % TPB
                    act.wait_ge(a.tr, b * UNITS + s + 1)
                    if j == 0 and hd >= 2:
                        act.wait_ge(a.pv, b * UNITS + TPB * (hd - 1))
                    nc.scalar.copy(m.eT[:, hd % 2, 0, :, j * P:(j + 1) * P],
                                   bank[2 + s % 2].rearrange("p (c n) -> p c n", c=TPB)).then_inc(a.hi, 1)

                def outT(g):
                    act.wait_ge(a.pv, b * UNITS + TPB * a.group * (g + 1))
                    nc.scalar.copy(a.oT[:, g, :], bank[4 + g % 2]).then_inc(a.ots, 1)

                for s in range(UNITS + 9):
                    if s < UNITS:
                        exp(s)
                    if 0 <= s - 3 < UNITS:
                        expT_hi(s - 3)
                    done = s - 8
                    if done > 0 and done % (TPB * a.group) == 0:
                        outT(done // (TPB * a.group) - 1)
                    if s == UNITS + 4 and next_ln is not None:
                        copy_xnT(next_ln, b + 1)

            act.wait_ge(ld_tok, 80)
            for b in range(B):
                nc.scalar.activation(tanhT[0:HD, b * S:(b + 1) * S], num_b[:, b * S:(b + 1) * S], ACT.Tanh,
                                     bias=b1c[:, 0:1], scale=w1c[:, 0:1]).then_inc(tanh_done, 1)
            def heads0(b):
                act.wait_ge(qkv_sb, b * TPB + TPB)
                nc.scalar.square(k2, k4).then_inc(squares, 1)
                nc.scalar.copy(ka[:, :, :, 0:DH0], k4)
                act.wait_ge(dev_rdy, b + 1)
                nc.scalar.square(dev2, dev).then_inc(squares, 1)
                nc.scalar.square(q2, q4).then_inc(squares, 1)
                act.drain()
                act.wait_ge(k_aug_rdy, b + 1)
                nc.scalar.copy(k_st[:, :, :, 0, :].bitcast(F32R), k_aug[:].unsqueeze(2).to_broadcast([P, TPB * H, 2, AUG])).then_inc(st_hi, 1)
                act.wait_ge(v_zero, 1)
                for a in range(HPG):
                    last = nc.scalar.copy(mB.v[:, :, a:H:HPG, a * AUG:a * AUG + DH0],
                                          qkv0[:, :, 2 * D:].rearrange("p j (g a d) -> p j g a d", a=HPG, d=DH0)[:, :, :, a, :])
                last.then_inc(v0_hi, 1)
                for n in range(H):
                    act.wait_ge(augT_ps, b * 2 * H + n + 1)
                    nc.scalar.copy(mB.kT[:, 0, n, :], bank[n % 4][:, :]).then_inc(augT_act, 1)
                    if n == 3:
                        act.wait_ge(nf, b + 1)
                        nc.scalar.activation(st0[:, 6], st0[:, 5], ACT.Exp, scale=-1.0).then_inc(enf, 1)
                act.wait_ge(aug, b + 1)
                nc.scalar.copy(q_st[:, :, 0:2, :].bitcast(F32R), q_aug[:].unsqueeze(2).to_broadcast([P, TPB * H, 2, AUG])).then_inc(st_hi, 1)
                for n in range(0, H, 2):
                    act.wait_ge(augT_ps, b * 2 * H + H + n + 1)
                    nc.scalar.copy(mB.qT[:, n, :], bank[n % 4][:, :]).then_inc(augT_act, 1)

            copy_xnT(lnB, 0)
            heads0(0)
            with act.Fori(0, B - 1) as b:
                attention(a0, b, lnB)
                heads0(b + 1)
            attention(a0, B - 1)

            for n in range(2):
                act.wait_ge(kw_ps, n + 1)
                nc.scalar.copy(keyw[:, n * 512:(n + 1) * 512], bank[n][:, :]).then_inc(kw_sb, 1)
            for n in range(2):
                act.wait_ge(kw_ps, n + 3)
                nc.scalar.copy(keyb[:, 0, n * 512:(n + 1) * 512], bank[2 + n][0:1, :]).then_inc(kw_sb, 1)

            def relu_inner(t):
                if not (isinstance(t, int) and t == 0):
                    act.wait_ge(vals_rdy, t * VD)
                    act.wait_ge(vals_pool, t * VP)
                for g in range(NV // IG):
                    act.wait_ge(in_ps, t * (NV // IG) + g + 1)
                    nc.scalar.activation(relu_in[:, IG * g:IG * g + IG, :],
                                         bank[g % 2][:, :].rearrange("p (v t) -> p v t", v=IG),
                                         ACT.Relu).then_inc(relu_rdy, 1)

            def softmax_exp(t):
                act.wait_ge(best, t + 1)
                nc.scalar.activation(pe_[:], pe_[:], ACT.Exp).then_inc(pexp, 1)

            def xnT_for_inner(t):
                if not (isinstance(t, int) and t == 0):
                    act.wait_ge(in_ps, t * (NV // IG))
                nc.scalar.copy(xnT[:, 0:P], xnT[:, P:2 * P]).then_inc(xnT_in, 1)

            def copy_xnT_tile(t):
                copy_xnT(lnC, t, P, dst=xnT[:, P:2 * P])

            def copy_uvpT(t):
                act.wait_ge(uvpT_ps, t + 1)
                for dst, c in ((uT, 1), (vT, 2), (pT, 3)):
                    for q in range(2):
                        last = nc.scalar.copy(dst[q * HALF:(q + 1) * HALF, :],
                                              bank[7][q * HALF:(q + 1) * HALF,
                                                      c * P + q * HALF:c * P + (q + 1) * HALF])
                for q in range(2):
                    rows = slice(q * HALF, (q + 1) * HALF)
                    last = nc.scalar.copy(psp[rows, 0], bank[7][rows, 3 * P + q * HALF:3 * P + (q + 1) * HALF])
                last.then_inc(uvpT_sb, 1)

            def copy_scores(t):
                if not (isinstance(t, int) and t == 0):
                    act.wait_ge(best, t)
                for q in range(2):
                    act.wait_ge(sc_ps, t * 2 + q + 1)
                    nc.scalar.copy(sc[:, 4 * q:4 * q + 4].rearrange("p h a n -> p (h a n)"),
                                   bank[q][:, :]).then_inc(sc_sb, 1)

            def second_index(t):
                act.wait_ge(best, t + 1)
                if not (isinstance(t, int) and t == 0):
                    act.wait_ge(ext_rdy, t)
                nc.scalar.copy(i8f[:], i8[:, :, 1, :]).then_inc(i8f_rdy, 1)

            def copy_weights(t):
                for c in range(GP):
                    act.wait_ge(g_ps, t * GP + c + 1)
                    if c == 0:
                        nc.scalar.copy(g_sb[:, 2, :], quad[:, 0, :]).then_inc(g_cp, 1)
                    if c >= 2:
                        act.wait_ge(vals_pool, t * VP + c)
                    nc.scalar.copy(g_sb[:, c % 2, :], quad[:, 2 * (c % 2) + 1, :]).then_inc(g_cp, 1)

            copy_xnT_tile(0)
            copy_scores(0)
            act.drain()
            xnT_for_inner(0)
            relu_inner(0)
            copy_xnT_tile(1)
            softmax_exp(0)
            second_index(0)
            copy_scores(1)
            copy_uvpT(0)
            act.drain()
            xnT_for_inner(1)
            with act.Fori(0, NT - 2) as t:
                copy_weights(t)
                copy_xnT_tile(t + 2)
                softmax_exp(t + 1)
                second_index(t + 1)
                copy_scores(t + 2)
                copy_uvpT(t + 1)
                relu_inner(t + 1)
                xnT_for_inner(t + 2)
            copy_weights(NT - 2)
            softmax_exp(NT - 1)
            second_index(NT - 1)
            copy_uvpT(NT - 1)
            relu_inner(NT - 1)
            copy_weights(NT - 1)

            def heads1(b):
                for n in range(2 * H + TPB):
                    act.wait_ge(p1_ps, b * (2 * H + TPB) + n + 1)
                    src = bank[n % 4][:, :]
                    if n < H:
                        nc.scalar.mul(mD.qT[:, n, :], src, a1.scale).then_inc(p1_hi, 1)
                    elif n < 2 * H:
                        nc.scalar.copy(mD.kT[:, 0, n - H, :], src).then_inc(p1_hi, 1)
                    else:
                        nc.scalar.copy(mD.v[:, n - 2 * H, :, 0:DH1],
                                       src.rearrange("p (h d) -> p h d", h=H)).then_inc(p1_hi, 1)

            copy_xnT(lnD, 0)
            heads1(0)
            with act.Fori(0, B - 1) as b:
                attention(a1, b, lnD)
                heads1(b + 1)
            attention(a1, B - 1)

            for b in range(B):
                act.wait_ge(lnE.ps, b + 1)
                nc.scalar.copy(xnT[:], bank[7][:, :])
                nc.scalar.copy(xnT_all[:, b * S:(b + 1) * S], bank[7][:, :]).then_inc(lnE.sb, 1)
            act.wait_ge(lg_exp_in, 1)
            nc.scalar.activation(logit, logit, ACT.Exp).then_inc(lg_exp, 1)
            def gelu(b, e):
                act.wait_ge(hid_ps, b * NE + e + 1)
                if isinstance(b, int) and b == 0 and e < 2:
                    pass
                else:
                    act.wait_ge(y_ps, b * NE + e - 1)
                nc.scalar.activation(hidT[:, e % 2, :], bank[e % 2][:, :], ACT.Gelu_apprx_tanh,
                                     bias=b1e[:, e:e + 1]).then_inc(hid_sb, 1)

            def keep_y0(e):
                act.wait_ge(y_ps, e + 1)
                nc.scalar.copy(y0[:, e, :], bank[2 + e % 2]).then_inc(y0_sb, 1)

            gelu(0, 0)
            act.wait_ge(affT_ps, 1)
            nc.scalar.copy(affT, bank[7][:, :]).then_inc(affT_sb, 1)
            for e in range(1, NE):
                gelu(0, e)
                keep_y0(e - 1)
                if e == GATED + 1:
                    act.wait_ge(gN_ps, 1)
                    nc.scalar.copy(gN, bank[6][:, :]).then_inc(gN_rdy, 1)
            keep_y0(NE - 1)
            with act.Fori(1, B) as b:
                for e in range(NE):
                    gelu(b, e)

        @block.vector
        def _(dve):
            V = nc.vector

            def ln_stats(ln, first, n):
                for j in range(n):
                    V.bn_stats(stats[:, j, :], h_tile(first + j))
                dve.drain()
                for j in range(n):
                    V.bn_aggr(mv[:, j, :], stats[:, j, :])
                dve.drain()
                V.tensor_scalar(veps[:, 0:n], mv[:, 0:n, 1], EPS, None, ALU.add).then_inc(ln.var, 1)

            def ln_scale(ln, i, first, n):
                if ln is lnE and i:
                    dve.wait_ge(ln.ps, i)
                dve.wait_ge(ln.rstd, i + 1)
                for j in range(n):
                    last = V.tensor_scalar(xn[:, j, :], h_tile(first + j), mv[:, j, 0:1], rstd[:, j:j + 1],
                                           ALU.subtract, ALU.mult)
                last.then_inc(ln.xn, 1)

            def layer_norm(ln, i, first, n):
                ln_stats(ln, first, n)
                ln_scale(ln, i, first, n)

            def attention(a, b, next_ln=None):
                m = a.mem

                def rowmax(s):
                    dve.wait_ge(a.qk, b * UNITS + s + 1)
                    V.tensor_reduce(m.negmax[:, s % 4:s % 4 + 1], bank[LOGITS[s % 3]][:, :], AX.X, ALU.max,
                                    negate=True).then_inc(a.mx, 1)

                def invert(s):
                    dve.wait_ge(a.ex, b * UNITS + s + 1)
                    if s >= 4:
                        dve.wait_ge(a.nr, b * UNITS + s - 3)
                    V.reciprocal(m.rrec[:, s % 4:s % 4 + 1], m.rowsum[:, s % 4:s % 4 + 1]).then_inc(a.rc, 1)

                def expT_lo(s):
                    hd, j = s // TPB, s % TPB
                    dve.wait_ge(a.hi, b * UNITS + s + 1)
                    part = m.eT[:, hd % 2, :, :, j * P:(j + 1) * P]
                    V.tensor_tensor(part[:, 1], bank[2 + s % 2].rearrange("p (c n) -> p c n", c=TPB),
                                    part[:, 0].bitcast(F32), ALU.subtract).then_inc(a.lo, 1)

                for s in range(UNITS + 4):
                    if s < UNITS:
                        rowmax(s)
                    if 0 <= s - 1 < UNITS:
                        invert(s - 1)
                    if 0 <= s - 4 < UNITS:
                        expT_lo(s - 4)
                    if s == UNITS and next_ln is not None:
                        ln_stats(next_ln, (b + 1) * TPB, TPB)
                    if s == UNITS + 2 and next_ln is not None:
                        ln_scale(next_ln, b + 1, (b + 1) * TPB, TPB)

            def residual(a, b):
                dve.wait_ge(a.proj, b + 1)
                V.tensor_tensor(h[:, ds(b * S, S)], h[:, ds(b * S, S)], bank[6], ALU.add).then_inc(a.add, 1)

            V.memset(tanhT[HD:HD + 1, :], 1.0).then_inc(tanh_done, 1)
            V.memset(q_aug[:], 0.0)
            V.memset(k_aug[:], 0.0)
            V.memset(mB.v[:].bitcast(F32), 0.0).then_inc(v_zero, 1)
            dve.drain()
            V.memset(ka[:, :, :, DH0 + 1:DH0 + 2], 1.0)
            dve.wait_ge(ld_tok, 80)
            V.tensor_copy(mask_f[:], mask_i[:])
            dve.drain()

            def embed(b):
                span = slice(b * S, (b + 1) * S)
                dve.wait_ge(emb_ps, b + 1)
                V.tensor_tensor(h[:, span].rearrange("p (j d) -> p j d", j=TPB),
                                bank[EMB[b]][:, :].rearrange("p (j d) -> p j d", j=TPB),
                                mask_f[:, b * TPB:(b + 1) * TPB].unsqueeze(2).to_broadcast([P, TPB, D]), ALU.mult)
                dve.wait_ge(gath[b], 16 * 2 * TPB)
                V.tensor_tensor(ev_rows[:, span], ev_rows[:, span], vv_rows[:, span], ALU.add)
                dve.drain()
                V.tensor_tensor(h[:, span], h[:, span], ev_rows[:, span], ALU.add).then_inc(h_ready, 1)
                dve.drain()

            def heads0(b, before=None):
                """A sequence's q, k and v with their biases, augmented and split."""
                def wide(s):
                    return st0[:, s].unsqueeze(3).to_broadcast([P, TPB, H, DH0])

                for j in range(TPB):
                    dve.wait_ge(qkv_ps, b * TPB + j + 1)
                    V.tensor_tensor(qkv0[:, j, :], bank[j][:, 0:3 * D], bqkv0[:], ALU.add).then_inc(qkv_sb, 1)
                if before is not None:
                    residual(a0, before)
                else:
                    embed(1)
                dve.drain()
                V.tensor_reduce(st0[:, 0], q4, AX.X, ALU.add)
                dve.drain()
                V.tensor_scalar(st0[:, 0], st0[:, 0], 1.0 / DH0, None, ALU.mult)
                dve.wait_ge(squares, 3 * b + 1)
                V.tensor_reduce(ka[:, :, :, DH0], k2, AX.X, ALU.add).then_inc(k_aug_rdy, 1)
                dve.drain()
                V.tensor_tensor(dev, q4, wide(0), ALU.subtract).then_inc(dev_rdy, 1)
                dve.drain()
                V.tensor_reduce(st0[:, 3], dev, AX.X, ALU.add, apply_absolute_value=True)
                dve.wait_ge(squares, 3 * b + 2)
                V.tensor_reduce(st0[:, 1], dev2, AX.X, ALU.add)
                dve.drain()
                V.tensor_scalar(st0[:, 1], st0[:, 1], 1.0 / DH0, EPS, ALU.mult, ALU.add).then_inc(sig2, 1)
                dve.wait_ge(squares, 3 * b + 3)
                V.tensor_reduce(st0[:, 8], q2, AX.X, ALU.add)
                dve.wait_ge(st_hi, 2 * b + 1)
                V.tensor_tensor(k_st[:, :, :, 1, :].bitcast(F32R), k_aug[:].unsqueeze(2).to_broadcast([P, TPB * H, 2, AUG]),
                                k_st[:, :, :, 0, :], ALU.subtract).then_inc(st_lo, 1)
                dve.wait_ge(v0_hi, b + 1)
                for a in range(HPG):
                    lo = a * AUG + DH0
                    last = V.tensor_tensor(mB.v[:, :, a:H:HPG, lo:lo + DH0],
                                           qkv0[:, :, 2 * D:].rearrange("p j (g a d) -> p j g a d", a=HPG, d=DH0)[:, :, :, a, :],
                                           mB.v[:, :, a:H:HPG, lo - DH0:lo].bitcast(F32), ALU.subtract)
                last.then_inc(v0_lo, 1)
                if before is None:
                    embed(2)
                    embed(3)
                dve.wait_ge(sigma, b + 1)
                V.tensor_scalar(st0[:, 4], st0[:, 2], EPS, None, ALU.add)
                dve.drain()
                V.reciprocal(st0[:, 4], st0[:, 4])
                dve.drain()
                V.tensor_tensor(st0[:, 5], st0[:, 3], st0[:, 4], ALU.mult).then_inc(nf, 1)
                dve.wait_ge(enf, b + 1)
                V.tensor_scalar(st0[:, 7], st0[:, 6], 1.0, None, ALU.add)
                dve.drain()
                V.reciprocal(st0[:, 7], st0[:, 7])
                dve.drain()
                V.tensor_scalar(st0[:, 10], st0[:, 7], 2.0, DH0 ** -0.5, ALU.mult, ALU.add)
                V.tensor_scalar(qa[:, :, :, DH0], st0[:, 7], -1.0, None, ALU.mult)
                dve.drain()
                V.tensor_tensor(qa[:, :, :, DH0 + 1], qa[:, :, :, DH0], st0[:, 8], ALU.mult)
                V.tensor_tensor(qa[:, :, :, 0:DH0], q4, wide(10), ALU.mult)
                dve.drain()
                V.engine_nop().then_inc(aug, 1)
                dve.wait_ge(st_hi, 2 * b + 2)
                V.tensor_tensor(q_st[:, :, 2:4, :].bitcast(F32R), q_aug[:].unsqueeze(2).to_broadcast([P, TPB * H, 2, AUG]),
                                q_st[:, :, 0:2, :], ALU.subtract).then_inc(st_lo, 1)
                for n in range(1, H, 2):
                    dve.wait_ge(augT_ps, b * 2 * H + H + n + 1)
                    V.tensor_copy(mB.qT[:, n, :], bank[n % 4][:, :]).then_inc(augT_dve, 1)

            embed(0)
            layer_norm(lnB, 0, 0, TPB)
            heads0(0)
            with dve.Fori(0, B - 1) as b:
                attention(a0, b, lnB)
                heads0(b + 1, b)
            attention(a0, B - 1)
            residual(a0, B - 1)
            dve.drain()

            dve.wait_ge(ld_pk, 48)
            V.tensor_copy(bqb_s, bq_s[:].unsqueeze(2).to_broadcast([P, H, P])).then_inc(bq_b, 1)

            def half_max():
                for n in range(2 * H):
                    V.max(m8[:, n // 2, n % 2, :], sc[:, n // 2, n % 2, :])
                dve.drain()

            def half_index(q):
                for n in range(q * H, q * H + H):
                    V.max_index(i8[:, n // 2, n % 2, :], m8[:, n // 2, n % 2, :], sc[:, n // 2, n % 2, :])

            def pair_scores():
                V.tensor_tensor(pair_s[:], m8[:, :, 0, :].unsqueeze(3).to_broadcast([P, H, TOP, TOP]),
                                m8[:, :, 1, :].unsqueeze(2).to_broadcast([P, H, TOP, TOP]), ALU.add)

            def pair_best():
                for n in range(H):
                    V.max(b8[:, n, :], pair_s[:, n].rearrange("p a b -> p (a b)"))
                dve.drain()
                V.tensor_tensor(pe_[:], b8[:], b8[:, :, 0:1].to_broadcast([P, H, TOP]),
                                ALU.subtract).then_inc(best, 1)
                for n in range(H):
                    V.max_index(bi[:, n, :], b8[:, n, :], pair_s[:, n].rearrange("p a b -> p (a b)"))
                dve.drain()

            def expert_numbers(t, ln_tile=None):
                if ln_tile is not None:
                    V.bn_stats(stats[:, 0, :], h_tile(ln_tile))
                flat = bi[:].rearrange("p h k -> p (h k)")
                V.tensor_scalar(bab[:, 1], flat, TOP - 1, None, ALU.bitwise_and)
                V.tensor_scalar(bab[:, 0], flat, 3, None, ALU.logical_shift_right)
                dve.wait_ge(pexp, t + 1)
                V.tensor_reduce(pz[:, 0], pe_[:], AX.X, ALU.add)
                dve.drain()
                for s in (1, 0):
                    last = V.tensor_tensor(ext[:, s], bab[:, s].unsqueeze(2).to_broadcast([P, HK, TOP]),
                                           iota8[:].to_broadcast([P, HK, TOP]), ALU.is_equal)
                    if s:
                        last.then_inc(place_rdy, 1)
                V.reciprocal(pz[:, 1], pz[:, 0])
                if ln_tile is not None:
                    V.bn_aggr(mv[:, 0, :], stats[:, 0, :])
                dve.drain()
                if ln_tile is not None:
                    V.tensor_scalar(veps[:, 0:1], mv[:, 0:1, 1], EPS, None, ALU.add).then_inc(lnC.var, 1)
                V.tensor_tensor(ext[:, 0].rearrange("p (h k) a -> p h k a", h=H),
                                ext[:, 0].rearrange("p (h k) a -> p h k a", h=H),
                                i8[:, :, 0, :].unsqueeze(2).to_broadcast([P, H, TOP, TOP]), ALU.mult)
                V.tensor_tensor(uvp[:, 2].rearrange("p q (h k) -> p q h k", h=H),
                                pe_[:].unsqueeze(1).to_broadcast([P, 2, H, TOP]),
                                pz[:, 1].unsqueeze(1).unsqueeze(3).to_broadcast([P, 2, H, TOP]), ALU.mult)
                dve.drain()
                V.tensor_reduce(ij[:, 0], ext[:, 0], AX.X, ALU.add)
                dve.wait_ge(ext_rdy, t + 1)
                V.tensor_reduce(ij[:, 1], ext[:, 1], AX.X, ALU.add)
                dve.drain()
                V.tensor_scalar(jhi[:], ij[:, 1], float(NV), None, ALU.is_ge)
                dve.drain()
                both = [P, 2, HK]
                V.scalar_tensor_tensor(uvp[:, 0], ij[:, 0:1].to_broadcast(both), 2.0,
                                       jhi[:].unsqueeze(1).to_broadcast(both), ALU.mult, ALU.add)
                if not (isinstance(t, int) and t == NT - 1):
                    dve.wait_ge(sc_sb, 2 * (t + 2))
                V.scalar_tensor_tensor(uvp[:, 1], jhi[:].unsqueeze(1).to_broadcast(both), -float(NV),
                                       ij[:, 1:2].to_broadcast(both), ALU.mult, ALU.add).then_inc(uvp_rdy, 1)

            def one_hots(t, meanwhile=None):
                if not (isinstance(t, int) and t == NT - 1):
                    half_max()
                dve.wait_ge(uvpT_sb, t + 1)
                V.tensor_tensor(pres[:, 0], pT[:], psp[:, 0], ALU.subtract)
                dve.drain()
                V.tensor_copy(psp[:, 1], pres[:, 0])
                dve.drain()
                V.tensor_tensor(psp[:, 2], pres[:, 0], psp[:, 1], ALU.subtract)
                V.tensor_tensor(one_v[:], iota_u[:, 0:NV, :], vT[:].unsqueeze(1).to_broadcast([P, NV, HALF]),
                                ALU.is_equal).then_inc(psp_rdy, 1)
                if meanwhile is not None:
                    meanwhile()
                dve.drain()
                for k in range(3):
                    for q in range(2 if k == 0 else 1):
                        rows = slice(q * HALF, (q + 1) * HALF)
                        V.tensor_tensor(w_v[rows, k, q], one_v[rows],
                                        psp[rows, k].unsqueeze(1).to_broadcast([HALF, NV, HALF]), ALU.mult)
                for c in range(GP):
                    tok = slice(c * GT, (c + 1) * GT)
                    V.tensor_tensor(one_u[:, :, tok], iota_u[:, :, tok],
                                    uT[:, tok].unsqueeze(1).to_broadcast([P, NU, GT]),
                                    ALU.is_equal).then_inc(onehot, 1)

            def weigh(t, c):
                dve.wait_ge(g_ps, t * GP + c + 1)
                if c == 1:
                    dve.wait_ge(relu_rdy, (t + 1) * (NV // IG))
                V.tensor_tensor(*weigh_args(c, 0, quad[:, 2 * (c % 2), :])).then_inc(vals_rdy, 1)

            def ffn_residual(t):
                dve.wait_ge(ffn_ps, t + 1)
                V.tensor_tensor(h_tile(t), h_tile(t), bank[6][:, 0:D], ALU.add).then_inc(ffn_add, 1)

            for n in range(2):
                dve.wait_ge(kw_sb, n + 3)
                part = keyb[:, :, n * 512:(n + 1) * 512]
                V.tensor_tensor(part[:, 1], bank[2 + n][0:1, :], part[:, 0].bitcast(F32), ALU.subtract).then_inc(kb_lo, 1)
            dve.wait_ge(consts, 4)
            layer_norm(lnC, 0, 0, 1)
            dve.wait_ge(sc_sb, 2)
            ln_stats(lnC, 1, 1)
            ln_scale(lnC, 1, 1, 1)
            half_max()
            half_index(0)
            half_index(1)
            pair_scores()
            dve.drain()
            pair_best()
            expert_numbers(0, 2)
            one_hots(0, lambda: ln_scale(lnC, 2, 2, 1))

            def spread_and_best(t, ln_tile=None):
                weigh(t, 1)
                half_index(0)
                weigh(t, 2)
                half_index(1)
                pair_scores()
                weigh(t, 3)
                dve.drain()
                pair_best()
                expert_numbers(t + 1, ln_tile)

            with dve.Fori(0, NT - 3) as t:
                spread_and_best(t, t + 3)
                one_hots(t + 1, lambda: ln_scale(lnC, t + 3, t + 3, 1))
                ffn_residual(t)
            for t in range(NT - 3, NT - 1):
                spread_and_best(t)
                one_hots(t + 1)
                ffn_residual(t)
            for c in range(1, GP):
                weigh(NT - 1, c)
            ffn_residual(NT - 1)
            dve.drain()

            def heads1(b, before=None):
                for n in range(2 * H + TPB):
                    if n == 2 * H and before is not None:
                        residual(a1, before)
                    dve.wait_ge(p1_hi, b * (2 * H + TPB) + n + 1)
                    src = bank[n % 4][:, :]
                    if n < H:
                        half = mD.qT[DH1:P, n, :]
                        V.scalar_tensor_tensor(half, src[DH1:P, :], a1.scale, half.bitcast(F32),
                                               ALU.mult, ALU.subtract).then_inc(p1_lo, 1)
                    elif n < 2 * H:
                        V.tensor_tensor(mD.kT[:, 1, n - H, :], src, mD.kT[:, 0, n - H, :].bitcast(F32),
                                        ALU.subtract).then_inc(p1_lo, 1)
                    else:
                        part = mD.v[:, n - 2 * H, :, :]
                        V.tensor_tensor(part[:, :, DH1:P], src.rearrange("p (h d) -> p h d", h=H),
                                        part[:, :, 0:DH1].bitcast(F32), ALU.subtract).then_inc(p1_lo, 1)

            layer_norm(lnD, 0, 0, TPB)
            heads1(0)
            with dve.Fori(0, B - 1) as b:
                attention(a1, b, lnD)
                heads1(b + 1, b)
            attention(a1, B - 1)
            residual(a1, B - 1)
            dve.drain()

            for b in range(B):
                layer_norm(lnE, b, b * TPB, TPB)
            V.memset(aff, 0.0)
            dve.wait_ge(lg_ps, B)
            l3 = logit.rearrange("p j b e -> p (j b) e")
            V.tensor_copy(l3, bank[6][:, 0:NT * NE].rearrange("p (n e) -> p n e", n=NT))
            dve.drain()
            V.tensor_reduce(rmax[:, 0], l3, AX.X, ALU.max)
            dve.drain()
            V.tensor_tensor(l3, l3, rmax[:, 0].unsqueeze(2).to_broadcast([P, NT, NE]),
                            ALU.subtract).then_inc(lg_exp_in, 1)
            dve.wait_ge(lg_exp, 1)
            V.tensor_reduce(rmax[:, 0], l3, AX.X, ALU.add)
            dve.drain()
            V.reciprocal(rmax[:, 1], rmax[:, 0])
            dve.drain()
            V.tensor_tensor(aff.rearrange("p j b e -> p (j b) e")[:, :, 0:NE], l3,
                            rmax[:, 1].unsqueeze(2).to_broadcast([P, NT, NE]), ALU.mult).then_inc(aff_rdy, 1)
            dve.wait_ge(affT_sb, 1)
            for r in range(CAP // 8):
                src = work if r else affT
                V.max(top8[:], src)
                dve.drain()
                V.match_replace(work, top8[:], src, -1.0)
                dve.drain()
            V.tensor_tensor(gT, affT, work, ALU.not_equal)
            dve.drain()
            V.tensor_tensor(gT, gT, affT, ALU.mult).then_inc(gT_rdy, 1)
            dve.wait_ge(gN_rdy, 1)
            for b in range(B):
                dve.wait_ge(b2_ps, b + 1)
                V.tensor_tensor(h[:, b * S:(b + 1) * S], h[:, b * S:(b + 1) * S], bank[4 + b % 2],
                                ALU.add).then_inc(y_add, 1)
            dve.drain()

            def add_y0(e):
                for j in range(TPB):
                    last = V.scalar_tensor_tensor(h[:, j * D:(j + 1) * D], y0[:, e, j * D:(j + 1) * D],
                                                  gN[:, j * P + e:j * P + e + 1], h[:, j * D:(j + 1) * D],
                                                  ALU.mult, ALU.add)
                return last

            spare = NE // (B - 1)
            dve.wait_ge(y0_sb, NE)
            with dve.Fori(0, B - 1) as i:
                for e in range(NE):
                    dve.wait_ge(y_ps, (i + 1) * NE + e + 1)
                    for j in range(TPB):
                        tile = (i + 1) * TPB + j
                        last = V.scalar_tensor_tensor(h_tile(tile), bank[2 + e % 2][:, j * D:(j + 1) * D],
                                                      gN[:, ds((i + 1) * EP + j * P + e, 1)], h_tile(tile),
                                                      ALU.mult, ALU.add)
                    last.then_inc(y_add, 1)
                    if e % (B - 1) == B - 2:
                        k = e // (B - 1)
                        for j in range(TPB):
                            V.scalar_tensor_tensor(h[:, j * D:(j + 1) * D], y0[:, ds(i * spare + k, 1), j * D:(j + 1) * D],
                                                   gN[:, ds(i * spare + (j * P + k), 1)], h[:, j * D:(j + 1) * D],
                                                   ALU.mult, ALU.add)
                    dve.drain()
                V.engine_nop().then_inc(seq_done, 1)
            for e in range(spare * (B - 1), NE):
                last = add_y0(e)
            last.then_inc(seq_done, 1)

        @block.tensor
        def _(pe):
            mm, tp = nc.tensor.matmul, nc.tensor.transpose

            def transpose_xn(ln, i, n=TPB):
                pe.wait_ge(ln.xn, i + 1)
                for j in range(n):
                    last = tp(bank[7][:, j * P:(j + 1) * P], xn[:, j, :], ident[:])
                last.then_inc(ln.ps, 1)

            def attention(a, b, logits, next_ln=None):
                m = a.mem

                def expT(s):
                    pe.wait_ge(a.nr, b * UNITS + s + 1)
                    if s >= 2:
                        pe.wait_ge(a.lo, b * UNITS + s - 1)
                    for c in range(TPB):
                        last = tp(bank[2 + s % 2][:, c * P:(c + 1) * P], m.en[:, s % 3, c * P:(c + 1) * P], ident[:])
                    last.then_inc(a.tr, 1)

                def pv(s):
                    hd, c = s // TPB, s % TPB
                    g = hd // a.group
                    if c == 0:
                        pe.wait_ge(a.lo, b * UNITS + TPB * (hd + 1))
                    if s % (TPB * a.group) == 0 and g >= 2:
                        pe.wait_ge(a.ots, b * a.groups + g - 1)
                    for part in range(2):
                        last = mm(bank[4 + g % 2], m.v[:, c, hd, :], m.eT[:, hd % 2, part, c, :],
                                  start=(hd % a.group == 0 and c == 0 and part == 0),
                                  stop=(hd % a.group == a.group - 1 and c == TPB - 1 and part == 1))
                    last.then_inc(a.pv, 1)

                for s in range(UNITS + 8):
                    if s < UNITS:
                        if s >= 3:
                            pe.wait_ge(a.ex, b * UNITS + s - 2)
                        logits(s)
                    if 0 <= s - 3 < UNITS:
                        expT(s - 3)
                    if s >= 8:
                        pv(s - 8)
                    if s == UNITS + 3 and next_ln is not None:
                        transpose_xn(next_ln, b + 1)

            def project(a, b, wo, bo):
                pe.wait_ge(a.ots, b * a.groups + a.groups)
                for j in range(TPB):
                    dst = bank[6][:, j * D:(j + 1) * D]
                    for g in range(a.groups):
                        mm(dst, a.oT[:, g, j * P:(j + 1) * P], wo(g), start=(g == 0), stop=False)
                    last = mm(dst, ones[0:1, :], bo, start=False, stop=True)
                last.then_inc(a.proj, 1)

            pe.wait_ge(ld_tok, 80)
            pe.wait_ge(tanh_done, B + 1)
            for b in range(B):
                for j in range(TPB):
                    last = mm(bank[EMB[b]][:, j * D:(j + 1) * D], tanhT[:, b * S + j * P:b * S + (j + 1) * P], w2b2[:],
                              start=True, stop=True)
                last.then_inc(emb_ps, 1)
            pe.wait_ge(consts, 1)
            pe.wait_ge(ld_a0, 64)

            def logits0(s):
                hd, j = s // TPB, s % TPB
                mm(bank[LOGITS[s % 3]][:, :], mB.qT[:, hd, j * P:(j + 1) * P], mB.kT[:, 0, hd, :],
                   start=True, stop=True).then_inc(a0.qk, 1)

            def project0(b):
                project(a0, b, lambda g: wo0[:, g, :], bo0[:])

            def heads0(b, before=None):
                pe.wait_ge(lnB.sb, b + 1)
                for j in range(TPB):
                    mm(bank[j][:, 0:3 * D], xnT[:, j * P:(j + 1) * P], wqkv0[:], start=True, stop=True).then_inc(qkv_ps, 1)
                if before is not None:
                    project0(before)
                pe.wait_ge(qkv_sb, b * TPB + TPB)
                for n in range(2 * H):
                    if n % H == 0:
                        pe.wait_ge(st_lo, 2 * b + n // H + 1)
                    if n >= 4:
                        if n - 4 < H or n % 2 == 0:
                            pe.wait_ge(augT_act, b * 12 + (n - 3 if n - 4 < H else H + (n - 4 - H) // 2 + 1))
                        else:
                            pe.wait_ge(augT_dve, b * 4 + (n - 4 - H) // 2 + 1)
                    for j in range(TPB):
                        row = j * H + n % H
                        src = q_st[:, row, :, :].rearrange("p q a -> p (q a)") if n >= H else \
                            k_st[:, row, :, :, :].rearrange("p q r a -> p (q r a)")
                        last = tp(bank[n % 4][:, j * P:(j + 1) * P], src, ident[:])
                    last.then_inc(augT_ps, 1)
                pe.wait_ge(v0_lo, b + 1)
                pe.wait_ge(augT_act, b * 12 + 12)
                pe.wait_ge(augT_dve, b * 4 + 4)

            transpose_xn(lnB, 0)
            heads0(0)
            with pe.Fori(0, B - 1) as b:
                attention(a0, b, logits0, lnB)
                heads0(b + 1, b)
            attention(a0, B - 1, logits0)
            project0(B - 1)

            pe.wait_ge(bq_b, 1)
            pe.wait_ge(ld_pk, 48)
            for k, lhs in enumerate((wqT_s, bqb_s)):
                for q in range(2):
                    for n in range(H // 2):
                        hd = q * (H // 2) + n
                        last = mm(bank[2 * k + q][:, n * P:(n + 1) * P], lhs[:, hd, :], keys_s[:, hd, :],
                                  start=True, stop=True)
                    last.then_inc(kw_ps, 1)
            pe.wait_ge(kw_sb, 4)
            pe.wait_ge(kb_lo, 2)
            pe.wait_ge(consts, 4)
            pe.wait_ge(ld_exp, 32)

            def scores(t):
                pe.wait_ge(lnC.sb, t + 1)
                if not (isinstance(t, int) and t == 0):
                    pe.wait_ge(relu_rdy, NV // IG if isinstance(t, int) and t == 1 else (t - 1) * (NV // IG))
                for q in range(2):
                    span = slice(q * 512, (q + 1) * 512)
                    mm(bank[q][:, :], xnT[:, P:2 * P], keyw[:, span], start=True, stop=False)
                    mm(bank[q][:, :], ones_r[:], keyb[:, 0, span], start=False, stop=False)
                    mm(bank[q][:, :], ones_r[:], keyb[:, 1, span], start=False, stop=True).then_inc(sc_ps, 1)

            def transpose_uvp(t):
                pe.wait_ge(uvp_rdy, t + 1)
                for n in range(3):
                    last = tp(bank[7][:, (n + 1) * P:(n + 2) * P], uvp[:, n].rearrange("p q k -> p (q k)"), ident[:])
                last.then_inc(uvpT_ps, 1)

            def inner(t, newest):
                pe.wait_ge(xnT_in, t + 1)
                for g in range(NV // IG):
                    if newest is None:
                        pe.wait_ge(relu_rdy, t * (NV // IG) + g - 1)
                    elif g < 2:
                        pe.wait_ge(sc_sb, newest * 2 + g + 1)
                    else:
                        pe.wait_ge(relu_rdy, t * (NV // IG) + g - 1)
                    for q in range(IG):
                        last = mm(bank[g % 2][:, q * P:(q + 1) * P], wd[:, IG * g + q, :], xnT[:, 0:P],
                                  start=True, stop=True)
                    last.then_inc(in_ps, 1)

            def spread(t):
                for c in range(GP):
                    pe.wait_ge(onehot, t * GP + c + 1)
                    if c % 2 == 0:
                        pe.wait_ge(w_second, 2 * t + c // 2 + 1)
                    if c >= 2:
                        pe.wait_ge(g_cp, t * VP + c)
                    if c >= 3:
                        pe.wait_ge(vals_rdy, t * VD + c - 2)
                    for i in range(GT):
                        half_pair = GT // 2
                        out_cols = slice(i % half_pair * 2 * NV, (i % half_pair + 1) * 2 * NV)
                        for k in range(3):
                            last = mm(quad[:, 2 * (c % 2) + i // half_pair, out_cols], one_u[:, :, c * GT + i],
                                      w_v[:, k, :, :, c * GT + i].rearrange("p q v -> p (q v)"),
                                      start=(k == 0), stop=(k == 2))
                    last.then_inc(g_ps, 1)

            def combine(t, between=None):
                pe.wait_ge(vals_rdy, (t + 1) * VD)
                pe.wait_ge(vals_pool, (t + 1) * VP)
                for v in range(NV):
                    if v == 3 * NV // 4 and between is not None:
                        between()
                    last = mm(bank[6][:, 0:D], vals[:, v, :], wu[:, v, :], start=(v == 0), stop=(v == NV - 1))
                last.then_inc(ffn_ps, 1)

            def next_scores(t):
                if not (isinstance(t, int) and t == 1):
                    pe.wait_ge(uvpT_sb, t - 1)
                transpose_xn(lnC, t, 1)
                scores(t)

            transpose_xn(lnC, 0, 1)
            scores(0)
            inner(0, 0)
            next_scores(1)
            transpose_uvp(0)
            with pe.Fori(0, NT - 2) as t:
                spread(t)
                next_scores(t + 2)
                combine(t, lambda: transpose_uvp(t + 1))
                inner(t + 1, t + 2)
            spread(NT - 2)
            combine(NT - 2, lambda: transpose_uvp(NT - 1))
            inner(NT - 1, None)
            spread(NT - 1)
            combine(NT - 1)

            pe.wait_ge(ld_a1, 64)

            def logits1(s):
                hd, j = s // TPB, s % TPB
                for part in range(2):
                    last = mm(bank[LOGITS[s % 3]][:, :], mD.qT[:, hd, j * P:(j + 1) * P], mD.kT[:, part, hd, :],
                              start=(part == 0), stop=(part == 1))
                last.then_inc(a1.qk, 1)

            def project1(b):
                pe.wait_ge(ld_wo1, 16)
                project(a1, b, lambda g: wo1[:, g, :], bo1[:])

            def heads1(b, before=None):
                pe.wait_ge(lnD.sb, b + 1)
                for n in range(2 * H + TPB):
                    if n == 2 * H and before is not None:
                        project1(before)
                    if n >= 4:
                        pe.wait_ge(p1_lo, b * (2 * H + TPB) + n - 3)
                    if n < 2 * H:
                        w = (wq1, wk1)[n // H][:, (n % H) * P:(n % H + 1) * P]
                        last = mm(bank[n % 4][:, :], w, xnT[:], start=True, stop=True)
                    else:
                        j = n - 2 * H
                        last = mm(bank[n % 4][:, :], xnT[:, j * P:(j + 1) * P], wv1, start=True, stop=True)
                    last.then_inc(p1_ps, 1)
                pe.wait_ge(p1_lo, (b + 1) * (2 * H + TPB))

            transpose_xn(lnD, 0)
            heads1(0)
            with pe.Fori(0, B - 1) as b:
                attention(a1, b, logits1, lnD)
                heads1(b + 1, b)
            attention(a1, B - 1, logits1)
            project1(B - 1)

            pe.wait_ge(ld_moe, 80)
            for b in range(B):
                if b:
                    pe.wait_ge(lnE.sb, b)
                transpose_xn(lnE, b)
                pe.wait_ge(lnE.sb, b + 1)
                for j in range(TPB):
                    last = mm(bank[6][:, (j * B + b) * NE:(j * B + b + 1) * NE], xnT[:, j * P:(j + 1) * P], gate_w[:],
                              start=True, stop=True)
                last.then_inc(lg_ps, 1)

            def up(b, e):
                if not (isinstance(b, int) and b == 0 and e < 2):
                    pe.wait_ge(hid_sb, b * NE + e - 1)
                mm(bank[e % 2][:, :], w1e[:, e, :], xnT_all[:, ds(b * S, S)], start=True, stop=True).then_inc(hid_ps, 1)

            def down(b, e):
                pe.wait_ge(hid_sb, b * NE + e + 1)
                for j in range(TPB):
                    last = mm(bank[2 + e % 2][:, j * D:(j + 1) * D], hidT[:, e % 2, j * P:(j + 1) * P], w2e[:, e, :],
                              start=True, stop=True)
                last.then_inc(y_ps, 1)

            def b2_term(b):
                if b >= 2:
                    pe.wait_ge(y_add, b - 1)
                for j in range(TPB):
                    last = mm(bank[4 + b % 2][:, j * D:(j + 1) * D], gT[b * EP:(b + 1) * EP, j * P:(j + 1) * P],
                              b2e[b * EP:(b + 1) * EP, :], start=True, stop=True)
                last.then_inc(b2_ps, 1)

            up(0, 0)
            pe.wait_ge(aff_rdy, 1)
            for j in range(TPB):
                last = tp(bank[7][:, j * P:(j + 1) * P], aff[:, j].rearrange("p b e -> p (b e)"), ident[:])
            last.then_inc(affT_ps, 1)
            for e in range(NE):
                if e + 1 < NE:
                    up(0, e + 1)
                if e >= 2:
                    pe.wait_ge(y0_sb, e - 1)
                down(0, e)
                if e == GATED:
                    pe.wait_ge(gT_rdy, 1)
                    for j in range(TPB):
                        last = tp(bank[6][:, j * P:(j + 1) * P], gT[:, j * P:(j + 1) * P], ident[:])
                    last.then_inc(gN_ps, 1)
                if e > GATED and e - GATED <= B:
                    b2_term(e - GATED - 1)
            pe.wait_ge(y0_sb, NE)
            with pe.Fori(0, B - 1) as i:
                up(i + 1, 0)
                for e in range(NE):
                    if e + 1 < NE:
                        up(i + 1, e + 1)
                    pe.wait_ge(y_add, B + i * NE + e - 1)
                    down(i + 1, e)


_OUT = ((4, 512, 128), "float32")


def kernel(**inputs):
    import numpy as np
    import concourse.bacc as bacc
    from concourse.bass_utils import run_bass_kernel_spmd

    g = {k: np.asarray(v) for k, v in inputs.items()}
    P, H, NK = 128, 8, 64
    c = np.ascontiguousarray

    def twice(w):
        return c(np.broadcast_to(w.reshape(P, 8, 1, 64), (P, 8, 2, 64))).reshape(P, 1024)

    keys = g["L0_ffn_keys"]
    kbd = np.zeros((P, H, P), keys.dtype)
    for q in range(2):
        kbd[q * 64:(q + 1) * 64, :, q * 64:(q + 1) * 64] = keys[:, q].transpose(2, 0, 1)
    b2 = np.zeros((4, 32, 128), g["L1_ffn_b2"].dtype)
    b2[:, 0:16] = g["L1_ffn_b2"]
    arrays = {
        "x_idx": c(g["x"].reshape(16, P).T),
        "val_idx": c(g["itok_BS_0_4999"].reshape(16, P).T),
        "num_rows": c(g["fside_BS_numeric_value"].reshape(2048)),
        "mask_idx": c(g["mask_BS_i1_0"].reshape(16, P).T),
        "event_table": g["L0_tok_event_table"],
        "value_table": g["L0_tok_value_table"],
        "tok_w1": c(g["L0_tok_w1"].reshape(64, 1)),
        "tok_b1": c(g["L0_tok_b1"].reshape(64, 1)),
        "tok_w2b2": np.concatenate([g["L0_tok_w2"], g["L0_tok_b2"][None]], 0),
        "a0_wqkv": np.concatenate([g["L0_attn_Wq"], g["L0_attn_Wk"], g["L0_attn_Wv"]], 1),
        "a0_bqkv": np.concatenate([g["L0_attn_bq"], g["L0_attn_bk"], g["L0_attn_bv"]])[None],
        "a0_wo": c(np.broadcast_to(g["L0_attn_Wo"].reshape(2, 4, 1, 16, P), (2, 4, 2, 16, P))
                   .transpose(1, 2, 3, 0, 4)).reshape(P, 2 * P),
        "a0_bo": g["L0_attn_bo"][None],
        "pk_wqT": c(g["L0_ffn_Wq"].reshape(P, H, P).transpose(2, 1, 0).reshape(P, H * P)),
        "pk_bq": c(g["L0_ffn_bq"].reshape(H, P).T),
        "pk_keys": kbd.reshape(P, H * P),
        "pk_down": c(g["L0_ffn_w_down"].reshape(128, 32, 128).transpose(2, 1, 0).reshape(P, 4096)),
        "pk_up": g["L0_ffn_w_up"].reshape(128, 4096),
        "a1_wq": twice(g["L1_attn_w_q"]),
        "a1_wk": twice(g["L1_attn_w_k"]),
        "a1_wv": g["L1_attn_w_v"],
        "a1_wo": c(np.broadcast_to(g["L1_attn_w_out"].reshape(8, 1, 64, P), (8, 2, 64, P))
                   .transpose(1, 2, 0, 3)).reshape(P, 8 * P),
        "a1_bo": g["L1_attn_b_out"][None],
        "moe_gate": g["L1_ffn_gate_weight"],
        "moe_w1": c(g["L1_ffn_w1"].transpose(1, 0, 2).reshape(P, 2048)),
        "moe_b1": c(g["L1_ffn_b1"].T),
        "moe_w2": c(g["L1_ffn_w2"].transpose(1, 0, 2).reshape(P, 2048)),
        "moe_b2": b2.reshape(P, 128),
    }
    nc = bacc.Bacc("TRN2", target_bir_lowering=False, num_devices=1)
    aps = {k: nc.dram_tensor("in_" + k, a.shape, mybir.dt.from_np(a.dtype), kind="ExternalInput").ap()
           for k, a in arrays.items()}
    out = nc.dram_tensor("out_0", _OUT[0], mybir.dt.float32, kind="ExternalOutput").ap()
    tower(nc, *aps.values(), out)
    r = run_bass_kernel_spmd(nc, [{"in_" + k: a for k, a in arrays.items()}], core_ids=[0])
    return r.results[0]["out_0"]
```
